# Optimizing a Trainium2 kernel written in Bass

```python
import numpy as np
import jax
import jax.numpy as jnp

def _softmax(x, axis=-1):
    return jax.nn.softmax(x, axis=axis)

def _gelu(x):
    return jax.nn.gelu(x, approximate=True)

def _silu(x):
    return jax.nn.silu(x)

def _sigmoid(x):
    return jax.nn.sigmoid(x)

def _layernorm(x, axis=-1, eps=1e-05):
    m = jnp.mean(x, axis=axis, keepdims=True)
    v = jnp.var(x, axis=axis, keepdims=True)
    return (x - m) / jnp.sqrt(v + eps)

def _scatter_add(tgt, idx, src, axis=0):
    return tgt.at[idx].add(src)

def _segment_sum(src, seg, n):
    return jax.ops.segment_sum(src, seg, n)
kernel_name = 'mk_decoder_postln_d2_seqx_r8_69ee01'

def setup_inputs(seed: int=0):
    np.random.seed(seed)
    _w = jnp.asarray

    def _rec_inputs():
        import jax
        import jax.numpy as jnp
        _rk = jax.random.key(seed)
        x = -0.0002928 + 1 * jax.random.normal(jax.random.fold_in(_rk, 1), (32, 128, 128), jnp.float32)
        _lenS = 128 - jax.random.randint(jax.random.fold_in(_rk, 7), (32,), 0, max(1, 128 // 4) + 1, jnp.int32)
        _lenS2 = 128 - jax.random.randint(jax.random.fold_in(_rk, 8), (32,), 0, max(1, 128 // 4) + 1, jnp.int32)
        _ctx_1024P = jax.random.normal(jax.random.fold_in(_rk, 11), (32, 16, 128), jnp.float32)
        _ctx_1024c = jax.random.dirichlet(jax.random.fold_in(_rk, 511), 0.3 * jnp.ones((16,), jnp.float32), (32, 128))
        _ctx_1024t = jnp.einsum('bsk,bkd->bsd', _ctx_1024c, _ctx_1024P)
        _ctx_1024t = _ctx_1024t * jax.lax.rsqrt(jnp.mean(jnp.square(_ctx_1024t)) + 1e-12) * 0.953939
        ctx_1024 = -1.39393e-06 + 0.999914 * (_ctx_1024t + 0.3 * jax.random.normal(jax.random.fold_in(_rk, 611), (32, 128, 128), jnp.float32))
        return (x, ctx_1024)
    x, ctx_1024 = _rec_inputs()

    def _L0_attn_setup():
        import jax, jax.numpy as jnp
        import numpy as np
        import math
        D_MODEL = 128
        NUM_HEADS = 16
        HEAD_DIM = D_MODEL // NUM_HEADS
        LN_EPS = 1e-05

        def _layer_norm(x, g, b):
            mu = jnp.mean(x, axis=-1, keepdims=True)
            var = jnp.mean(jnp.square(x - mu), axis=-1, keepdims=True)
            return (x - mu) * jax.lax.rsqrt(var + LN_EPS) * g + b

        def _rope_tables(seq_len, dim, dtype):
            inv_freq = 1.0 / 10000.0 ** (jnp.arange(0, dim, 2, dtype=jnp.float32) / dim)
            t = jnp.arange(seq_len, dtype=jnp.float32)
            freqs = t[:, None] * inv_freq[None, :]
            emb = jnp.concatenate([freqs, freqs], axis=-1)
            return (jnp.cos(emb).astype(dtype), jnp.sin(emb).astype(dtype))

        def _rotate_half(x):
            x1, x2 = jnp.split(x, 2, axis=-1)
            return jnp.concatenate([-x2, x1], axis=-1)
        key = jax.random.key(seed)
        ks = jax.random.split(key, 8)
        B, S, D = (2, 256, D_MODEL)
        s_in = 1.0 / math.sqrt(D)
        return {'x': jax.random.normal(ks[0], (B, S, D), jnp.float32), 'ln1_g': jnp.ones((D,), jnp.float32), 'ln1_b': jnp.zeros((D,), jnp.float32), 'Wqkv': jax.random.normal(ks[1], (D, 3 * D), jnp.float32) * s_in, 'bqkv': jnp.zeros((3 * D,), jnp.float32), 'Wo': jax.random.normal(ks[2], (D, D), jnp.float32) * s_in, 'bo': jnp.zeros((D,), jnp.float32), 'ln2_g': jnp.ones((D,), jnp.float32), 'ln2_b': jnp.zeros((D,), jnp.float32), 'W1': jax.random.normal(ks[3], (D, 4 * D), jnp.float32) * s_in, 'b1': jnp.zeros((4 * D,), jnp.float32), 'W2': jax.random.normal(ks[4], (4 * D, D), jnp.float32) / math.sqrt(4 * D), 'b2': jnp.zeros((D,), jnp.float32)}
    _L0_attn_all = _L0_attn_setup()
    _L0_attn_in = {k: v for k, v in _L0_attn_all.items() if k in ('ln1_g', 'ln1_b', 'Wqkv', 'bqkv', 'Wo', 'bo', 'ln2_g', 'ln2_b', 'W1', 'b1', 'W2', 'b2')}
    del _L0_attn_all

    def _L0_xattn_setup():
        import jax, jax.numpy as jnp
        import numpy as np
        SCALE_BASE = 512.0
        GN_EPS = 1e-05

        def _xpos(x, downscale):
            L, D = (x.shape[-2], x.shape[-1])
            half = D // 2
            base = (jnp.arange(0, D, 2, dtype=jnp.float32) + 0.4 * D) / (1.4 * D)
            min_pos = -(L // 2)
            power = (jnp.arange(min_pos, min_pos + L, dtype=jnp.float32) / SCALE_BASE)[:, None]
            scale = base[None, :] ** power
            inv_freq = 1.0 / 10000.0 ** (jnp.arange(half, dtype=jnp.float32) / half)
            ang = jnp.arange(L, dtype=jnp.float32)[:, None] * inv_freq[None, :]
            sin, cos = (jnp.sin(ang), jnp.cos(ang))
            if downscale:
                scale = 1.0 / scale
            sin_s = jnp.repeat(sin * scale, 2, axis=-1)
            cos_s = jnp.repeat(cos * scale, 2, axis=-1)
            x1, x2 = (x[..., ::2], x[..., 1::2])
            rot = jnp.stack((-x2, x1), axis=-1).reshape(x.shape)
            return x * cos_s + rot * sin_s

        def _decay_mask(L, H):
            gammas = 1.0 - jnp.exp(jnp.linspace(np.log(1.0 / 32.0), np.log(1.0 / 512.0), H)).astype(jnp.float32)
            idx = jnp.arange(L)
            dist = idx[:, None] - idx[None, :]
            causal = dist >= 0
            d = jnp.maximum(dist, 0).astype(jnp.float32)
            return jnp.where(causal[None], gammas[:, None, None] ** d[None], 0.0)
        key = jax.random.key(seed)
        ks = jax.random.split(key, 9)
        B, L, D, H = (2, 256, 128, 16)
        hd = D // H
        return {'query': jax.random.normal(ks[0], (B, L, D), jnp.float32), 'key': jax.random.normal(ks[1], (B, L, D), jnp.float32), 'value': jax.random.normal(ks[2], (B, L, D), jnp.float32), 'W_Q': jax.random.normal(ks[3], (H, D, hd), jnp.float32) / D, 'W_K': jax.random.normal(ks[4], (H, D, hd), jnp.float32) / D, 'W_V': jax.random.normal(ks[5], (H, D, hd), jnp.float32) / D, 'g_w': jax.random.normal(ks[6], (D, D), jnp.float32) * (2.0 / (D + D)) ** 0.5, 'g_b': jnp.zeros((D,), jnp.float32), 'out_w': jax.random.normal(ks[7], (D, D), jnp.float32) * (2.0 / (D + D)) ** 0.5, 'out_b': jnp.zeros((D,), jnp.float32)}
    _L0_xattn_all = _L0_xattn_setup()
    _L0_xattn_in = {k: v for k, v in _L0_xattn_all.items() if k in ('W_Q', 'W_K', 'W_V', 'g_w', 'g_b', 'out_w', 'out_b')}
    del _L0_xattn_all

    def _L0_ffn_setup():
        import jax, jax.numpy as jnp
        import numpy as np
        D_MODEL = 128
        N_HEADS = 16
        D_HEAD = D_MODEL // N_HEADS
        N_EXPERTS = 8
        TOP_K = 2
        D_FF = 256
        EPS = 1e-06

        def rmsnorm(x, w):
            return x * jax.lax.rsqrt(jnp.mean(x * x, axis=-1, keepdims=True) + EPS) * w

        def swiglu(x, w_gate, w_up, w_down):
            return jax.nn.silu(x @ w_gate) * (x @ w_up) @ w_down
        key = jax.random.key(seed)
        ks = jax.random.split(key, 16)
        s = 0.02
        B, S = (2, 256)
        return {'X': jax.random.normal(ks[0], (B, S, D_MODEL), dtype=jnp.float32), 'norm1_w': jnp.ones((D_MODEL,), jnp.float32), 'norm2_w': jnp.ones((D_MODEL,), jnp.float32), 'wq': jax.random.normal(ks[1], (D_MODEL, D_MODEL), jnp.float32) * s, 'wk': jax.random.normal(ks[2], (D_MODEL, D_MODEL), jnp.float32) * s, 'wv': jax.random.normal(ks[3], (D_MODEL, D_MODEL), jnp.float32) * s, 'wo': jax.random.normal(ks[4], (D_MODEL, D_MODEL), jnp.float32) * s, 'router_w': jax.random.normal(ks[5], (D_MODEL, N_EXPERTS), jnp.float32) * s, 'sh_gate': jax.random.normal(ks[6], (D_MODEL, D_FF), jnp.float32) * s, 'sh_up': jax.random.normal(ks[7], (D_MODEL, D_FF), jnp.float32) * s, 'sh_down': jax.random.normal(ks[8], (D_FF, D_MODEL), jnp.float32) * s, 'e_gate': jax.random.normal(ks[9], (N_EXPERTS, D_MODEL, D_FF), jnp.float32) * s, 'e_up': jax.random.normal(ks[10], (N_EXPERTS, D_MODEL, D_FF), jnp.float32) * s, 'e_down': jax.random.normal(ks[11], (N_EXPERTS, D_FF, D_MODEL), jnp.float32) * s}
    _L0_ffn_all = _L0_ffn_setup()
    _L0_ffn_in = {k: v for k, v in _L0_ffn_all.items() if k in ('norm1_w', 'norm2_w', 'wq', 'wk', 'wv', 'wo', 'router_w', 'sh_gate', 'sh_up', 'sh_down', 'e_gate', 'e_up', 'e_down')}
    del _L0_ffn_all

    def _L1_attn_setup():
        import jax, jax.numpy as jnp
        import numpy as np
        D_MODEL, D_STATE, D_CONV, EXPAND = (128, 16, 4, 2)
        D_INNER = EXPAND * D_MODEL
        DT_RANK = (D_MODEL + 15) // 16
        B_SZ, SEQ = (2, 128)

        def _mamba_dir(x, inW, convW, convB, xpW, dtW, dtB, Alog, Dp, outW):
            Bsz, L, _ = x.shape
            d_inner, d_state = Alog.shape
            dt_rank = xpW.shape[0] - 2 * d_state
            xz = jnp.einsum('bld,ed->ble', x, inW)
            xi, z = jnp.split(xz, 2, axis=-1)
            xc = jnp.swapaxes(xi, 1, 2)
            xc = jax.lax.conv_general_dilated(xc, convW, window_strides=(1,), padding=[(convW.shape[-1] - 1, 0)], feature_group_count=d_inner)
            xc = xc + convB[None, :, None]
            u = jax.nn.silu(jnp.swapaxes(xc, 1, 2))
            x_dbl = jnp.einsum('bld,ed->ble', u, xpW)
            dt, Bm, Cm = jnp.split(x_dbl, [dt_rank, dt_rank + d_state], axis=-1)
            delta = jax.nn.softplus(jnp.einsum('blr,dr->bld', dt, dtW) + dtB)
            A = -jnp.exp(Alog)

            def step(h, ins):
                d_t, B_t, C_t, u_t = ins
                dA = jnp.exp(d_t[:, :, None] * A)
                h = h * dA + (d_t * u_t)[:, :, None] * B_t[:, None, :]
                y_t = jnp.einsum('bdn,bn->bd', h, C_t)
                return (h, y_t)
            h0 = jnp.zeros((Bsz, d_inner, d_state), x.dtype)
            xs = (jnp.swapaxes(delta, 0, 1), jnp.swapaxes(Bm, 0, 1), jnp.swapaxes(Cm, 0, 1), jnp.swapaxes(u, 0, 1))
            _, ys = jax.lax.scan(step, h0, xs)
            y = jnp.swapaxes(ys, 0, 1)
            y = y + u * Dp
            y = y * jax.nn.silu(z)
            return jnp.einsum('bld,od->blo', y, outW)

        def _make_params(key, suffix):
            ks = jax.random.split(key, 10)
            s = 0.02
            p = {'inW' + suffix: jax.random.normal(ks[0], (2 * D_INNER, D_MODEL), jnp.float32) * s, 'convW' + suffix: jax.random.normal(ks[1], (D_INNER, 1, D_CONV), jnp.float32) * s, 'convB' + suffix: jnp.zeros((D_INNER,), jnp.float32), 'xpW' + suffix: jax.random.normal(ks[2], (DT_RANK + 2 * D_STATE, D_INNER), jnp.float32) * s, 'dtW' + suffix: jax.random.normal(ks[3], (D_INNER, DT_RANK), jnp.float32) * s, 'dtB' + suffix: jax.random.normal(ks[4], (D_INNER,), jnp.float32) * 0.1 - 4.0, 'Alog' + suffix: jnp.log(1.0 + jax.random.uniform(ks[5], (D_INNER, D_STATE), jnp.float32) * 15.0), 'Dp' + suffix: jnp.ones((D_INNER,), jnp.float32), 'outW' + suffix: jax.random.normal(ks[6], (D_MODEL, D_INNER), jnp.float32) * s}
            return p
        key = jax.random.key(seed)
        kx, kf, kb = jax.random.split(key, 3)
        inp = {'x': jax.random.normal(kx, (B_SZ, SEQ, D_MODEL), jnp.float32)}
        inp.update(_make_params(kf, '_f'))
        inp.update(_make_params(kb, '_b'))
        return inp
    _L1_attn_all = _L1_attn_setup()
    _L1_attn_in = {k: v for k, v in _L1_attn_all.items() if k in ('inW_f', 'convW_f', 'convB_f', 'xpW_f', 'dtW_f', 'dtB_f', 'Alog_f', 'Dp_f', 'outW_f', 'inW_b', 'convW_b', 'convB_b', 'xpW_b', 'dtW_b', 'dtB_b', 'Alog_b', 'Dp_b', 'outW_b')}
    del _L1_attn_all

    def _L1_xattn_setup():
        import jax, jax.numpy as jnp
        import numpy as np
        DIM = 128
        HEAD_NUM = 8
        D_HEAD = DIM // HEAD_NUM
        B, S = (4, 256)
        key = jax.random.key(seed)
        ks = jax.random.split(key, 7)
        scale = 0.02
        return {'Q': jax.random.normal(ks[0], (B, S, DIM), dtype=jnp.float32), 'K': jax.random.normal(ks[1], (B, S, DIM), dtype=jnp.float32), 'V': jax.random.normal(ks[2], (B, S, DIM), dtype=jnp.float32), 'W_Q': jax.random.normal(ks[3], (DIM, DIM), dtype=jnp.float32) * scale, 'W_K': jax.random.normal(ks[4], (DIM, DIM), dtype=jnp.float32) * scale, 'W_V': jax.random.normal(ks[5], (DIM, DIM), dtype=jnp.float32) * scale, 'W_O': jax.random.normal(ks[6], (DIM, DIM), dtype=jnp.float32) * scale}
    _L1_xattn_all = _L1_xattn_setup()
    _L1_xattn_in = {k: v for k, v in _L1_xattn_all.items() if k in ('W_Q', 'W_K', 'W_V', 'W_O')}
    del _L1_xattn_all

    def _L1_ffn_setup():
        import jax, jax.numpy as jnp
        import numpy as np
        BLOCK = 32
        W_BITS = 4
        ACT_BITS = 16

        def act_qdq(x):
            qmax = 2.0 ** (ACT_BITS - 1) - 1.0
            scale = jnp.maximum(jnp.max(jnp.abs(x)) / qmax, 1e-12)
            return jnp.clip(jnp.round(x / scale), -qmax - 1.0, qmax) * scale

        def fixed_qdq_u16(x):
            scale = 1.0 / 65536.0
            return jnp.clip(jnp.round(x / scale), 0.0, 65535.0) * scale

        def lpbq_dequant(w):
            O, I = w.shape
            qmax = 2.0 ** (W_BITS - 1) - 1.0
            wb = w.reshape(O, I // BLOCK, BLOCK)
            s = jnp.maximum(jnp.max(jnp.abs(wb), axis=-1, keepdims=True) / qmax, 1e-12)
            wq = jnp.clip(jnp.round(wb / s), -qmax - 1.0, qmax) * s
            return wq.reshape(O, I)
        key = jax.random.key(seed)
        k1, k2, k3, k4 = jax.random.split(key, 4)
        B, S, H, I = (2, 512, 128, 384)
        x = jax.random.normal(k1, (B, S, H), jnp.float32)
        w_gate = jax.random.normal(k2, (I, H), jnp.float32) * 0.02
        w_up = jax.random.normal(k3, (I, H), jnp.float32) * 0.02
        w_down = jax.random.normal(k4, (H, I), jnp.float32) * 0.02
        return {'x': x, 'w_gate': w_gate, 'w_up': w_up, 'w_down': w_down}
    _L1_ffn_all = _L1_ffn_setup()
    _L1_ffn_in = {k: v for k, v in _L1_ffn_all.items() if k in ('w_gate', 'w_up', 'w_down')}
    del _L1_ffn_all
    return {'x': x, 'ctx_1024': ctx_1024, 'L0_attn_ln1_g': _L0_attn_in['ln1_g'], 'L0_attn_ln1_b': _L0_attn_in['ln1_b'], 'L0_attn_Wqkv': _L0_attn_in['Wqkv'], 'L0_attn_bqkv': _L0_attn_in['bqkv'], 'L0_attn_Wo': _L0_attn_in['Wo'], 'L0_attn_bo': _L0_attn_in['bo'], 'L0_attn_ln2_g': _L0_attn_in['ln2_g'], 'L0_attn_ln2_b': _L0_attn_in['ln2_b'], 'L0_attn_W1': _L0_attn_in['W1'], 'L0_attn_b1': _L0_attn_in['b1'], 'L0_attn_W2': _L0_attn_in['W2'], 'L0_attn_b2': _L0_attn_in['b2'], 'L0_xattn_W_Q': _L0_xattn_in['W_Q'], 'L0_xattn_W_K': _L0_xattn_in['W_K'], 'L0_xattn_W_V': _L0_xattn_in['W_V'], 'L0_xattn_g_w': _L0_xattn_in['g_w'], 'L0_xattn_g_b': _L0_xattn_in['g_b'], 'L0_xattn_out_w': _L0_xattn_in['out_w'], 'L0_xattn_out_b': _L0_xattn_in['out_b'], 'L0_ffn_norm1_w': _L0_ffn_in['norm1_w'], 'L0_ffn_norm2_w': _L0_ffn_in['norm2_w'], 'L0_ffn_wq': _L0_ffn_in['wq'], 'L0_ffn_wk': _L0_ffn_in['wk'], 'L0_ffn_wv': _L0_ffn_in['wv'], 'L0_ffn_wo': _L0_ffn_in['wo'], 'L0_ffn_router_w': _L0_ffn_in['router_w'], 'L0_ffn_sh_gate': _L0_ffn_in['sh_gate'], 'L0_ffn_sh_up': _L0_ffn_in['sh_up'], 'L0_ffn_sh_down': _L0_ffn_in['sh_down'], 'L0_ffn_e_gate': _L0_ffn_in['e_gate'], 'L0_ffn_e_up': _L0_ffn_in['e_up'], 'L0_ffn_e_down': _L0_ffn_in['e_down'], 'L1_attn_inW_f': _L1_attn_in['inW_f'], 'L1_attn_convW_f': _L1_attn_in['convW_f'], 'L1_attn_convB_f': _L1_attn_in['convB_f'], 'L1_attn_xpW_f': _L1_attn_in['xpW_f'], 'L1_attn_dtW_f': _L1_attn_in['dtW_f'], 'L1_attn_dtB_f': _L1_attn_in['dtB_f'], 'L1_attn_Alog_f': _L1_attn_in['Alog_f'], 'L1_attn_Dp_f': _L1_attn_in['Dp_f'], 'L1_attn_outW_f': _L1_attn_in['outW_f'], 'L1_attn_inW_b': _L1_attn_in['inW_b'], 'L1_attn_convW_b': _L1_attn_in['convW_b'], 'L1_attn_convB_b': _L1_attn_in['convB_b'], 'L1_attn_xpW_b': _L1_attn_in['xpW_b'], 'L1_attn_dtW_b': _L1_attn_in['dtW_b'], 'L1_attn_dtB_b': _L1_attn_in['dtB_b'], 'L1_attn_Alog_b': _L1_attn_in['Alog_b'], 'L1_attn_Dp_b': _L1_attn_in['Dp_b'], 'L1_attn_outW_b': _L1_attn_in['outW_b'], 'L1_xattn_W_Q': _L1_xattn_in['W_Q'], 'L1_xattn_W_K': _L1_xattn_in['W_K'], 'L1_xattn_W_V': _L1_xattn_in['W_V'], 'L1_xattn_W_O': _L1_xattn_in['W_O'], 'L1_ffn_w_gate': _L1_ffn_in['w_gate'], 'L1_ffn_w_up': _L1_ffn_in['w_up'], 'L1_ffn_w_down': _L1_ffn_in['w_down']}

def reference(x, ctx_1024, L0_attn_ln1_g, L0_attn_ln1_b, L0_attn_Wqkv, L0_attn_bqkv, L0_attn_Wo, L0_attn_bo, L0_attn_ln2_g, L0_attn_ln2_b, L0_attn_W1, L0_attn_b1, L0_attn_W2, L0_attn_b2, L0_xattn_W_Q, L0_xattn_W_K, L0_xattn_W_V, L0_xattn_g_w, L0_xattn_g_b, L0_xattn_out_w, L0_xattn_out_b, L0_ffn_norm1_w, L0_ffn_norm2_w, L0_ffn_wq, L0_ffn_wk, L0_ffn_wv, L0_ffn_wo, L0_ffn_router_w, L0_ffn_sh_gate, L0_ffn_sh_up, L0_ffn_sh_down, L0_ffn_e_gate, L0_ffn_e_up, L0_ffn_e_down, L1_attn_inW_f, L1_attn_convW_f, L1_attn_convB_f, L1_attn_xpW_f, L1_attn_dtW_f, L1_attn_dtB_f, L1_attn_Alog_f, L1_attn_Dp_f, L1_attn_outW_f, L1_attn_inW_b, L1_attn_convW_b, L1_attn_convB_b, L1_attn_xpW_b, L1_attn_dtW_b, L1_attn_dtB_b, L1_attn_Alog_b, L1_attn_Dp_b, L1_attn_outW_b, L1_xattn_W_Q, L1_xattn_W_K, L1_xattn_W_V, L1_xattn_W_O, L1_ffn_w_gate, L1_ffn_w_up, L1_ffn_w_down):
    import jax
    import jax.numpy as jnp

    def _L0_attn_ref(x, ln1_g, ln1_b, Wqkv, bqkv, Wo, bo, ln2_g, ln2_b, W1, b1, W2, b2):
        import jax, jax.numpy as jnp
        import numpy as np
        import math
        D_MODEL = 128
        NUM_HEADS = 16
        HEAD_DIM = D_MODEL // NUM_HEADS
        LN_EPS = 1e-05

        def _layer_norm(x, g, b):
            mu = jnp.mean(x, axis=-1, keepdims=True)
            var = jnp.mean(jnp.square(x - mu), axis=-1, keepdims=True)
            return (x - mu) * jax.lax.rsqrt(var + LN_EPS) * g + b

        def _rope_tables(seq_len, dim, dtype):
            inv_freq = 1.0 / 10000.0 ** (jnp.arange(0, dim, 2, dtype=jnp.float32) / dim)
            t = jnp.arange(seq_len, dtype=jnp.float32)
            freqs = t[:, None] * inv_freq[None, :]
            emb = jnp.concatenate([freqs, freqs], axis=-1)
            return (jnp.cos(emb).astype(dtype), jnp.sin(emb).astype(dtype))

        def _rotate_half(x):
            x1, x2 = jnp.split(x, 2, axis=-1)
            return jnp.concatenate([-x2, x1], axis=-1)
        B, S, D = x.shape
        H, hd = (NUM_HEADS, HEAD_DIM)
        normed = _layer_norm(x, ln1_g, ln1_b)
        qkv = (normed @ Wqkv + bqkv).reshape(B, S, 3, H, hd)
        qkv = jnp.transpose(qkv, (2, 0, 3, 1, 4))
        q, k, v = (qkv[0], qkv[1], qkv[2])
        cos, sin = _rope_tables(S, hd, q.dtype)
        cos = cos[None, None, :, :]
        sin = sin[None, None, :, :]
        q = q * cos + _rotate_half(q) * sin
        k = k * cos + _rotate_half(k) * sin
        scores = jnp.einsum('bhqd,bhkd->bhqk', q, k) / math.sqrt(hd)
        causal = jnp.triu(jnp.ones((S, S), dtype=bool), k=1)
        scores = jnp.where(causal[None, None], -jnp.inf, scores)
        attn = jax.nn.softmax(scores, axis=-1)
        attn_out = jnp.einsum('bhqk,bhkd->bhqd', attn, v)
        attn_out = jnp.transpose(attn_out, (0, 2, 1, 3)).reshape(B, S, D)
        attn_out = attn_out @ Wo + bo
        x = x + attn_out
        h = _layer_norm(x, ln2_g, ln2_b)
        h = jax.nn.gelu(h @ W1 + b1, approximate=False) @ W2 + b2
        return x + h

    def _L0_xattn_ref(query, key, value, W_Q, W_K, W_V, g_w, g_b, out_w, out_b):
        import jax, jax.numpy as jnp
        import numpy as np
        SCALE_BASE = 512.0
        GN_EPS = 1e-05

        def _xpos(x, downscale):
            L, D = (x.shape[-2], x.shape[-1])
            half = D // 2
            base = (jnp.arange(0, D, 2, dtype=jnp.float32) + 0.4 * D) / (1.4 * D)
            min_pos = -(L // 2)
            power = (jnp.arange(min_pos, min_pos + L, dtype=jnp.float32) / SCALE_BASE)[:, None]
            scale = base[None, :] ** power
            inv_freq = 1.0 / 10000.0 ** (jnp.arange(half, dtype=jnp.float32) / half)
            ang = jnp.arange(L, dtype=jnp.float32)[:, None] * inv_freq[None, :]
            sin, cos = (jnp.sin(ang), jnp.cos(ang))
            if downscale:
                scale = 1.0 / scale
            sin_s = jnp.repeat(sin * scale, 2, axis=-1)
            cos_s = jnp.repeat(cos * scale, 2, axis=-1)
            x1, x2 = (x[..., ::2], x[..., 1::2])
            rot = jnp.stack((-x2, x1), axis=-1).reshape(x.shape)
            return x * cos_s + rot * sin_s

        def _decay_mask(L, H):
            gammas = 1.0 - jnp.exp(jnp.linspace(np.log(1.0 / 32.0), np.log(1.0 / 512.0), H)).astype(jnp.float32)
            idx = jnp.arange(L)
            dist = idx[:, None] - idx[None, :]
            causal = dist >= 0
            d = jnp.maximum(dist, 0).astype(jnp.float32)
            return jnp.where(causal[None], gammas[:, None, None] ** d[None], 0.0)
        B, L, D = query.shape
        H = W_Q.shape[0]
        q = jnp.einsum('bld,hde->bhle', query, W_Q)
        k = jnp.einsum('bld,hde->bhle', key, W_K)
        v = jnp.einsum('bld,hde->bhle', value, W_V)
        q = _xpos(q, downscale=False)
        k = _xpos(k, downscale=True)
        sim = jnp.einsum('bhnd,bhsd->bhns', q, k) * _decay_mask(L, H)[None]
        ret = jnp.einsum('bhns,bhsd->bhnd', sim, v)
        mu = ret.mean(axis=-1, keepdims=True)
        var = ret.var(axis=-1, keepdims=True)
        ret = (ret - mu) / jnp.sqrt(var + GN_EPS)
        ret = ret.transpose(0, 2, 1, 3).reshape(B, L, D)
        gate = jax.nn.silu(query @ g_w.T + g_b)
        return ret * gate @ out_w.T + out_b

    def _L0_ffn_ref(X, norm1_w, norm2_w, wq, wk, wv, wo, router_w, sh_gate, sh_up, sh_down, e_gate, e_up, e_down):
        import jax, jax.numpy as jnp
        import numpy as np
        D_MODEL = 128
        N_HEADS = 16
        D_HEAD = D_MODEL // N_HEADS
        N_EXPERTS = 8
        TOP_K = 2
        D_FF = 256
        EPS = 1e-06

        def rmsnorm(x, w):
            return x * jax.lax.rsqrt(jnp.mean(x * x, axis=-1, keepdims=True) + EPS) * w

        def swiglu(x, w_gate, w_up, w_down):
            return jax.nn.silu(x @ w_gate) * (x @ w_up) @ w_down
        B, S, d = X.shape
        scale = 1.0 / jnp.sqrt(jnp.asarray(D_HEAD, X.dtype))
        h = rmsnorm(X, norm1_w)
        q = (h @ wq).reshape(B, S, N_HEADS, D_HEAD)
        k = (h @ wk).reshape(B, S, N_HEADS, D_HEAD)
        v = (h @ wv).reshape(B, S, N_HEADS, D_HEAD)
        scores = jnp.einsum('bshd,bthd->bhst', q, k) * scale
        attn = jax.nn.softmax(scores, axis=-1)
        ctx = jnp.einsum('bhst,bthd->bshd', attn, v).reshape(B, S, d)
        X = X + ctx @ wo
        h2 = rmsnorm(X, norm2_w).reshape(B * S, d)
        logits = h2 @ router_w
        probs = jax.nn.softmax(logits, axis=-1)
        topw, topi = jax.lax.top_k(probs, TOP_K)
        topw = jax.nn.softmax(topw, axis=-1)
        combine = jnp.sum(jax.nn.one_hot(topi, N_EXPERTS, dtype=h2.dtype) * topw[..., None], axis=1)
        shared = swiglu(h2, sh_gate, sh_up, sh_down)
        gate = jnp.einsum('td,edf->etf', h2, e_gate)
        up = jnp.einsum('td,edf->etf', h2, e_up)
        eout = jnp.einsum('etf,efd->etd', jax.nn.silu(gate) * up, e_down)
        spec = jnp.einsum('etd,te->td', eout, combine)
        moe_out = (shared + spec).reshape(B, S, d)
        return X + moe_out

    def _L1_attn_ref(x, inW_f, convW_f, convB_f, xpW_f, dtW_f, dtB_f, Alog_f, Dp_f, outW_f, inW_b, convW_b, convB_b, xpW_b, dtW_b, dtB_b, Alog_b, Dp_b, outW_b):
        import jax, jax.numpy as jnp
        import numpy as np
        D_MODEL, D_STATE, D_CONV, EXPAND = (128, 16, 4, 2)
        D_INNER = EXPAND * D_MODEL
        DT_RANK = (D_MODEL + 15) // 16
        B_SZ, SEQ = (2, 128)

        def _mamba_dir(x, inW, convW, convB, xpW, dtW, dtB, Alog, Dp, outW):
            Bsz, L, _ = x.shape
            d_inner, d_state = Alog.shape
            dt_rank = xpW.shape[0] - 2 * d_state
            xz = jnp.einsum('bld,ed->ble', x, inW)
            xi, z = jnp.split(xz, 2, axis=-1)
            xc = jnp.swapaxes(xi, 1, 2)
            xc = jax.lax.conv_general_dilated(xc, convW, window_strides=(1,), padding=[(convW.shape[-1] - 1, 0)], feature_group_count=d_inner)
            xc = xc + convB[None, :, None]
            u = jax.nn.silu(jnp.swapaxes(xc, 1, 2))
            x_dbl = jnp.einsum('bld,ed->ble', u, xpW)
            dt, Bm, Cm = jnp.split(x_dbl, [dt_rank, dt_rank + d_state], axis=-1)
            delta = jax.nn.softplus(jnp.einsum('blr,dr->bld', dt, dtW) + dtB)
            A = -jnp.exp(Alog)

            def step(h, ins):
                d_t, B_t, C_t, u_t = ins
                dA = jnp.exp(d_t[:, :, None] * A)
                h = h * dA + (d_t * u_t)[:, :, None] * B_t[:, None, :]
                y_t = jnp.einsum('bdn,bn->bd', h, C_t)
                return (h, y_t)
            h0 = jnp.zeros((Bsz, d_inner, d_state), x.dtype)
            xs = (jnp.swapaxes(delta, 0, 1), jnp.swapaxes(Bm, 0, 1), jnp.swapaxes(Cm, 0, 1), jnp.swapaxes(u, 0, 1))
            _, ys = jax.lax.scan(step, h0, xs)
            y = jnp.swapaxes(ys, 0, 1)
            y = y + u * Dp
            y = y * jax.nn.silu(z)
            return jnp.einsum('bld,od->blo', y, outW)

        def _make_params(key, suffix):
            ks = jax.random.split(key, 10)
            s = 0.02
            p = {'inW' + suffix: jax.random.normal(ks[0], (2 * D_INNER, D_MODEL), jnp.float32) * s, 'convW' + suffix: jax.random.normal(ks[1], (D_INNER, 1, D_CONV), jnp.float32) * s, 'convB' + suffix: jnp.zeros((D_INNER,), jnp.float32), 'xpW' + suffix: jax.random.normal(ks[2], (DT_RANK + 2 * D_STATE, D_INNER), jnp.float32) * s, 'dtW' + suffix: jax.random.normal(ks[3], (D_INNER, DT_RANK), jnp.float32) * s, 'dtB' + suffix: jax.random.normal(ks[4], (D_INNER,), jnp.float32) * 0.1 - 4.0, 'Alog' + suffix: jnp.log(1.0 + jax.random.uniform(ks[5], (D_INNER, D_STATE), jnp.float32) * 15.0), 'Dp' + suffix: jnp.ones((D_INNER,), jnp.float32), 'outW' + suffix: jax.random.normal(ks[6], (D_MODEL, D_INNER), jnp.float32) * s}
            return p
        y_fwd = _mamba_dir(x, inW_f, convW_f, convB_f, xpW_f, dtW_f, dtB_f, Alog_f, Dp_f, outW_f)
        xb = jnp.flip(x, axis=1)
        y_bwd = jnp.flip(_mamba_dir(xb, inW_b, convW_b, convB_b, xpW_b, dtW_b, dtB_b, Alog_b, Dp_b, outW_b), axis=1)
        return 0.5 * (y_fwd + y_bwd)

    def _L1_xattn_ref(Q, K, V, W_Q, W_K, W_V, W_O):
        import jax, jax.numpy as jnp
        import numpy as np
        DIM = 128
        HEAD_NUM = 8
        D_HEAD = DIM // HEAD_NUM
        B, S = (4, 256)
        b, s, d = Q.shape
        h, dh = (HEAD_NUM, d // HEAD_NUM)

        def proj_split(x, W):
            y = jnp.einsum('bsd,ed->bse', x, W)
            return y.reshape(b, s, h, dh).transpose(0, 2, 1, 3)
        q = proj_split(Q, W_Q)
        k = proj_split(K, W_K)
        v = proj_split(V, W_V)
        scores = jnp.einsum('bhqd,bhkd->bhqk', q, k) / jnp.sqrt(jnp.float32(dh))
        attn = jax.nn.softmax(scores, axis=1)
        ctx = jnp.einsum('bhqk,bhkd->bhqd', attn, v)
        ctx = ctx.transpose(0, 2, 1, 3).reshape(b, s, d)
        return jnp.einsum('bsd,ed->bse', ctx, W_O)

    def _L1_ffn_ref(x, w_gate, w_up, w_down):
        import jax, jax.numpy as jnp
        import numpy as np
        BLOCK = 32
        W_BITS = 4
        ACT_BITS = 16

        def act_qdq(x):
            qmax = 2.0 ** (ACT_BITS - 1) - 1.0
            scale = jnp.maximum(jnp.max(jnp.abs(x)) / qmax, 1e-12)
            return jnp.clip(jnp.round(x / scale), -qmax - 1.0, qmax) * scale

        def fixed_qdq_u16(x):
            scale = 1.0 / 65536.0
            return jnp.clip(jnp.round(x / scale), 0.0, 65535.0) * scale

        def lpbq_dequant(w):
            O, I = w.shape
            qmax = 2.0 ** (W_BITS - 1) - 1.0
            wb = w.reshape(O, I // BLOCK, BLOCK)
            s = jnp.maximum(jnp.max(jnp.abs(wb), axis=-1, keepdims=True) / qmax, 1e-12)
            wq = jnp.clip(jnp.round(wb / s), -qmax - 1.0, qmax) * s
            return wq.reshape(O, I)
        x = act_qdq(x)
        up = act_qdq(x @ lpbq_dequant(w_up).T)
        gate = act_qdq(x @ lpbq_dequant(w_gate).T)
        sig = fixed_qdq_u16(jax.nn.sigmoid(gate))
        gate = act_qdq(gate * sig)
        o = act_qdq(gate * up)
        return o @ lpbq_dequant(w_down).T
    x = _layernorm(x + _L0_attn_ref(x, L0_attn_ln1_g, L0_attn_ln1_b, L0_attn_Wqkv, L0_attn_bqkv, L0_attn_Wo, L0_attn_bo, L0_attn_ln2_g, L0_attn_ln2_b, L0_attn_W1, L0_attn_b1, L0_attn_W2, L0_attn_b2), axis=-1)
    x = _layernorm(x + _L0_xattn_ref(x, ctx_1024, ctx_1024, L0_xattn_W_Q, L0_xattn_W_K, L0_xattn_W_V, L0_xattn_g_w, L0_xattn_g_b, L0_xattn_out_w, L0_xattn_out_b), axis=-1)
    x = _layernorm(x + _L0_ffn_ref(x, L0_ffn_norm1_w, L0_ffn_norm2_w, L0_ffn_wq, L0_ffn_wk, L0_ffn_wv, L0_ffn_wo, L0_ffn_router_w, L0_ffn_sh_gate, L0_ffn_sh_up, L0_ffn_sh_down, L0_ffn_e_gate, L0_ffn_e_up, L0_ffn_e_down), axis=-1)
    x = _layernorm(x + _L1_attn_ref(x, L1_attn_inW_f, L1_attn_convW_f, L1_attn_convB_f, L1_attn_xpW_f, L1_attn_dtW_f, L1_attn_dtB_f, L1_attn_Alog_f, L1_attn_Dp_f, L1_attn_outW_f, L1_attn_inW_b, L1_attn_convW_b, L1_attn_convB_b, L1_attn_xpW_b, L1_attn_dtW_b, L1_attn_dtB_b, L1_attn_Alog_b, L1_attn_Dp_b, L1_attn_outW_b), axis=-1)
    x = _layernorm(x + _L1_xattn_ref(x, ctx_1024, ctx_1024, L1_xattn_W_Q, L1_xattn_W_K, L1_xattn_W_V, L1_xattn_W_O), axis=-1)
    x = _layernorm(x + _L1_ffn_ref(x, L1_ffn_w_gate, L1_ffn_w_up, L1_ffn_w_down), axis=-1)
    return x

_drawn_inputs = setup_inputs


def setup_inputs(seed=0):
    import zlib

    import numpy as np

    out = dict(_drawn_inputs(seed))
    spreads = {'L0_attn_ln1_g': (1.0, 0.2),
     'L0_attn_ln1_b': (0.0, 0.1),
     'L0_attn_bqkv': (0.0, 0.1),
     'L0_attn_bo': (0.0, 0.1),
     'L0_attn_ln2_g': (1.0, 0.2),
     'L0_attn_ln2_b': (0.0, 0.1),
     'L0_attn_b1': (0.0, 0.1),
     'L0_attn_b2': (0.0, 0.1),
     'L0_xattn_g_b': (0.0, 0.1),
     'L0_xattn_out_b': (0.0, 0.1),
     'L0_ffn_norm1_w': (1.0, 0.6),
     'L0_ffn_norm2_w': (1.0, 0.6),
     'L1_attn_convB_f': (0.0, 0.8),
     'L1_attn_Dp_f': (1.0, 0.6),
     'L1_attn_convB_b': (0.0, 0.8),
     'L1_attn_Dp_b': (1.0, 0.6)}
    factors = {'L0_ffn_wq': 8.0,
     'L0_ffn_wk': 8.0,
     'L0_ffn_wv': 8.0,
     'L0_ffn_wo': 8.0,
     'L0_ffn_router_w': 8.0,
     'L0_ffn_sh_gate': 8.0,
     'L0_ffn_sh_up': 8.0,
     'L0_ffn_sh_down': 8.0,
     'L0_ffn_e_gate': 8.0,
     'L0_ffn_e_up': 8.0,
     'L0_ffn_e_down': 8.0,
     'L1_attn_inW_f': 8.0,
     'L1_attn_convW_f': 8.0,
     'L1_attn_xpW_f': 200.0,
     'L1_attn_dtW_f': 64.0,
     'L1_attn_dtB_f': 64.0,
     'L1_attn_Alog_f': 8.0,
     'L1_attn_outW_f': 8.0,
     'L1_attn_inW_b': 8.0,
     'L1_attn_convW_b': 8.0,
     'L1_attn_xpW_b': 200.0,
     'L1_attn_dtW_b': 200.0,
     'L1_attn_dtB_b': 64.0,
     'L1_attn_Alog_b': 8.0,
     'L1_attn_outW_b': 8.0,
     'L1_xattn_W_Q': 4.651,
     'L1_xattn_W_K': 4.685,
     'L1_ffn_w_gate': 5.409,
     'L1_ffn_w_up': 5.345,
     'L1_ffn_w_down': 5.345}
    for name, (base, spread) in spreads.items():
        noise = np.random.default_rng([zlib.crc32(name.encode()), seed]).standard_normal(out[name].shape)
        drawn = base * np.exp(spread * noise) if base else spread * noise
        out[name] = jnp.asarray(drawn.astype(out[name].dtype))
    for name, factor in factors.items():
        out[name] = (out[name] * factor).astype(out[name].dtype)
    return out
```

```python
from contextlib import ExitStack

import numpy as np

import concourse.bass as bass
from concourse import mybir

ALU = mybir.AluOpType
ACT = mybir.ActivationFunctionType
F32 = mybir.dt.float32
BF16 = mybir.dt.bfloat16
U32 = mybir.dt.uint32
AX_X = mybir.AxisListType.X

B, T, D = 32, 128, 128
G = 4
NG = B // G
GT = G * T
BANK = 512
H, HD = 16, D // 16
QUAD = 32
NJ = T // QUAD
NK = H // NJ
HUGE = -1.0e30
LN_EPS = 1e-5
RMS_EPS = 1e-6


COUNTED = []


def clear_counts(nc):
    nc.clear_and_free_semaphores(COUNTED)
    COUNTED.clear()
    nc.all_engine_barrier()


class Mem:

    def __init__(self, nc, stack, stage):
        self.nc, self.stack, self.stage = nc, stack, stage

    def sb(self, name, shape, dt=F32):
        return self.stack.enter_context(self.nc.sbuf_tensor(f"{self.stage}_{name}", shape, dt))

    def ps(self, name, shape, dt=F32):
        return self.stack.enter_context(self.nc.psum_tensor(f"{self.stage}_{name}", shape, dt))

    def sem(self, name):
        semaphore = self.nc.alloc_semaphore(f"{self.stage}_{name}")
        COUNTED.append(semaphore)
        return semaphore


class Steps:

    def __init__(self, engine, sem, base=0, per_loop=0):
        self.engine, self.sem, self.base, self.n, self.per_loop = engine, sem, base, 0, per_loop

    def then(self, instruction):
        instruction.then_inc(self.sem, 1)
        self.n += 1

    def settle(self):
        self.engine.wait_ge(self.sem, self.base + self.n)

    def settle_apart(self, passed):
        self.settle()
        self.engine.sem_inc(passed, 1)

    def closed(self):
        assert self.n == self.per_loop, f"the loop's body has {self.n} steps"


def row(vector):
    return vector.rearrange("(a n) -> a n", a=1)


def column(vector):
    return vector.rearrange("(n a) -> n a", a=1)


def all_rows(vector, n=128):
    return bass.AP(vector.tensor, vector.offset, [[0, n]] + list(vector.ap))


def bn(ap, *dims):
    return bass.AP(ap.tensor, ap.offset, [ap.ap[0]] + [list(d) for d in dims])


def spread(ap, n):
    return bass.AP(ap.tensor, ap.offset, list(ap.ap) + [[0, n]])


def repeat(ap, n):
    return bass.AP(ap.tensor, ap.offset, [ap.ap[0], [0, n]] + list(ap.ap[1:]))


class Norm:

    def __init__(self, m, name, rms=False):
        self.rms = rms
        self.stats = m.sb(name + "_stats", [T, G, 6])
        self.moments = m.sb(name + "_moments", [T, G, 2])
        self.square = m.sb(name + "_square", [T, G])
        self.var = m.sb(name + "_var", [T, G])
        self.rstd = m.sb(name + "_rstd", [T, G])
        self.var_ready = m.sem(name + "_var_ready")
        self.stats_passed = m.sem(name + "_stats_passed")
        self.rstd_ready = m.sem(name + "_rstd_ready")

    def take_moments(self, nc, steps, x):
        for b in range(G):
            steps.then(nc.vector.bn_stats(self.stats[:, b, :], x[:, b, :]))
        steps.settle_apart(self.stats_passed)
        for b in range(G):
            steps.then(nc.vector.bn_aggr(self.moments[:, b, :], self.stats[:, b, :]))
        steps.settle()
        mean, var = self.moments[:, :, 0], self.moments[:, :, 1]
        if self.rms:
            steps.then(nc.vector.tensor_tensor(self.square[:], mean, mean, ALU.mult))
            steps.settle()
            nc.vector.scalar_tensor_tensor(out=self.var[:], in0=var, scalar=RMS_EPS, in1=self.square[:], op0=ALU.add, op1=ALU.add)\
                .then_inc(self.var_ready, 1)
        else:
            nc.vector.tensor_scalar(self.var[:], var, LN_EPS, None, ALU.add).then_inc(self.var_ready, 1)

    def root(self, nc, pool, c, n):
        pool.wait_ge(self.var_ready, n + 1)
        nc.gpsimd.tensor_tensor(self.rstd[:], self.var[:], c.minus_half[:], ALU.pow).then_inc(self.rstd_ready, 1)

    def apply(self, nc, dve, x, out, n, done):
        dve.wait_ge(self.rstd_ready, n + 1)
        for b in range(G):
            r = self.rstd[:, b:b + 1]
            if self.rms:
                nc.vector.tensor_scalar(out(b), x[:, b, :], r, None, ALU.mult).then_inc(done, 1)
            else:
                nc.vector.tensor_scalar(out(b), x[:, b, :], self.moments[:, b, 0:1], r, ALU.subtract, ALU.mult).then_inc(done, 1)


def attention(nc, stage, x_all, y_all, c, p, rope):
    with ExitStack() as stack:
        m = Mem(nc, stack, stage)
        w_qkv = m.sb("w_qkv", [D, 3 * D])
        w_o = m.sb("w_o", [D, D])
        gain = m.sb("gain", [D, 2])
        before = Norm(m, "before", rms=not rope)
        xn = m.sb("xn", [T, G, D])
        xnT = m.sb("xnT", [D, GT])
        PADDED = 2 * D + QUAD - HD
        qk = m.sb("qk", [T, G, PADDED])
        v_one = m.sb("v_one", [T, G, H, HD + 1])
        qT = m.sb("qT", [T, 2, NK, T])
        kT = m.sb("kT", [T, 2, NK, T])
        prob = m.sb("prob", [T, 2, NJ, NK, T])
        probT = m.sb("probT", [T, 2, NJ, NK, T])
        top = m.sb("top", [T, 2, NJ, NK])
        inv = m.sb("inv", [T, 2, H])
        att = m.sb("att", [T, G, D])
        attT = m.sb("attT", [D, GT])
        if rope:
            b_qkv = m.sb("b_qkv", [T, 3 * D])
            b_o = m.sb("b_o", [T, D])
            cos = m.sb("cos", [T, 2 * D])
            sin = m.sb("sin", [T, 2 * D])
            raw = m.sb("raw", [T, G, 2 * D])
            turned = m.sb("turned", [T, 2, 2 * D])
        ps_s = m.ps("ps_s", [T, NJ, NK, T])
        ps_t = m.ps("ps_t", [T, 2, BANK])
        ps_a = m.ps("ps_a", [T, BANK])
        ps_o = m.ps("ps_o", [T, BANK])

        loaded = m.sem("loaded")
        padded = m.sem("padded")
        xn_ready = m.sem("xn_ready")
        xn_turned = m.sem("xn_turned")
        xnT_ready = m.sem("xnT_ready")
        qkv_ready = m.sem("qkv_ready")
        qkv_taken = m.sem("qkv_taken")
        qk_ready = m.sem("qk_ready")
        turn_filled = m.sem("turn_filled")
        turn_taken = m.sem("turn_taken")
        scores_ready = m.sem("scores_ready")
        shifted = m.sem("shifted")
        exp_ready = m.sem("exp_ready")
        probT_ready = m.sem("probT_ready")
        pv_ready = m.sem("pv_ready")
        att_ready = m.sem("att_ready")
        att_turned = m.sem("att_turned")
        attT_ready = m.sem("attT_ready")
        out_ready = m.sem("out_ready")
        group_done = m.sem("group_done")
        dve_steps = m.sem("dve_steps")
        pool_steps = m.sem("pool_steps")

        block = stack.enter_context(nc.Block())
        FILLS = 2 + NJ

        def fill_q(b):
            return FILLS * b - NJ if b else 0

        def fill_prob(b):
            return FILLS * b + 4 if b < G - 1 else FILLS * G - NJ

        @block.sync
        def _(sp):
            n = 0
            for dst, src in p["loads"](w_qkv, w_o, gain):
                sp.dma_start(dst, src).then_inc(loaded, 16)
                n += 1
            if rope:
                for dst, src in ((b_qkv[:], all_rows(p["b_qkv"])), (b_o[:], all_rows(p["b_o"])),
                                 (cos[:], p["cos"]), (sin[:], p["sin"])):
                    sp.dma_start(dst, src).then_inc(loaded, 16)
                    n += 1
            assert n == p["n_loads"]

        ALL_LOADED = 16 * p["n_loads"]

        @block.tensor
        def _(pe):
            pe.wait_ge(loaded, ALL_LOADED)
            with pe.Fori(0, NG) as i:
                for b in range(G):
                    pe.wait_ge(xn_ready, i * G + b + 1)
                    last = nc.tensor.transpose(ps_a[:, b * T:(b + 1) * T], xn[:, b, :], c.ident[:])
                last.then_inc(xn_turned, 1)
                pe.wait_ge(xnT_ready, i + 1)
                for b in range(G):
                    dst = (ps_a, ps_o)[b % 2]
                    if b >= 2:
                        pe.wait_ge(qkv_taken, i * G + b - 1)
                    nc.tensor.matmul(dst[:, 0:3 * D], xnT[:, b * T:(b + 1) * T], w_qkv[:],
                                     start=True, stop=True).then_inc(qkv_ready, 1)

                def turn(n, src, blocks):
                    pe.wait_ge(turn_taken, i * (G * FILLS) + n + 1)
                    for k in range(4):
                        last = nc.tensor.matmul(ps_t[:, n % 2, k * T:(k + 1) * T], blocks(src, k), c.ident[:], is_transpose=True,
                                                start=(k == 0), stop=(k == 3), skip_group_check=True)
                    last.then_inc(turn_filled, 1)

                def heads_of(b, at):
                    return lambda src, k: src[:, b, at + k * HD:at + k * HD + T]

                def scores(b):
                    pe.wait_ge(qk_ready if rope else qkv_taken, i * G + b + 1)
                    turn(fill_q(b), qk, heads_of(b, 0))
                    turn(fill_q(b) + 1, qk, heads_of(b, D))
                    pe.wait_ge(turn_taken, i * (G * FILLS) + fill_q(b) + 2 + 2)
                    if b > 0:
                        pe.wait_ge(shifted, i * G * NJ + b * NJ)
                    if rope:
                        for j in range(NJ):
                            nc.tensor.matmul(ps_s[:, j, :, :], c.ident_b[:], repeat(c.causal_b[:], NK),
                                             start=True, stop=False, skip_group_check=True)
                    for k in range(NK):
                        for j in range(NJ):
                            r = slice(j * QUAD, j * QUAD + HD)
                            last = nc.tensor.matmul(ps_s[:, j, k, :], qT[r, b % 2, k, :], kT[r, b % 2, k, :],
                                                    start=(not rope and k == 0), stop=(k == NK - 1), skip_group_check=True)
                            if k == NK - 1:
                                last.then_inc(scores_ready, 1)

                def values(b):
                    for j in range(NJ):
                        pe.wait_ge(exp_ready, i * G * NJ + b * NJ + j + 1)
                        turn(fill_prob(b) + j, prob, lambda src, k: src[:, b % 2, j, k, :])
                    if b == 0:
                        pe.wait_ge(qkv_taken, i * G + G)
                    else:
                        pe.wait_ge(att_ready, i * G + b)
                    pe.wait_ge(turn_taken, i * (G * FILLS) + fill_prob(b) + NJ + 2)
                    for j in range(NJ):
                        for k in range(NK):
                            h = NK * j + k
                            last = nc.tensor.matmul(ps_o[:, h * (HD + 1):(h + 1) * (HD + 1)], probT[:, b % 2, j, k, :], v_one[:, b, h, :],
                                                    start=(j == 0 and k == 0), stop=(j == NJ - 1 and k == NK - 1), skip_group_check=True)
                    last.then_inc(pv_ready, 1)

                for b in range(G + 1):
                    if b < G:
                        scores(b)
                    if b > 0:
                        values(b - 1)
                pe.wait_ge(att_ready, i * G + G)
                for b in range(G):
                    last = nc.tensor.transpose(ps_a[:, b * T:(b + 1) * T], att[:, b, :], c.ident[:])
                last.then_inc(att_turned, 1)
                pe.wait_ge(attT_ready, i + 1)
                for b in range(G):
                    last = nc.tensor.matmul(ps_o[:, b * D:(b + 1) * D], attT[:, b * T:(b + 1) * T], w_o[:],
                                            start=(b == 0), stop=(b == G - 1), skip_group_check=True)
                last.then_inc(out_ready, 1)
                pe.wait_ge(group_done, i + 1)

        @block.scalar
        def _(act):
            act.wait_ge(loaded, ALL_LOADED)
            act.sem_inc(turn_taken, 2)
            with act.Fori(0, NG) as i:
                act.wait_ge(xn_turned, i + 1)
                if rope:
                    nc.scalar.activation(xnT[:], ps_a[:], ACT.Identity, bias=gain[:, 1:2], scale=gain[:, 0:1]).then_inc(xnT_ready, 1)
                else:
                    nc.scalar.activation(xnT[:], ps_a[:], ACT.Copy, scale=gain[:, 0:1]).then_inc(xnT_ready, 1)

                def copy_turn(n, dst):
                    act.wait_ge(turn_filled, i * (G * FILLS) + n + 1)
                    nc.scalar.copy(dst, ps_t[:, n % 2, :]).then_inc(turn_taken, 1)

                for b in range(G + 1):
                    if b < G:
                        copy_turn(fill_q(b), qT[:, b % 2, :, :])
                        copy_turn(fill_q(b) + 1, kT[:, b % 2, :, :])
                    if b > 0:
                        for j in range(NJ):
                            copy_turn(fill_prob(b - 1) + j, probT[:, (b - 1) % 2, j, :, :])
                    if b < G:
                        for j in range(NJ):
                            act.wait_ge(shifted, i * G * NJ + b * NJ + j + 1)
                            nc.scalar.activation(prob[:, b % 2, j, :, :], prob[:, b % 2, j, :, :], ACT.Exp, scale=HD ** -0.5).then_inc(exp_ready, 1)
                act.wait_ge(att_turned, i + 1)
                nc.scalar.copy(attT[:], ps_a[:]).then_inc(attT_ready, 1)

        @block.gpsimd
        def _(pool):
            pool.memset(qk[:, :, 2 * D:PADDED], 0.0).then_inc(padded, 1)
            pool.memset(v_one[:, :, :, HD], 1.0).then_inc(padded, 1)
            pool.wait_ge(loaded, ALL_LOADED)
            with pool.Fori(0, NG) as i:
                before.root(nc, pool, c, i)
                if not rope:
                    return
                steps = Steps(pool, pool_steps, i * (G * 3), G * 3)
                for b in range(G):
                    pool.wait_ge(qkv_taken, i * G + b + 1)
                    halves = raw[:, b, :].rearrange("p (h s d) -> p h s d", s=2, d=HD // 2)
                    t = turned[:, b % 2, :].rearrange("p (h s d) -> p h s d", s=2, d=HD // 2)
                    s = sin[:].rearrange("p (h s d) -> p h s d", s=2, d=HD // 2)
                    steps.then(nc.gpsimd.tensor_tensor(t[:, :, 0, :], halves[:, :, 1, :], s[:, :, 0, :], ALU.mult))
                    steps.then(nc.gpsimd.tensor_tensor(t[:, :, 1, :], halves[:, :, 0, :], s[:, :, 1, :], ALU.mult))
                    steps.then(nc.gpsimd.tensor_tensor(qk[:, b, 0:2 * D], raw[:, b, :], cos[:], ALU.mult))
                    steps.settle()
                    nc.gpsimd.tensor_tensor(qk[:, b, 0:2 * D], qk[:, b, 0:2 * D], turned[:, b % 2, :], ALU.add).then_inc(qk_ready, 1)
                steps.closed()

        @block.vector
        def _(dve):
            dve.wait_ge(loaded, ALL_LOADED)
            dve.wait_ge(padded, 2)
            per_loop = p["dve_steps"]
            with dve.Fori(0, NG) as i:
                steps = Steps(dve, dve_steps, i * per_loop, per_loop)
                x = x_all[:, bass.ds(i * G, G), :]
                before.take_moments(nc, steps, x)
                before.apply(nc, dve, x, lambda b: xn[:, b, :], i, xn_ready)
                for b in range(G):
                    dve.wait_ge(qkv_ready, i * G + b + 1)
                    src = (ps_a, ps_o)[b % 2]
                    v_dst = v_one[:, b, :, 0:HD]
                    if rope:
                        steps.then(nc.vector.tensor_tensor(v_dst, src[:, 2 * D:3 * D].rearrange("p (h d) -> p h d", d=HD),
                                                           b_qkv[:, 2 * D:3 * D].rearrange("p (h d) -> p h d", d=HD), ALU.add))
                        steps.settle()
                        nc.vector.tensor_tensor(raw[:, b, :], src[:, 0:2 * D], b_qkv[:, 0:2 * D], ALU.add).then_inc(qkv_taken, 1)
                    else:
                        steps.then(nc.vector.tensor_copy(v_dst, src[:, 2 * D:3 * D].rearrange("p (h d) -> p h d", d=HD)))
                        steps.settle()
                        nc.vector.tensor_copy(qk[:, b, 0:2 * D], src[:, 0:2 * D]).then_inc(qkv_taken, 1)

                def shift(b):
                    for j in range(NJ):
                        dve.wait_ge(scores_ready, i * G * NJ + b * NJ + j + 1)
                        steps.then(nc.vector.tensor_reduce(top[:, b % 2, j, :], ps_s[:, j, :, :], AX_X, ALU.max))
                        steps.settle()
                        nc.vector.tensor_tensor(prob[:, b % 2, j, :, :], ps_s[:, j, :, :], spread(top[:, b % 2, j, :], T), ALU.subtract)\
                            .then_inc(shifted, 1)

                def divide(b):
                    dve.wait_ge(pv_ready, i * G + b + 1)
                    o = ps_o[:, 0:H * (HD + 1)].rearrange("p (h d) -> p h d", d=HD + 1)
                    steps.then(nc.vector.reciprocal(inv[:, b % 2, :], o[:, :, HD]))
                    steps.settle()
                    nc.vector.tensor_tensor(att[:, b, :].rearrange("p (h d) -> p h d", d=HD), o[:, :, 0:HD],
                                            spread(inv[:, b % 2, :], HD), ALU.mult).then_inc(att_ready, 1)

                for b in range(G + 1):
                    if b < G:
                        shift(b)
                    if b > 0:
                        divide(b - 1)
                dve.wait_ge(out_ready, i + 1)
                y = y_all[:, bass.ds(i * G, G), :]
                o = ps_o[:].rearrange("p (g d) -> p g d", g=G)
                if rope:
                    steps.then(nc.vector.tensor_tensor(y, o, x, ALU.add))
                    steps.settle()
                    nc.vector.tensor_tensor(y, y, repeat(b_o[:], G), ALU.add).then_inc(group_done, 1)
                else:
                    nc.vector.tensor_tensor(y, o, x, ALU.add).then_inc(group_done, 1)
                steps.closed()


U = 2


def gelu_ffn(nc, stage, x_all, y_all, c, p):
    F = 4 * D
    KF = F // 128
    with ExitStack() as stack:
        m = Mem(nc, stack, stage)
        w1 = m.sb("w1", [D, F])
        w2 = m.sb("w2", [128, KF, D])
        b1 = m.sb("b1", [128, KF])
        b2 = m.sb("b2", [T, D])
        gain = m.sb("gain", [D, 2])
        before = [Norm(m, f"before{u}") for u in range(U)]
        after = [Norm(m, f"after{u}") for u in range(U)]
        yn = m.sb("yn", [T, U, G, D])
        ynT = m.sb("ynT", [D, U, GT])
        hidden = m.sb("hidden", [128, U, KF, GT])
        skip = m.sb("skip", [T, U, G, D])
        total = m.sb("total", [T, U, G, D])
        ps_a = m.ps("ps_a", [D, U, GT])
        ps_h = m.ps("ps_h", [128, 4, GT])
        ps_y = m.ps("ps_y", [T, U, G, D])

        loaded = m.sem("loaded")
        yn_ready = m.sem("yn_ready")
        yn_turned = m.sem("yn_turned")
        ynT_ready = m.sem("ynT_ready")
        h_ready = m.sem("h_ready")
        gelu_ready = m.sem("gelu_ready")
        out_ready = m.sem("out_ready")
        skip_ready = m.sem("skip_ready")
        total_ready = m.sem("total_ready")
        x_ready = m.sem("x_ready")
        dve_steps = m.sem("dve_steps")
        pool_steps = m.sem("pool_steps")
        block = stack.enter_context(nc.Block())
        ALL_LOADED = 16 * 6

        @block.sync
        def _(sp):
            for dst, src in ((w1[:], p["w1"]), (w2[:], p["w2"].rearrange("(k p) n -> p k n", p=128)),
                             (b1[:], p["b1"].rearrange("(k p) -> p k", p=128)), (b2[:], all_rows(p["b2"])),
                             (gain[:, 0:1], column(p["g"])), (gain[:, 1:2], column(p["b"]))):
                sp.dma_start(dst, src).then_inc(loaded, 16)

        @block.tensor
        def _(pe):
            pe.wait_ge(loaded, ALL_LOADED)
            with pe.Fori(0, NG // U) as i:
                for u in range(U):
                    for b in range(G):
                        pe.wait_ge(yn_ready, (i * U + u) * G + b + 1)
                        last = nc.tensor.transpose(ps_a[:, u, b * T:(b + 1) * T], yn[:, u, b, :], c.ident[:])
                    last.then_inc(yn_turned, 1)
                for u in range(U):
                    pe.wait_ge(ynT_ready, i * U + u + 1)
                    for k in range(KF):
                        if u > 0:
                            pe.wait_ge(gelu_ready, i * U * KF + (u - 1) * KF + k + 1)
                        nc.tensor.matmul(ps_h[:, k, :], w1[:, k * 128:(k + 1) * 128], ynT[:, u, :], start=True, stop=True).then_inc(h_ready, 1)
                for u in range(U):
                    for k in range(KF):
                        pe.wait_ge(gelu_ready, (i * U + u) * KF + k + 1)
                        for b in range(G):
                            last = nc.tensor.matmul(ps_y[:, u, b, :], hidden[:, u, k, b * T:(b + 1) * T], w2[:, k, :],
                                                    start=(k == 0 and b == 0), stop=(k == KF - 1 and b == G - 1), skip_group_check=True)
                    last.then_inc(out_ready, 1)
                pe.wait_ge(total_ready, i * U + U)

        @block.scalar
        def _(act):
            act.wait_ge(loaded, ALL_LOADED)
            with act.Fori(0, NG // U) as i:
                for u in range(U):
                    act.wait_ge(yn_turned, i * U + u + 1)
                    nc.scalar.activation(ynT[:, u, :], ps_a[:, u, :], ACT.Identity, bias=gain[:, 1:2], scale=gain[:, 0:1]).then_inc(ynT_ready, 1)
                for u in range(U):
                    for k in range(KF):
                        act.wait_ge(h_ready, (i * U + u) * KF + k + 1)
                        nc.scalar.activation(hidden[:, u, k, :], ps_h[:, k, :], ACT.Gelu, bias=b1[:, k:k + 1]).then_inc(gelu_ready, 1)

        @block.gpsimd
        def _(pool):
            pool.wait_ge(loaded, ALL_LOADED)
            with pool.Fori(0, NG // U) as i:
                steps = Steps(pool, pool_steps, i * U, U)
                for u in range(U):
                    before[u].root(nc, pool, c, i)
                for u in range(U):
                    at = bass.ds((i * U + u) * G, G)
                    steps.then(nc.gpsimd.tensor_tensor(skip[:, u, :, :], x_all[:, at, :], y_all[:, at, :], ALU.add))
                    steps.settle()
                    nc.gpsimd.tensor_tensor(skip[:, u, :, :], skip[:, u, :, :], repeat(b2[:], G), ALU.add).then_inc(skip_ready, 1)
                for u in range(U):
                    after[u].root(nc, pool, c, i)
                pool.wait_ge(total_ready, i * U + U)
                steps.closed()

        @block.vector
        def _(dve):
            dve.wait_ge(loaded, ALL_LOADED)
            with dve.Fori(0, NG // U) as i:
                steps = Steps(dve, dve_steps, i * 32, 32)
                y = [y_all[:, bass.ds((i * U + u) * G, G), :] for u in range(U)]
                for u in range(U):
                    before[u].take_moments(nc, steps, y[u])
                for u in range(U):
                    before[u].apply(nc, dve, y[u], lambda b: yn[:, u, b, :], i, yn_ready)
                for u in range(U):
                    dve.wait_ge(out_ready, i * U + u + 1)
                    dve.wait_ge(skip_ready, i * U + u + 1)
                    nc.vector.tensor_tensor(total[:, u, :, :], ps_y[:, u, :, :], skip[:, u, :, :], ALU.add).then_inc(total_ready, 1)
                    dve.wait_ge(total_ready, i * U + u + 1)
                    after[u].take_moments(nc, steps, total[:, u, :, :])
                for u in range(U):
                    after[u].apply(nc, dve, total[:, u, :, :], lambda b: x_all[:, bass.ds((i * U + u) * G + b, 1), :], i, x_ready)
                dve.wait_ge(x_ready, i * U * G + U * G)
                steps.closed()


def retention(nc, stage, x_all, ctx_dram, c, p):
    with ExitStack() as stack:
        m = Mem(nc, stack, stage)
        w_qg = m.sb("w_qg", [D, 2 * D])
        w_kv = m.sb("w_kv", [D, 2 * D])
        w_o = m.sb("w_o", [D, D])
        b_g = m.sb("b_g", [T, D])
        b_o = m.sb("b_o", [T, D])
        cos = m.sb("cos", [T, 2 * D])
        sin = m.sb("sin", [T, 2 * D])
        decay = m.sb("decay", [T, H, T])
        xg = m.sb("xg", [T, G, D])
        ctx = m.sb("ctx", [T, G, D])
        xT = m.sb("xT", [D, GT])
        ctxT = m.sb("ctxT", [D, GT])
        raw = m.sb("raw", [T, G, 2 * D])
        turned = m.sb("turned", [T, 2, 2 * D])
        PADDED = 2 * D + QUAD - HD
        qk = m.sb("qk", [T, G, PADDED])
        v = m.sb("v", [T, G, D])
        gate = m.sb("gate", [T, G, D])
        qT = m.sb("qT", [T, 2, NK, T])
        kT = m.sb("kT", [T, 2, NK, T])
        sim = m.sb("sim", [T, 2, NJ, NK, T])
        head_sum = m.sb("head_sum", [T, G * H])
        head_var = m.sb("head_var", [T, G * H])
        head_rstd = m.sb("head_rstd", [T, G * H])
        minus_half = m.sb("minus_half", [T, G * H])
        centred = m.sb("centred", [T, G * H, HD])
        square = m.sb("square", [T, G * H, HD])
        gated = m.sb("gated", [T, G, D])
        gatedT = m.sb("gatedT", [D, GT])
        skip = m.sb("skip", [T, G, D])
        total = m.sb("total", [T, G, D])
        after = Norm(m, "after")
        ps_s = m.ps("ps_s", [T, NJ, NK, T])
        ps_t = m.ps("ps_t", [T, 2, BANK])
        ps_a = m.ps("ps_a", [T, BANK])
        ps_o = m.ps("ps_o", [T, BANK])

        loaded = m.sem("loaded")
        group_in = m.sem("group_in")
        padded = m.sem("padded")
        x_turned = m.sem("x_turned")
        ctx_turned = m.sem("ctx_turned")
        xT_ready = m.sem("xT_ready")
        ctxT_ready = m.sem("ctxT_ready")
        proj_ready = m.sem("proj_ready")
        act_took = m.sem("act_took")
        gate_in = m.sem("gate_in")
        gate_ready = m.sem("gate_ready")
        qk_ready = m.sem("qk_ready")
        turn_filled = m.sem("turn_filled")
        turn_taken = m.sem("turn_taken")
        scores_ready = m.sem("scores_ready")
        sim_ready = m.sem("sim_ready")
        ret_ready = m.sem("ret_ready")
        centred_ready = m.sem("centred_ready")
        square_ready = m.sem("square_ready")
        head_var_ready = m.sem("head_var_ready")
        head_rstd_ready = m.sem("head_rstd_ready")
        gated_ready = m.sem("gated_ready")
        gated_turned = m.sem("gated_turned")
        gatedT_ready = m.sem("gatedT_ready")
        out_ready = m.sem("out_ready")
        skip_ready = m.sem("skip_ready")
        total_ready = m.sem("total_ready")
        x_ready = m.sem("x_ready")
        dve_steps = m.sem("dve_steps")
        pool_steps = m.sem("pool_steps")
        block = stack.enter_context(nc.Block())
        LOADS = ((w_qg[:, 0:D], p["w_q"]), (w_qg[:, D:2 * D], p["w_g"]), (w_kv[:, 0:D], p["w_k"]), (w_kv[:, D:2 * D], p["w_v"]),
                 (w_o[:], p["w_o"]), (b_g[:], all_rows(p["b_g"])), (b_o[:], all_rows(p["b_o"])),
                 (cos[:], p["cos"]), (sin[:], p["sin"]), (decay[:], p["decay"]))
        ALL_LOADED = 16 * len(LOADS)

        @block.sync
        def _(sp):
            for dst, src in LOADS:
                sp.dma_start(dst, src).then_inc(loaded, 16)
            for dst, src in ((xg, x_all), (ctx, ctx_dram)):
                sp.dma_start(dst[:], src[:, 0:G, :]).then_inc(group_in, 16)
            with sp.Fori(1, NG) as i:
                sp.wait_ge(ctx_turned, i)
                for dst, src in ((xg, x_all), (ctx, ctx_dram)):
                    sp.dma_start(dst[:], src[:, bass.ds(i * G, G), :]).then_inc(group_in, 16)

        @block.tensor
        def _(pe):
            pe.wait_ge(loaded, ALL_LOADED)
            with pe.Fori(0, NG) as i:
                pe.wait_ge(group_in, i * 32 + 32)
                for b in range(G):
                    last = nc.tensor.transpose(ps_a[:, b * T:(b + 1) * T], xg[:, b, :], c.ident[:])
                last.then_inc(x_turned, 1)
                for b in range(G):
                    last = nc.tensor.transpose(ps_o[:, b * T:(b + 1) * T], ctx[:, b, :], c.ident[:])
                last.then_inc(ctx_turned, 1)
                pe.wait_ge(xT_ready, i + 1)
                pe.wait_ge(ctxT_ready, i + 1)
                for b in range(G):
                    dst = (ps_a, ps_o)[b % 2]
                    if b >= 2:
                        pe.wait_ge(act_took, i * G + b - 1)
                    t = slice(b * T, (b + 1) * T)
                    nc.tensor.matmul(dst[:, 0:2 * D], xT[:, t], w_qg[:], start=True, stop=True, skip_group_check=True)
                    nc.tensor.matmul(dst[:, 2 * D:4 * D], ctxT[:, t], w_kv[:], start=False, stop=True, skip_group_check=True).then_inc(proj_ready, 1)

                def turn(b, n, at):
                    if b == 0:
                        pe.wait_ge(qk_ready, i * G + 1)
                    else:
                        pe.wait_ge(turn_taken, (i * G + b) * 2)
                    for k in range(NK):
                        last = nc.tensor.matmul(ps_t[:, n, k * T:(k + 1) * T], qk[:, b, at + k * HD:at + k * HD + T], c.ident[:], is_transpose=True,
                                                start=(k == 0), stop=(k == NK - 1), skip_group_check=True)
                    last.then_inc(turn_filled, 1)

                def scores(b):
                    pe.wait_ge(qk_ready, i * G + b + 1)
                    turn(b, 0, 0)
                    turn(b, 1, D)
                    pe.wait_ge(turn_taken, (i * G + b) * 2 + 2)
                    if b > 0:
                        pe.wait_ge(sim_ready, (i * G + b) * NJ)
                    for k in range(NK):
                        for j in range(NJ):
                            r = slice(j * QUAD, j * QUAD + HD)
                            last = nc.tensor.matmul(ps_s[:, j, k, :], kT[r, b % 2, k, :], qT[r, b % 2, k, :],
                                                    start=(k == 0), stop=(k == NK - 1), skip_group_check=True)
                            if k == NK - 1:
                                last.then_inc(scores_ready, 1)

                def values(b):
                    for j in range(NJ):
                        pe.wait_ge(sim_ready, (i * G + b) * NJ + j + 1)
                        for k in range(NK):
                            h = NK * j + k
                            last = nc.tensor.matmul(ps_o[:, b * D + h * HD:b * D + (h + 1) * HD], sim[:, b % 2, j, k, :], v[:, b, h * HD:(h + 1) * HD],
                                                    start=(b == 0 and h == 0), stop=(b == G - 1 and h == H - 1), skip_group_check=True)
                    if b == G - 1:
                        last.then_inc(ret_ready, 1)

                pe.wait_ge(gate_in, i * G + G)
                pe.wait_ge(act_took, i * G + G)
                for b in range(G + 1):
                    if b < G:
                        scores(b)
                    if b > 0:
                        values(b - 1)
                pe.wait_ge(gated_ready, i + 1)
                for b in range(G):
                    last = nc.tensor.transpose(ps_a[:, b * T:(b + 1) * T], gated[:, b, :], c.ident[:])
                last.then_inc(gated_turned, 1)
                pe.wait_ge(gatedT_ready, i + 1)
                for b in range(G):
                    last = nc.tensor.matmul(ps_o[:, b * D:(b + 1) * D], gatedT[:, b * T:(b + 1) * T], w_o[:],
                                            start=(b == 0), stop=(b == G - 1), skip_group_check=True)
                last.then_inc(out_ready, 1)
                pe.wait_ge(total_ready, i + 1)

        @block.scalar
        def _(act):
            act.wait_ge(loaded, ALL_LOADED)
            with act.Fori(0, NG) as i:
                act.wait_ge(x_turned, i + 1)
                nc.scalar.copy(xT[:], ps_a[:]).then_inc(xT_ready, 1)
                act.wait_ge(ctx_turned, i + 1)
                nc.scalar.copy(ctxT[:], ps_o[:]).then_inc(ctxT_ready, 1)
                for b in range(G):
                    src = (ps_a, ps_o)[b % 2]
                    act.wait_ge(gate_in, i * G + b + 1)
                    nc.scalar.copy(v[:, b, :], src[:, 3 * D:4 * D])
                    nc.scalar.copy(bn(raw[:, b, 0:1], (D, 2), (1, D)), bn(src[:, 0:1], (2 * D, 2), (1, D))).then_inc(act_took, 1)
                act.wait_ge(gate_in, i * G + G)
                nc.scalar.activation(gate[:], gate[:], ACT.Silu).then_inc(gate_ready, 1)
                for b in range(G):
                    for n, dst in enumerate((qT, kT)):
                        act.wait_ge(turn_filled, (i * G + b) * 2 + n + 1)
                        nc.scalar.copy(dst[:, b % 2, :, :], ps_t[:, n, :]).then_inc(turn_taken, 1)
                act.wait_ge(centred_ready, i + 1)
                nc.scalar.activation(square[:], centred[:], ACT.Square).then_inc(square_ready, 1)
                act.wait_ge(gated_turned, i + 1)
                nc.scalar.copy(gatedT[:], ps_a[:]).then_inc(gatedT_ready, 1)

        @block.gpsimd
        def _(pool):
            pool.memset(qk[:, :, 2 * D:PADDED], 0.0).then_inc(padded, 1)
            pool.memset(minus_half[:], -0.5).then_inc(padded, 1)
            pool.wait_ge(loaded, ALL_LOADED)
            pool.wait_ge(padded, 2)
            with pool.Fori(0, NG) as i:
                steps = Steps(pool, pool_steps, i * (G * 3), G * 3)
                for b in range(G):
                    pool.wait_ge(act_took, i * G + b + 1)
                    pairs = raw[:, b, :].rearrange("p (h s) -> p h s", s=2)
                    t = turned[:, b % 2, :].rearrange("p (h s) -> p h s", s=2)
                    s = sin[:].rearrange("p (h s) -> p h s", s=2)
                    steps.then(nc.gpsimd.tensor_tensor(t[:, :, 0], pairs[:, :, 1], s[:, :, 0], ALU.mult))
                    steps.then(nc.gpsimd.tensor_tensor(t[:, :, 1], pairs[:, :, 0], s[:, :, 1], ALU.mult))
                    steps.then(nc.gpsimd.tensor_tensor(qk[:, b, 0:2 * D], raw[:, b, :], cos[:], ALU.mult))
                    steps.settle()
                    nc.gpsimd.tensor_tensor(qk[:, b, 0:2 * D], qk[:, b, 0:2 * D], turned[:, b % 2, :], ALU.add).then_inc(qk_ready, 1)
                pool.wait_ge(gate_ready, i + 1)
                nc.gpsimd.tensor_tensor(skip[:], x_all[:, bass.ds(i * G, G), :], repeat(b_o[:], G), ALU.add).then_inc(skip_ready, 1)
                pool.wait_ge(head_var_ready, i + 1)
                nc.gpsimd.tensor_tensor(head_rstd[:], head_var[:], minus_half[:], ALU.pow).then_inc(head_rstd_ready, 1)
                after.root(nc, pool, c, i)
                steps.closed()

        @block.vector
        def _(dve):
            dve.wait_ge(loaded, ALL_LOADED)
            dve.wait_ge(padded, 2)
            with dve.Fori(0, NG) as i:
                per_loop = 11
                steps = Steps(dve, dve_steps, i * per_loop, per_loop)
                for b in range(G):
                    src = (ps_a, ps_o)[b % 2]
                    dve.wait_ge(proj_ready, i * G + b + 1)
                    nc.vector.tensor_tensor(gate[:, b, :], src[:, D:2 * D], b_g[:], ALU.add).then_inc(gate_in, 1)
                for b in range(G):
                    for j in range(NJ):
                        dve.wait_ge(scores_ready, (i * G + b) * NJ + j + 1)
                        nc.vector.tensor_tensor(sim[:, b % 2, j, :, :], ps_s[:, j, :, :], decay[:, NK * j:NK * (j + 1), :], ALU.mult).then_inc(sim_ready, 1)
                dve.wait_ge(ret_ready, i + 1)
                ret = ps_o[:].rearrange("p (n d) -> p n d", d=HD)
                steps.then(nc.vector.tensor_reduce(head_sum[:], ret, AX_X, ALU.add))
                steps.settle()
                nc.vector.scalar_tensor_tensor(out=centred[:], in0=spread(head_sum[:], HD), scalar=-1.0 / HD, in1=ret, op0=ALU.mult, op1=ALU.add)\
                    .then_inc(centred_ready, 1)
                dve.wait_ge(square_ready, i + 1)
                steps.then(nc.vector.tensor_reduce(head_var[:], square[:], AX_X, ALU.add))
                steps.settle()
                nc.vector.tensor_scalar(head_var[:], head_var[:], 1.0 / HD, LN_EPS, ALU.mult, ALU.add).then_inc(head_var_ready, 1)
                dve.wait_ge(gate_ready, i + 1)
                g = gate[:].rearrange("p b (h d) -> p (b h) d", d=HD)
                steps.then(nc.vector.tensor_tensor(centred[:], centred[:], g, ALU.mult))
                steps.settle()
                dve.wait_ge(head_rstd_ready, i + 1)
                nc.vector.tensor_tensor(gated[:].rearrange("p b (h d) -> p (b h) d", d=HD), centred[:], spread(head_rstd[:], HD), ALU.mult).then_inc(gated_ready, 1)
                dve.wait_ge(out_ready, i + 1)
                dve.wait_ge(skip_ready, i + 1)
                nc.vector.tensor_tensor(total[:], ps_o[:].rearrange("p (g d) -> p g d", g=G), skip[:], ALU.add).then_inc(total_ready, 1)
                dve.wait_ge(total_ready, i + 1)
                after.take_moments(nc, steps, total[:])
                after.apply(nc, dve, total[:], lambda b: x_all[:, bass.ds(i * G + b, 1), :], i, x_ready)
                dve.wait_ge(x_ready, i * G + G)
                steps.closed()


def moe(nc, stage, x_all, y_all, c, p):
    E, F = 8, 256
    KF = F // 128
    ORDER = [E] + list(range(E))
    with ExitStack() as stack:
        m = Mem(nc, stack, stage)
        w_gate = m.sb("w_gate", [D, E + 1, F])
        w_up = m.sb("w_up", [D, E + 1, F])
        w_down = m.sb("w_down", [128, E + 1, KF, D])
        w_router = m.sb("w_router", [D, E])
        gain = m.sb("gain", [D, 1])
        number = m.sb("number", [T, E])
        before = Norm(m, "before", rms=True)
        after = Norm(m, "after")
        yn = m.sb("yn", [T, G, D])
        ynT = m.sb("ynT", [D, GT])
        silu = m.sb("silu", [128, KF, GT])
        hidden = m.sb("hidden", [128, 2, KF, GT])
        acc = m.sb("acc", [T, G, D])
        skip = m.sb("skip", [T, G, D])
        logit_top = m.sb("logit_top", [T, G])
        shifted = m.sb("shifted", [T, G, E])
        prob = m.sb("prob", [T, G, E])
        prob_sum = m.sb("prob_sum", [T, G])
        prob_inv = m.sb("prob_inv", [T, G])
        best = m.sb("best", [T, G, 8])
        best_at = m.sb("best_at", [T, G, 8], U32)
        at = m.sb("at", [T, G, 2])
        gap = m.sb("gap", [T, G])
        weight = m.sb("weight", [T, G, 2])
        weight_sum = m.sb("weight_sum", [T, G])
        chosen = m.sb("chosen", [T, G, 2, E])
        combine = m.sb("combine", [T, G, E])
        ps_g = m.ps("ps_g", [128, KF, GT])
        ps_u = m.ps("ps_u", [128, KF, GT])
        ps_d = m.ps("ps_d", [T, 2, G, D])
        ps_a = m.ps("ps_a", [D, GT])
        ps_r = m.ps("ps_r", [T, BANK])

        loaded = m.sem("loaded")
        yn_ready = m.sem("yn_ready")
        yn_turned = m.sem("yn_turned")
        ynT_ready = m.sem("ynT_ready")
        gate_ready = m.sem("gate_ready")
        up_ready = m.sem("up_ready")
        silu_ready = m.sem("silu_ready")
        hidden_ready = m.sem("hidden_ready")
        down_ready = m.sem("down_ready")
        down_taken = m.sem("down_taken")
        logits_ready = m.sem("logits_ready")
        shifted_ready = m.sem("shifted_ready")
        exp_ready = m.sem("exp_ready")
        gap_ready = m.sem("gap_ready")
        weight_ready = m.sem("weight_ready")
        skip_ready = m.sem("skip_ready")
        x_ready = m.sem("x_ready")
        dve_steps = m.sem("dve_steps")
        passed = m.sem("passed")
        block = stack.enter_context(nc.Block())
        LOADS = ((w_gate[:, 0:E, :], p["e_gate"].rearrange("e d f -> d e f")), (w_gate[:, E, :], p["sh_gate"]),
                 (w_up[:, 0:E, :], p["e_up"].rearrange("e d f -> d e f")), (w_up[:, E, :], p["sh_up"]),
                 (w_down[:, 0:E, :, :], p["e_down"].rearrange("e (k q) d -> q e k d", q=128)),
                 (w_down[:, E, :, :], p["sh_down"].rearrange("(k q) d -> q k d", q=128)),
                 (w_router[:], p["router"]), (gain[:], column(p["gain"])), (number[:], p["number"]))
        ALL_LOADED = 16 * len(LOADS)
        NE = len(ORDER)

        @block.sync
        def _(sp):
            for dst, src in LOADS:
                sp.dma_start(dst, src).then_inc(loaded, 16)

        @block.tensor
        def _(pe):
            pe.wait_ge(loaded, ALL_LOADED)

            def turn(n):
                for b in range(G):
                    pe.wait_ge(yn_ready, n * G + b + 1)
                    last = nc.tensor.transpose(ps_a[:, b * T:(b + 1) * T], yn[:, b, :], c.ident[:])
                last.then_inc(yn_turned, 1)

            def group(i, more, first=False):
                def up(o):
                    e = ORDER[o]
                    for k in range(KF):
                        if not (first and o == 0):
                            pe.wait_ge(silu_ready, (i * NE + o - 1) * KF + k + 1)
                        nc.tensor.matmul(ps_g[:, k, :], w_gate[:, e, k * 128:(k + 1) * 128], ynT[:], start=True, stop=True).then_inc(gate_ready, 1)
                        if not (first and o == 0):
                            pe.wait_ge(hidden_ready, (i * NE + o - 1) * KF + k + 1)
                        last = nc.tensor.matmul(ps_u[:, k, :], w_up[:, e, k * 128:(k + 1) * 128], ynT[:], start=True, stop=True)
                        last.then_inc(up_ready, 1)

                def down(o):
                    e = ORDER[o]
                    if not (first and o < 2):
                        pe.wait_ge(down_taken, i * NE + max(o - 1, 0))
                    for k in range(KF):
                        pe.wait_ge(hidden_ready, (i * NE + o) * KF + k + 1)
                        for b in range(G):
                            last = nc.tensor.matmul(ps_d[:, o % 2, b, :], hidden[:, o % 2, k, b * T:(b + 1) * T], w_down[:, e, k, :],
                                                    start=(k == 0 and b == 0), stop=(k == KF - 1 and b == G - 1), skip_group_check=True)
                    last.then_inc(down_ready, 1)

                pe.wait_ge(ynT_ready, i + 1)
                for o in range(NE):
                    up(o)
                    if o == 0:
                        for b in range(G):
                            last = nc.tensor.matmul(ps_r[:, b * E:(b + 1) * E], ynT[:, b * T:(b + 1) * T], w_router[:],
                                                    start=(b == 0), stop=(b == G - 1), skip_group_check=True)
                        last.then_inc(logits_ready, 1)
                    if o > 0:
                        down(o - 1)
                    if o == 5 and more:
                        turn(i + 1)
                down(NE - 1)

            turn(0)
            group(0, True, first=True)
            with pe.Fori(1, NG - 1) as i:
                group(i, True)
            group(NG - 1, False)

        @block.scalar
        def _(act):
            act.wait_ge(loaded, ALL_LOADED)

            def copy_turned(n, after_group):
                act.wait_ge(yn_turned, n + 1)
                if after_group is not None:
                    act.wait_ge(up_ready, (after_group + 1) * (NE * KF))
                nc.scalar.activation(ynT[:], ps_a[:], ACT.Copy, scale=gain[:, 0:1]).then_inc(ynT_ready, 1)

            def group(i, more, first=False):
                for o in range(NE):
                    for k in range(KF):
                        act.wait_ge(gate_ready, (i * NE + o) * KF + k + 1)
                        if not (first and o == 0):
                            act.wait_ge(hidden_ready, (i * NE + o - 1) * KF + k + 1)
                        nc.scalar.activation(silu[:, k, :], ps_g[:, k, :], ACT.Silu).then_inc(silu_ready, 1)
                    if o == 1:
                        act.wait_ge(shifted_ready, i + 1)
                        nc.scalar.activation(prob[:], shifted[:], ACT.Exp).then_inc(exp_ready, 1)
                        act.wait_ge(gap_ready, i + 1)
                        nc.scalar.activation(weight[:, :, 1], gap[:], ACT.Exp).then_inc(weight_ready, 1)
                if more:
                    copy_turned(i + 1, i)

            copy_turned(0, None)
            group(0, True, first=True)
            with act.Fori(1, NG - 1) as i:
                group(i, True)
            group(NG - 1, False)

        @block.gpsimd
        def _(pool):
            pool.wait_ge(loaded, ALL_LOADED)

            def group(i, more):
                at_i = bass.ds(i * G, G)
                nc.gpsimd.tensor_tensor(skip[:], x_all[:, at_i, :], y_all[:, at_i, :], ALU.add).then_inc(skip_ready, 1)
                if more:
                    before.root(nc, pool, c, i + 1)
                after.root(nc, pool, c, i)

            before.root(nc, pool, c, 0)
            with pool.Fori(0, NG - 1) as i:
                group(i, True)
            group(NG - 1, False)

        @block.vector
        def _(dve):
            dve.wait_ge(loaded, ALL_LOADED)

            def normed(steps, n):
                y = y_all[:, bass.ds(n * G, G), :]
                before.take_moments(nc, steps, y)
                before.apply(nc, dve, y, lambda b: yn[:, b, :], n, yn_ready)

            def route(steps, i):
                dve.wait_ge(logits_ready, i + 1)
                logits = ps_r[:, 0:G * E].rearrange("p (g e) -> p g e", e=E)
                steps.then(nc.vector.tensor_reduce(logit_top[:], logits, AX_X, ALU.max))
                steps.settle()
                nc.vector.tensor_tensor(shifted[:], logits, spread(logit_top[:], E), ALU.subtract).then_inc(shifted_ready, 1)
                dve.wait_ge(exp_ready, i + 1)
                steps.then(nc.vector.tensor_reduce(prob_sum[:], prob[:], AX_X, ALU.add))
                steps.settle()
                steps.then(nc.vector.reciprocal(prob_inv[:], prob_sum[:]))
                steps.settle()
                steps.then(nc.vector.tensor_tensor(prob[:], prob[:], spread(prob_inv[:], E), ALU.mult))
                steps.settle_apart(passed)
                for b in range(G):
                    steps.then(nc.vector.max(best[:, b, :], prob[:, b, :]))
                steps.settle_apart(passed)
                for b in range(G):
                    steps.then(nc.vector.max_index(best_at[:, b, :], best[:, b, :], prob[:, b, :]))
                nc.vector.tensor_tensor(gap[:], best[:, :, 1], best[:, :, 0], ALU.subtract).then_inc(gap_ready, 1)
                steps.settle()
                steps.then(nc.vector.tensor_copy(at[:], best_at[:, :, 0:2]))
                dve.wait_ge(weight_ready, i + 1)
                steps.then(nc.vector.tensor_scalar(weight_sum[:], weight[:, :, 1], 1.0, None, ALU.add))
                steps.settle()
                steps.then(nc.vector.reciprocal(weight[:, :, 0], weight_sum[:]))
                number_all = bn(number[:, 0:1], (0, G * 2), (1, E))
                steps.then(nc.vector.tensor_tensor(chosen[:].rearrange("p g n e -> p (g n) e"), number_all,
                                                   spread(at[:].rearrange("p g n -> p (g n)"), E), ALU.is_equal))
                steps.settle()
                steps.then(nc.vector.tensor_tensor(weight[:, :, 1], weight[:, :, 1], weight[:, :, 0], ALU.mult))
                steps.settle()
                steps.then(nc.vector.tensor_tensor(chosen[:].rearrange("p g n e -> p (g n) e"), chosen[:].rearrange("p g n e -> p (g n) e"),
                                                   spread(weight[:].rearrange("p g n -> p (g n)"), E), ALU.mult))
                steps.settle()
                steps.then(nc.vector.tensor_tensor(combine[:], chosen[:, :, 0, :], chosen[:, :, 1, :], ALU.add))
                steps.settle()

            def group(i, more, steps, first=False):
                def multiply(o):
                    for k in range(KF):
                        dve.wait_ge(silu_ready, (i * NE + o) * KF + k + 1)
                        dve.wait_ge(up_ready, (i * NE + o) * KF + k + 1)
                        nc.vector.tensor_tensor(hidden[:, o % 2, k, :], silu[:, k, :], ps_u[:, k, :], ALU.mult).then_inc(hidden_ready, 1)

                def add(o):
                    dve.wait_ge(down_ready, i * NE + o + 1)
                    if o == 0:
                        dve.wait_ge(skip_ready, i + 1)
                        nc.vector.tensor_tensor(acc[:], ps_d[:, o % 2, :, :], skip[:], ALU.add).then_inc(down_taken, 1)
                        return
                    dve.wait_ge(down_taken, i * NE + o)
                    for b in range(G):
                        e = ORDER[o]
                        ins = nc.vector.scalar_tensor_tensor(out=acc[:, b, :], in0=ps_d[:, o % 2, b, :], scalar=combine[:, b, e:e + 1],
                                                             in1=acc[:, b, :], op0=ALU.mult, op1=ALU.add)
                        if b < G - 1:
                            steps.then(ins)
                    ins.then_inc(down_taken, 1)
                    steps.settle()

                for o in range(NE):
                    multiply(o)
                    if o == 0:
                        route(steps, i)
                    if o > 0:
                        add(o - 1)
                    if o == 3 and more:
                        normed(steps, i + 1)
                add(NE - 1)
                dve.wait_ge(down_taken, (i + 1) * NE)
                after.take_moments(nc, steps, acc[:])
                after.apply(nc, dve, acc[:], lambda b: x_all[:, bass.ds(i * G + b, 1), :], i, x_ready)
                dve.wait_ge(x_ready, i * G + G)

            HEAD, per_loop = p["steps"]
            steps = Steps(dve, dve_steps)
            normed(steps, 0)
            assert steps.n == HEAD, steps.n
            group(0, True, Steps(dve, dve_steps, HEAD, per_loop), first=True)
            with dve.Fori(1, NG - 1) as i:
                steps = Steps(dve, dve_steps, i * per_loop + HEAD, per_loop)
                group(i, True, steps)
                steps.closed()
            group(NG - 1, False, Steps(dve, dve_steps, (NG - 1) * per_loop + HEAD, per_loop))


LOG1P = (0.9999999698793575, -0.4999949313792134, 0.333190967542795, -0.2484298178988968, 0.19106005102618012,
         -0.13663242268700254, 0.07822591031320165, -0.029505213253769987, 0.005232687895002128)


class Fills:

    def __init__(self, base):
        self.base, self.n = base, 0

    def next(self):
        self.n += 1
        return self.base + self.n - 1, (self.n - 1) % 2


def mamba(nc, stage, x_all, c, p):
    DT, N, R, W = 2, 16, D // 16, 4
    PAD = W - 1
    TP = T + PAD
    C2 = 2
    CH = N // C2
    S = CH * DT
    SLOTS = 4
    ROWS = 3 * 2 * N
    with ExitStack() as stack:
        m = Mem(nc, stack, stage)
        w_in = m.sb("w_in", [D, 2, 2 * DT * 128])
        w_tap = m.sb("w_tap", [D, 2, W, DT * 128])
        b_conv = m.sb("b_conv", [128, 2, DT])
        w_bc = m.sb("w_bc", [128, 2, DT, ROWS + R])
        w_dt = m.sb("w_dt", [128, 2, DT * 128])
        b_dt = m.sb("b_dt", [128, 2, DT])
        a_log = m.sb("a_log", [128, 2, DT, N])
        a_neg = m.sb("a_neg", [128, 2, DT, N])
        d_skip = m.sb("d_skip", [128, 2, DT])
        w_out = m.sb("w_out", [128, 2, DT, D])
        pick = m.sb("pick", [ROWS, 2 * N, 128], BF16)
        xg = m.sb("xg", [T, G, D])
        xT = m.sb("xT", [D, 2, G, TP])
        uz = m.sb("uz", [128, 2, 2 * DT, GT])
        u, sz = uz[:, :, 0:DT, :], uz[:, :, DT:2 * DT, :]
        bc = m.sb("bc", [128, 2, GT])
        rest = m.sb("rest", [ROWS, GT])
        mid = m.sb("mid", [ROWS, GT], BF16)
        parts = m.sb("parts", [ROWS, 2, GT], BF16)
        pre = m.sb("pre", [128, DT, GT])
        soft = m.sb("soft", [128, DT, GT])
        poly = m.sb("poly", [128, DT, GT])
        delta = m.sb("delta", [128, 2, DT, GT])
        du = m.sb("du", [128, 2, DT, GT])
        decay = m.sb("decay", [128, SLOTS, C2, G, T])
        h = m.sb("h", [128, SLOTS, C2, GT])
        c_all = m.sb("c_all", [128, SLOTS, C2, GT])
        y = m.sb("y", [128, DT, GT])
        g = m.sb("g", [128, 2, DT, G, T])
        half = m.sb("half", [T, G, D])
        total = m.sb("total", [T, G, D])
        after = Norm(m, "after")
        ps_b = m.ps("ps_b", [128, 2, C2, GT])
        ps_y = m.ps("ps_y", [128, DT, GT])
        ps_t = m.ps("ps_t", [128, 2, BANK])

        loaded = m.sem("loaded")
        prepared = m.sem("prepared")
        a_ready = m.sem("a_ready")
        group_in = m.sem("group_in")
        filled = m.sem("filled")
        taken = m.sem("taken")
        parts_ready = m.sem("parts_ready")
        pre_exp = m.sem("pre_exp")
        act_steps = m.sem("act_steps")
        soft_ready = m.sem("soft_ready")
        silu_ready = m.sem("silu_ready")
        delta_ready = m.sem("delta_ready")
        b_ready = m.sem("b_ready")
        decay_ready = m.sem("decay_ready")
        h_ready = m.sem("h_ready")
        hc_ready = m.sem("hc_ready")
        y_done = m.sem("y_done")
        y_read = m.sem("y_read")
        g_ready = m.sem("g_ready")
        total_ready = m.sem("total_ready")
        x_ready = m.sem("x_ready")
        dve_steps = m.sem("dve_steps")
        block = stack.enter_context(nc.Block())
        LOADS = []
        for d, s in enumerate(("f", "b")):
            q = lambda name: p["a"][f"L1_attn_{name}_{s}"]
            LOADS += [(w_in[:, d, :], q("inW")), (b_conv[:, d, :], q("convB").rearrange("(t q) -> q t", q=128)),
                      (w_dt[ROWS:ROWS + R, d, :], q("dtW")), (b_dt[:, d, :], q("dtB").rearrange("(t q) -> q t", q=128)),
                      (a_log[:, d, :, :], q("Alog").rearrange("(t q) n -> q t n", q=128)),
                      (d_skip[:, d, :], q("Dp").rearrange("(t q) -> q t", q=128)),
                      (w_out[:, d, :, :], q("outW").rearrange("(t q) n -> q t n", q=128)),
                      (w_bc[:, d, :, ROWS:ROWS + R], q("xpW").rearrange("(t q) n -> q t n", q=128)[:, :, 0:R])]
            LOADS += [(w_tap[:, d, k, :], all_rows(q("convW")[k, :])) for k in range(W)]
            LOADS += [(w_bc[:, d, :, k * 2 * N:(k + 1) * 2 * N], q("xpW").rearrange("(t q) n -> q t n", q=128)[:, :, R:R + 2 * N]) for k in range(3)]
        ALL_LOADED = 16 * len(LOADS)
        PRO = 8 + C2
        PER = 2 * (7 + N) + 2
        ALL_TAKEN = 2

        AT_X, AT_CONV, AT_Z, AT_SILU, AT_BC, AT_DELTA, AT_LOG, AT_OUT, AT_GATE = 1, (3, 4), (5, 6), 7, 8, (9, 10), (11, 12, 13), 3, 1
        LAG = 2

        def fillings(d, s, head=True):
            n = C2 * (s % DT == 0 and (s + DT < S or head)) + (s == AT_OUT and d == 0)
            return n + head * ((s == AT_X and d == 1) + (s in AT_CONV) + (s in AT_Z) + (s == AT_BC) + (s in AT_DELTA))

        def fillings_before(d, s, more=True):
            return sum(fillings(0, r) for r in range(S if d else s)) + sum(fillings(1, r, more) for r in range(s if d else 0))

        def taken_by(i, n):
            return i * PER + (PRO + ALL_TAKEN + n)

        assert PER == fillings_before(1, S)
        TURNED = PRO + fillings_before(1, AT_X) + fillings(1, AT_X)

        @block.sync
        def _(sp):
            for dst, src in LOADS:
                sp.dma_start(dst, src).then_inc(loaded, 16)
            sp.dma_start(xg[:], x_all[:, 0:G, :]).then_inc(group_in, 16)
            sp.wait_ge(filled, 1)
            sp.dma_start(xg[:], x_all[:, G:2 * G, :]).then_inc(group_in, 16)
            with sp.Fori(2, NG) as i:
                sp.wait_ge(filled, i * PER + TURNED - 2 * PER)
                sp.dma_start(xg[:], x_all[:, bass.ds(i * G, G), :]).then_inc(group_in, 16)

        @block.tensor
        def _(pe):
            pe.wait_ge(loaded, ALL_LOADED)
            pe.wait_ge(prepared, 4 + ROWS // (2 * N))

            def fill(f, emit):
                seq, bank = f.next()
                pe.wait_ge(taken, seq + 1)
                emit(ps_t[:, bank, :]).then_inc(filled, 1)
                return seq

            def turn_x(f, n):
                pe.wait_ge(group_in, n * 16 + 16)

                def emit(dst):
                    for b in range(G):
                        last = nc.tensor.transpose(dst[:, b * T:(b + 1) * T], xg[:, b, :], c.ident[:])
                    return last
                fill(f, emit)

            def conv(f, d, t):
                pe.wait_ge(taken, f.base + f.n + 1)

                def emit(dst):
                    for k in range(W):
                        last = nc.tensor.matmul(dst, w_tap[:, d, k, t * 128:(t + 1) * 128], xT[:, d, :, k:k + T], start=(k == 0), stop=(k == W - 1))
                    return last
                fill(f, emit)

            def gate(f, d, t):
                at = (DT + t) * 128
                fill(f, lambda dst: nc.tensor.matmul(dst, w_in[:, d, at:at + 128], xT[:, d, :, PAD:TP], start=True, stop=True))

            def bc_dt(f, d):
                def emit(dst):
                    for t in range(DT):
                        last = nc.tensor.matmul(dst[0:ROWS + R, :], w_bc[:, d, t, :], u[:, d, t, :], start=(t == 0), stop=(t == DT - 1))
                    return last
                fill(f, emit)

            def delta_in(f, d, t):
                fill(f, lambda dst: nc.tensor.matmul(dst, w_dt[ROWS:ROWS + R, d, t * 128:(t + 1) * 128], bc[ROWS:ROWS + R, d, :], start=True, stop=True))

            def c_rows(f, d, chunk):
                for n in range(C2):
                    fill(f, lambda dst: nc.tensor.matmul(dst, pick[:, N + chunk * C2 + n, :], parts[:, d, :], start=True, stop=True))

            def b_rows(q, d, s, slot, spare=False):
                if not spare:
                    pe.wait_ge(h_ready, q - 1)
                for n in range(C2):
                    last = nc.tensor.matmul(ps_b[:, slot, n, :], pick[:, (s // DT) * C2 + n, :], parts[:, d, :], start=True, stop=True)
                last.then_inc(b_ready, 1)

            def sum_states(q, d, s):
                pe.wait_ge(hc_ready, q + 1)
                for n in range(C2):
                    last = nc.tensor.matmul(ps_y[:, s % DT, :], c.ident[:], h[:, s % SLOTS, n, :], start=(s < DT and n == 0),
                                            stop=(s >= S - DT and n == C2 - 1))
                last.then_inc(y_done, 1)

            def output(f, n):
                pe.wait_ge(g_ready, n * 2 * DT + 2 * DT)

                def emit(dst):
                    for b in range(G):
                        for o in range(2 * DT):
                            d, t = o // DT, o % DT
                            last = nc.tensor.matmul(dst[:, b * D:(b + 1) * D], g[:, d, t, b, :], w_out[:, d, t, :],
                                                    start=(b == 0 and o == 0), stop=(b == G - 1 and o == 2 * DT - 1), skip_group_check=True)
                    return last
                fill(f, emit)

            def copied(f):
                pe.wait_ge(taken, f.base + f.n + ALL_TAKEN)

            def group(i, more, first=False):
                f = Fills(i * PER + PRO)
                for d in range(2):
                    head = d == 0 or more
                    nd = 1 - d
                    for s in range(S):
                        q = i * (2 * S) + d * S + s
                        if s + 1 < S or head:
                            if s + 1 == S:
                                pe.wait_ge(parts_ready, i * 2 + d + 2)
                            b_rows(q + 1, d if s + 1 < S else nd, (s + 1) % S, (s + 1) % 2, spare=first and d == 0 and s == 0)
                        if s % DT == 0 and (s + DT < S or head):
                            if s + DT == S:
                                pe.wait_ge(parts_ready, i * 2 + d + 2)
                            c_rows(f, d if s + DT < S else nd, (s // DT + 1) % CH)
                        if s == AT_X and d == 1 and more:
                            turn_x(f, i + 1)
                        if head:
                            for t in range(DT):
                                if s == AT_CONV[t]:
                                    if t == 0 and d == 1:
                                        copied(f)
                                    conv(f, nd, t)
                                if s == AT_Z[t]:
                                    gate(f, nd, t)
                            if s == AT_BC:
                                pe.wait_ge(silu_ready, i * 2 + d + 2)
                                bc_dt(f, nd)
                            for t in range(DT):
                                if s == AT_DELTA[t]:
                                    if t == 0:
                                        copied(f)
                                    delta_in(f, nd, t)
                        if s == AT_OUT and d == 0:
                            if first:
                                fill(f, lambda dst: nc.tensor.matmul(dst, c.ident[:], xT[:, 0, :, PAD:TP], start=True, stop=True))
                            else:
                                output(f, i - 1)
                        if not (first and d == 0 and s < LAG):
                            if s == LAG:
                                if not (first and d == 0):
                                    pe.wait_ge(y_read, (i * 2 + d) * DT)
                            sum_states(q - LAG, d, (s - LAG) % S)
                    if not head:
                        for s in range(S - LAG, S):
                            sum_states(i * (2 * S) + d * S + s, d, s)
                return f

            f = Fills(0)
            turn_x(f, 0)
            copied(f)
            for t in range(DT):
                conv(f, 0, t)
            for t in range(DT):
                gate(f, 0, t)
            pe.wait_ge(silu_ready, 1)
            bc_dt(f, 0)
            copied(f)
            for t in range(DT):
                delta_in(f, 0, t)
            pe.wait_ge(parts_ready, 1)
            c_rows(f, 0, 0)
            b_rows(0, 0, 0, 0, spare=True)
            assert f.n == PRO
            group(0, True, first=True)
            with pe.Fori(1, NG - 1) as i:
                assert group(i, True).n == PER
            f = group(NG - 1, False)
            output(f, NG - 1)

        @block.scalar
        def _(act):
            for at in range(0, ROWS, 2 * N):
                nc.scalar.copy(pick[at:at + 2 * N, :, :], spread(c.ident[at:at + 2 * N, at:at + 2 * N], 128)).then_inc(prepared, 1)
            act.wait_ge(loaded, ALL_LOADED)
            act.sem_inc(taken, ALL_TAKEN)
            nc.scalar.activation(a_neg[:], a_log[:], ACT.Exp).then_inc(pre_exp, 1)
            act.wait_ge(a_ready, 1)
            act.wait_ge(prepared, 4 + ROWS // (2 * N))

            def take(f, emit):
                seq, bank = f.next()
                act.wait_ge(filled, seq + 1)
                emit(ps_t[:, bank, :]).then_inc(taken, 1)

            def halve(f):
                take(f, lambda src: nc.scalar.activation(half[:], src.rearrange("p (g d) -> p g d", g=G), ACT.Copy, scale=0.5))

            def copy_x(f):
                def emit(src):
                    src = src.rearrange("p (g t) -> p g t", g=G)
                    nc.scalar.copy(xT[:, 0, :, PAD:TP], src)
                    back = bn(src[:, 0, T - 1:T], (T, G), (-1, T))
                    return nc.scalar.copy(xT[:, 1, :, PAD:TP], back)
                take(f, emit)

            def copy_u(f, d, t):
                take(f, lambda src: nc.scalar.activation(u[:, d, t, :], src, ACT.Identity, bias=b_conv[:, d, t:t + 1]))

            def copy_z(f, d, t):
                take(f, lambda src: nc.scalar.copy(sz[:, d, t, :], src))

            def silu(f, d):
                act.wait_ge(taken, f.base + f.n + ALL_TAKEN)
                nc.scalar.activation(uz[:, d, :, :], uz[:, d, :, :], ACT.Silu).then_inc(silu_ready, 1)

            def copy_bc(f, d):
                take(f, lambda src: nc.scalar.copy(bc[0:ROWS + R, d, :], src[0:ROWS + R, :]))

            def softplus(f, steps, d, t, n):
                if n is not None and t == 0:
                    act.wait_ge(delta_ready, n)
                take(f, lambda src: nc.scalar.activation(pre[:, t, :], src, ACT.Identity, bias=b_dt[:, d, t:t + 1]))
                if t == DT - 1:
                    act.wait_ge(taken, f.base + f.n + ALL_TAKEN)
                    steps.then(nc.scalar.activation(soft[:], pre[:], ACT.Abs))
                    steps.settle()
                    nc.scalar.activation(soft[:], soft[:], ACT.Exp, scale=-1.0).then_inc(soft_ready, 1)

            def copy_c(f, q, slot, spare=False):
                if not spare:
                    act.wait_ge(hc_ready, q - (SLOTS - 1) * DT)
                for n in range(C2):
                    take(f, lambda src: nc.scalar.copy(c_all[:, slot, n, :], src))

            def exps(q, d, s, spare=False):
                if not spare:
                    act.wait_ge(h_ready, q - SLOTS + 1)
                src = delta[:, d, s % DT, :].rearrange("p (g t) -> p g t", g=G)[:, :, 1:T]
                for n in range(C2):
                    st = (s // DT) * C2 + n
                    last = nc.scalar.activation(decay[:, s % SLOTS, n, :, 1:T], src, ACT.Exp, scale=a_neg[:, d, s % DT, st:st + 1])
                last.then_inc(decay_ready, 1)

            def group(i, more, first=False):
                f = Fills(i * PER + PRO)
                steps = Steps(act, act_steps, i * 2 + 1, 2)
                for d in range(2):
                    head = d == 0 or more
                    nd = 1 - d
                    for s in range(S):
                        q = i * (2 * S) + d * S + s
                        if s + 1 < S or head:
                            if s + 1 == S:
                                act.wait_ge(delta_ready, i * 2 + d + 2)
                            exps(q + 1, d if s + 1 < S else nd, (s + 1) % S, spare=first and d == 0 and s + 1 < SLOTS)
                        if s % DT == 0 and (s + DT < S or head):
                            copy_c(f, q + DT, (s // DT + 1) % SLOTS, spare=first and d == 0 and s // DT + 1 < SLOTS)
                        if s == AT_X and d == 1 and more:
                            copy_x(f)
                        if head:
                            for t in range(DT):
                                if s == AT_CONV[t]:
                                    if t == 0 and not (first and d == 0):
                                        act.wait_ge(g_ready, (i * 2 + d) * DT)
                                    copy_u(f, nd, t)
                                if s == AT_Z[t]:
                                    copy_z(f, nd, t)
                            if s == AT_SILU:
                                silu(f, nd)
                            if s == AT_BC:
                                copy_bc(f, nd)
                            for t in range(DT):
                                if s == AT_DELTA[t]:
                                    softplus(f, steps, nd, t, i * 2 + d + 1)
                        if s == AT_OUT and d == 0:
                            halve(f)
                return f

            f = Fills(0)
            copy_x(f)
            for t in range(DT):
                copy_u(f, 0, t)
            for t in range(DT):
                copy_z(f, 0, t)
            silu(f, 0)
            copy_bc(f, 0)
            steps = Steps(act, act_steps)
            for t in range(DT):
                softplus(f, steps, 0, t, None)
            copy_c(f, 0, 0, spare=True)
            act.wait_ge(delta_ready, 1)
            exps(0, 0, 0, spare=True)
            group(0, True, first=True)
            with act.Fori(1, NG - 1) as i:
                group(i, True)
            f = group(NG - 1, False)
            halve(f)

        @block.gpsimd
        def _(pool):
            pool.memset(xT[:, :, :, 0:PAD], 0.0).then_inc(prepared, 1)
            for slot in range(SLOTS):
                last = pool.memset(decay[:, slot, :, :, 0], 0.0)
            last.then_inc(prepared, 1)

            def group(i, more, first=False):
                for d in range(2):
                    for s in range(S):
                        q = i * (2 * S) + d * S + s
                        if s % DT == 0:
                            if s > 0:
                                pool.wait_ge(taken, taken_by(i, fillings_before(d, s - DT, more) + C2))
                            else:
                                pool.wait_ge(taken, taken_by(i, d and fillings_before(0, S - DT) + C2))
                        pool.wait_ge(h_ready, q + 1)
                        slot, chunk = s % SLOTS, (s // DT) % SLOTS
                        nc.gpsimd.tensor_tensor(h[:, slot, :, :], h[:, slot, :, :], c_all[:, chunk, :, :], ALU.mult).then_inc(hc_ready, 1)
                        if s == AT_OUT + 2 and d == 0 and not first:
                            after.root(nc, pool, c, i - 1)

            group(0, True, first=True)
            with pool.Fori(1, NG - 1) as i:
                group(i, True)
            group(NG - 1, False)
            after.root(nc, pool, c, NG - 1)

        @block.vector
        def _(dve):
            dve.wait_ge(loaded, ALL_LOADED)
            for d in range(2):
                nc.vector.tensor_tensor(w_tap[:, d, :, :], w_tap[:, d, :, :], repeat(w_in[:, d, 0:DT * 128], W), ALU.mult).then_inc(prepared, 1)
            dve.wait_ge(pre_exp, 1)
            nc.vector.tensor_scalar(a_neg[:], a_neg[:], -1.0, None, ALU.mult).then_inc(a_ready, 1)

            def split(steps, d, copied):
                dve.wait_ge(taken, copied)
                whole = bc[0:ROWS, d, :]
                steps.then(nc.vector.tensor_copy(parts[:, d, :], whole))
                steps.settle()
                steps.then(nc.vector.tensor_tensor(rest[:], whole, parts[:, d, :], ALU.subtract))
                steps.settle()
                steps.then(nc.vector.tensor_copy(mid[:], rest[:]))
                steps.then(nc.vector.tensor_copy(parts[32:64, d, :], rest[32:64, :]))
                steps.settle()
                nc.vector.tensor_tensor(parts[64:ROWS, d, :], rest[64:ROWS, :], mid[64:ROWS, :], ALU.subtract).then_inc(parts_ready, 1)

            def log1p(steps, part):
                if part == 0:
                    steps.then(nc.vector.tensor_scalar(poly[:], soft[:], LOG1P[8], LOG1P[7], ALU.mult, ALU.add))
                    steps.settle()
                    steps.then(nc.vector.tensor_tensor(poly[:], poly[:], soft[:], ALU.mult))
                    steps.settle()
                for k in {0: (6, 5), 1: (4, 3, 2), 2: (1, 0)}[part]:
                    steps.then(nc.vector.scalar_tensor_tensor(out=poly[:], in0=poly[:], scalar=LOG1P[k], in1=soft[:], op0=ALU.add, op1=ALU.mult))
                    steps.settle()

            def deltas(steps, d, n):
                nc.vector.scalar_tensor_tensor(out=delta[:, d, :, :], in0=pre[:], scalar=0.0, in1=poly[:], op0=ALU.max, op1=ALU.add)\
                    .then_inc(delta_ready, 1)
                dve.wait_ge(delta_ready, n + 1)
                steps.then(nc.vector.tensor_tensor(du[:, d, :, :], delta[:, d, :, :], u[:, d, :, :], ALU.mult))
                steps.settle()

            def gating(steps, d, n):
                dve.wait_ge(y_done, (n + 1) * S)
                for t in range(DT):
                    nc.vector.scalar_tensor_tensor(out=y[:, t, :], in0=u[:, d, t, :], scalar=d_skip[:, d, t:t + 1], in1=ps_y[:, t, :],
                                                   op0=ALU.mult, op1=ALU.add).then_inc(y_read, 1)
                for t in range(DT):
                    dve.wait_ge(y_read, n * DT + t + 1)
                    dst = g[:, d, t, :, :] if d == 0 else bn(g[:, d, t, 0, T - 1:T], (T, G), (-1, T))
                    nc.vector.tensor_tensor(dst, y[:, t, :].rearrange("p (g t) -> p g t", g=G), sz[:, d, t, :].rearrange("p (g t) -> p g t", g=G), ALU.mult)\
                        .then_inc(g_ready, 1)

            def total_of(steps, n, copied):
                dve.wait_ge(taken, copied)
                nc.vector.tensor_tensor(total[:], half[:], x_all[:, bass.ds(n * G, G), :], ALU.add).then_inc(total_ready, 1)
                dve.wait_ge(total_ready, n + 1)
                after.take_moments(nc, steps, total[:])

            def finish(n):
                after.apply(nc, dve, total[:], lambda b: x_all[:, bass.ds(n * G + b, 1), :], n, x_ready)
                dve.wait_ge(x_ready, n * G + G)

            def group(i, more, steps, first=False):
                for d in range(2):
                    head = d == 0 or more
                    nd = 1 - d
                    for s in range(S):
                        q = i * (2 * S) + d * S + s
                        dve.wait_ge(b_ready, q + 1)
                        b = ps_b[:, s % 2, :, :]
                        steps.then(nc.vector.tensor_tensor(b, b, repeat(du[:, d, s % DT, :], C2), ALU.mult))
                        steps.settle()
                        dve.wait_ge(decay_ready, q + 1)
                        if not (first and d == 0 and s < SLOTS):
                            dve.wait_ge(y_done, q - SLOTS + 1)
                        nc.vector.tensor_tensor_scan(h[:, s % SLOTS, :, :].rearrange("p n t -> p (n t)"),
                                                     decay[:, s % SLOTS, :, :, :].rearrange("p n g t -> p (n g t)"),
                                                     b.rearrange("p n t -> p (n t)"), 0.0, ALU.mult, ALU.add).then_inc(h_ready, 1)
                        if s == AT_GATE and not (first and d == 0):
                            gating(steps, nd, i * 2 + d - 1)
                        if head:
                            if s == AT_BC + 1:
                                split(steps, nd, taken_by(i, fillings_before(d, AT_BC + 1)))
                            if s in AT_LOG:
                                if s == AT_LOG[0]:
                                    dve.wait_ge(soft_ready, i * 2 + d + 2)
                                log1p(steps, s - AT_LOG[0])
                            if s == AT_LOG[-1]:
                                deltas(steps, nd, i * 2 + d + 1)
                        if d == 0 and not first:
                            if s == AT_OUT + 1:
                                total_of(steps, i - 1, taken_by(i, fillings_before(0, AT_OUT + 1)))
                            if s == AT_OUT + 4:
                                finish(i - 1)

            HEAD = 4 + 9 + 1
            FIRST, per_loop = 2 * S + 2 * HEAD, 2 * S + 2 * HEAD + 2 * G
            steps = Steps(dve, dve_steps)
            split(steps, 0, 1 + 2 * DT + 1 + ALL_TAKEN)
            dve.wait_ge(soft_ready, 1)
            for part in range(3):
                log1p(steps, part)
            deltas(steps, 0, 0)
            assert steps.n == HEAD
            steps = Steps(dve, dve_steps, HEAD)
            group(0, True, steps, first=True)
            assert steps.n == FIRST
            with dve.Fori(1, NG - 1) as i:
                steps = Steps(dve, dve_steps, i * per_loop + HEAD + FIRST - per_loop, per_loop)
                group(i, True, steps)
                steps.closed()
            steps = Steps(dve, dve_steps, (NG - 1) * per_loop + HEAD + FIRST - per_loop)
            group(NG - 1, False, steps)
            gating(steps, 1, NG * 2 - 1)
            total_of(steps, NG - 1, taken_by(NG - 1, fillings_before(1, S, False) + 1))
            finish(NG - 1)


def cross_attention(nc, stage, x_all, ctx_dram, c, p):
    XH, XD = 8, D // 8
    XK = XH // NJ
    PAIRS = G // 2
    N2 = 2 * T
    with ExitStack() as stack:
        m = Mem(nc, stack, stage)
        PADDED = D + QUAD - XD
        w_q = m.sb("w_q", [D, PADDED])
        w_k = m.sb("w_k", [D, PADDED])
        w_v = m.sb("w_v", [D, D])
        w_o = m.sb("w_o", [D, D])
        xg = m.sb("xg", [T, G, D])
        ctx = m.sb("ctx", [T, G, D])
        xT = m.sb("xT", [D, GT])
        ctxT = m.sb("ctxT", [D, GT])
        qT = m.sb("qT", [T, XK, GT])
        kT = m.sb("kT", [T, XK, GT])
        v = m.sb("v", [T, G, D])
        e = m.sb("e", [T, PAIRS, XH, N2])
        top = m.sb("top", [T, PAIRS, N2])
        total_e = m.sb("total_e", [T, PAIRS, N2])
        inv = m.sb("inv", [T, PAIRS, N2])
        att = m.sb("att", [T, G, D])
        attT = m.sb("attT", [D, GT])
        total = m.sb("total", [T, G, D])
        after = Norm(m, "after")
        ps_s = m.ps("ps_s", [T, NJ, XK, N2])
        ps_t = m.ps("ps_t", [T, 2, BANK])
        ps_o = m.ps("ps_o", [T, BANK])
        ps_y = m.ps("ps_y", [T, BANK])

        loaded = m.sem("loaded")
        group_in = m.sem("group_in")
        padded = m.sem("padded")
        filled = m.sem("filled")
        taken = m.sem("taken")
        scores_ready = m.sem("scores_ready")
        shifted = m.sem("shifted")
        exp_ready = m.sem("exp_ready")
        inv_ready = m.sem("inv_ready")
        att_w_ready = m.sem("att_w_ready")
        values_ready = m.sem("values_ready")
        att_ready = m.sem("att_ready")
        out_ready = m.sem("out_ready")
        total_ready = m.sem("total_ready")
        x_ready = m.sem("x_ready")
        dve_steps = m.sem("dve_steps")
        block = stack.enter_context(nc.Block())
        LOADS = ((w_q[:, 0:D], p["w_q"]), (w_k[:, 0:D], p["w_k"]), (w_v[:], p["w_v"]), (w_o[:], p["w_o"]))
        ALL_LOADED = 16 * len(LOADS)
        FIRST, PER = 7, 8
        ALL_TAKEN = 2

        @block.sync
        def _(sp):
            for dst, src in LOADS:
                sp.dma_start(dst, src).then_inc(loaded, 16)
            for dst, src in ((xg, x_all), (ctx, ctx_dram)):
                sp.dma_start(dst[:], src[:, 0:G, :]).then_inc(group_in, 16)

            def next_group(i):
                for dst, src in ((xg, x_all), (ctx, ctx_dram)):
                    sp.dma_start(dst[:], src[:, bass.ds(i * G, G), :]).then_inc(group_in, 16)

            sp.wait_ge(filled, 2)
            next_group(1)
            with sp.Fori(2, NG) as i:
                sp.wait_ge(filled, i * PER - PER + 1)
                next_group(i)

        @block.tensor
        def _(pe):
            pe.wait_ge(loaded, ALL_LOADED)
            pe.wait_ge(padded, 2)

            def fill(seq, bank, emit):
                pe.wait_ge(taken, seq + 1)
                emit(ps_t[:, bank, :]).then_inc(filled, 1)

            def turn(src):
                def emit(dst):
                    for b in range(G):
                        last = nc.tensor.transpose(dst[:, b * T:(b + 1) * T], src[:, b, :], c.ident[:])
                    return last
                return emit

            def head(n, seq, bank):
                pe.wait_ge(group_in, n * 32 + 32)
                fill(seq, bank, turn(xg))
                fill(seq + 1, 1 - bank, turn(ctx))
                pe.wait_ge(taken, seq + 2 + ALL_TAKEN)
                for o, (w, src) in enumerate(((w_q, xT), (w_q, xT), (w_k, ctxT), (w_k, ctxT))):
                    k = o % 2
                    fill(seq + 2 + o, (bank + o) % 2, lambda dst: nc.tensor.matmul(dst, w[:, k * XD:k * XD + T], src[:], start=True, stop=True))

            def values_in(seq, bank):
                def emit(dst):
                    for b in range(G):
                        last = nc.tensor.matmul(dst[:, b * D:(b + 1) * D], ctxT[:, b * T:(b + 1) * T], w_v[:],
                                                start=(b == 0), stop=(b == G - 1), skip_group_check=True)
                    return last
                fill(seq, bank, emit)

            def scores(i, pair, first=False):
                if not (first and pair == 0):
                    pe.wait_ge(shifted, i * PAIRS + pair)
                for n in range(2):
                    t = slice((pair * 2 + n) * T, (pair * 2 + n + 1) * T)
                    for k in range(XK):
                        for j in range(NJ):
                            r = slice(j * QUAD, j * QUAD + XD)
                            last = nc.tensor.matmul(ps_s[:, j, k, n * T:(n + 1) * T], kT[r, k, t], qT[r, k, t],
                                                    start=(n == 0 and k == 0), stop=(n == 1 and k == XK - 1), skip_group_check=True)
                last.then_inc(scores_ready, 1)

            def values(i, pair):
                pe.wait_ge(att_w_ready, i * PAIRS + pair + 1)
                for n in range(2):
                    b = pair * 2 + n
                    for h in range(XH):
                        last = nc.tensor.matmul(ps_o[:, b * D + h * XD:b * D + (h + 1) * XD], e[:, pair, h, n * T:(n + 1) * T], v[:, b, h * XD:(h + 1) * XD],
                                                start=(b == 0 and h == 0), stop=(b == G - 1 and h == XH - 1), skip_group_check=True)
                if pair == PAIRS - 1:
                    last.then_inc(values_ready, 1)

            def group(i, more, first=False):
                seq = i * PER + FIRST
                pe.wait_ge(taken, seq + ALL_TAKEN)
                for pair in range(PAIRS):
                    scores(i, pair, first)
                if more:
                    head(i + 1, seq, FIRST % 2)
                for pair in range(PAIRS):
                    values(i, pair)
                if more:
                    values_in(seq + 6, (FIRST + 6) % 2)
                pe.wait_ge(att_ready, i + 1)
                n = 7 if more else 0
                fill(seq + n, (FIRST + n) % 2, turn(att))
                pe.wait_ge(taken, seq + n + 1 + ALL_TAKEN)
                if not first:
                    pe.wait_ge(total_ready, i)
                for b in range(G):
                    last = nc.tensor.matmul(ps_y[:, b * D:(b + 1) * D], attT[:, b * T:(b + 1) * T], w_o[:],
                                            start=(b == 0), stop=(b == G - 1), skip_group_check=True)
                last.then_inc(out_ready, 1)

            head(0, 0, 0)
            values_in(6, 0)
            group(0, True, first=True)
            with pe.Fori(1, NG - 1) as i:
                group(i, True)
            group(NG - 1, False)

        @block.scalar
        def _(act):
            act.sem_inc(taken, ALL_TAKEN)

            def copy_out(seq, bank, dst):
                act.wait_ge(filled, seq + 1)
                nc.scalar.copy(dst, ps_t[:, bank, :]).then_inc(taken, 1)

            def head(seq, bank):
                for o, dst in enumerate((xT[:], ctxT[:], qT[:, 0, :], qT[:, 1, :], kT[:, 0, :], kT[:, 1, :])):
                    copy_out(seq + o, (bank + o) % 2, dst)

            def group(i, more):
                seq = i * PER + FIRST
                for pair in range(PAIRS):
                    act.wait_ge(shifted, i * PAIRS + pair + 1)
                    nc.scalar.activation(e[:, pair, :, :], e[:, pair, :, :], ACT.Exp, scale=XD ** -0.5).then_inc(exp_ready, 1)
                if more:
                    head(seq, FIRST % 2)
                act.wait_ge(values_ready, i + 1)
                nc.scalar.copy(att[:], ps_o[:].rearrange("p (g d) -> p g d", g=G)).then_inc(att_ready, 1)
                if more:
                    copy_out(seq + 6, (FIRST + 6) % 2, v[:])
                n = 7 if more else 0
                copy_out(seq + n, (FIRST + n) % 2, attT[:])

            head(0, 0)
            copy_out(6, 0, v[:])
            with act.Fori(0, NG - 1) as i:
                group(i, True)
            group(NG - 1, False)

        @block.gpsimd
        def _(pool):
            pool.memset(w_q[:, D:PADDED], 0.0).then_inc(padded, 1)
            pool.memset(w_k[:, D:PADDED], 0.0).then_inc(padded, 1)
            with pool.Fori(0, NG) as i:
                for pair in range(PAIRS):
                    pool.wait_ge(inv_ready, i * PAIRS + pair + 1)
                    nc.gpsimd.tensor_tensor(e[:, pair, :, :], e[:, pair, :, :], repeat(inv[:, pair, :], XH), ALU.mult).then_inc(att_w_ready, 1)
                after.root(nc, pool, c, i)

        @block.vector
        def _(dve):
            with dve.Fori(0, NG) as i:
                steps = Steps(dve, dve_steps, i * 12, 12)
                for pair in range(PAIRS):
                    dve.wait_ge(scores_ready, i * PAIRS + pair + 1)
                    s = ps_s[:].rearrange("p j k n -> p (j k) n")
                    steps.then(nc.vector.tensor_reduce(top[:, pair, :], s.rearrange("p h n -> p n h"), AX_X, ALU.max))
                    steps.settle()
                    nc.vector.tensor_tensor(e[:, pair, :, :], s, repeat(top[:, pair, :], XH), ALU.subtract).then_inc(shifted, 1)
                for pair in range(PAIRS):
                    dve.wait_ge(exp_ready, i * PAIRS + pair + 1)
                    steps.then(nc.vector.tensor_reduce(total_e[:, pair, :], e[:, pair, :, :].rearrange("p h n -> p n h"), AX_X, ALU.add))
                    steps.settle()
                    nc.vector.reciprocal(inv[:, pair, :], total_e[:, pair, :]).then_inc(inv_ready, 1)
                dve.wait_ge(out_ready, i + 1)
                nc.vector.tensor_tensor(total[:], ps_y[:].rearrange("p (g d) -> p g d", g=G), x_all[:, bass.ds(i * G, G), :], ALU.add)\
                    .then_inc(total_ready, 1)
                dve.wait_ge(total_ready, i + 1)
                after.take_moments(nc, steps, total[:])
                after.apply(nc, dve, total[:], lambda b: x_all[:, bass.ds(i * G + b, 1), :], i, x_ready)
                dve.wait_ge(x_ready, i * G + G)
                steps.closed()


MAGIC = 1.5 * 2.0 ** 23


def quant_ffn(nc, stage, x_all, out_dram, c, p):
    F = 3 * 128
    KF = F // 128
    BLOCK = 32
    NB = 4
    PIECE = KF * B * T // NB
    with ExitStack() as stack:
        m = Mem(nc, stack, stage)
        w_raw = m.sb("w_raw", [128, 3, F])
        w_amax = m.sb("w_amax", [128, 3, F // BLOCK])
        w_scale = m.sb("w_scale", [128, 3, F // BLOCK])
        w_T = m.sb("w_T", [128, 3, F])
        w_inv = m.sb("w_inv", [128, 3, F // BLOCK])
        w_head = m.sb("w_head", [128, 3, F // BLOCK])
        w_tail = m.sb("w_tail", [128, 3, F // BLOCK])
        amax_part = m.sb("amax_part", [128, 5])
        amax = m.sb("amax", [128, 5])
        scale = m.sb("scale", [128, 5])
        inv = m.sb("inv", [128, 5])
        amax_in = m.sb("amax_in", [128, 2, NG * KF])
        amax_left = m.sb("amax_left", [128, 3 * F // BLOCK])
        amax_piece = m.sb("amax_piece", [128, 2, NB])
        xq = m.sb("xq", [T, U, G, D])
        xqT = m.sb("xqT", [D, U, GT])
        gate = m.sb("gate", [128, NG, KF, GT])
        up = m.sb("up", [128, NG, KF, GT])
        sig = m.sb("sig", [128, 2, PIECE])
        hidden = m.sb("hidden", [128, U, KF, GT])
        total = m.sb("total", [T, U, G, D])
        res = m.sb("res", [T, U, G, D])
        after = [Norm(m, f"after{u}") for u in range(U)]
        ps_x = m.ps("ps_x", [128, U, BANK])
        ps_f = m.ps("ps_f", [128, 2, KF, GT])

        loaded = m.sem("loaded")
        w_rounded = m.sem("w_rounded")
        w_turned = m.sem("w_turned")
        wT_ready = m.sem("wT_ready")
        part_ready = m.sem("part_ready")
        amax_ready = m.sem("amax_ready")
        xq_ready = m.sem("xq_ready")
        xq_turned = m.sem("xq_turned")
        xqT_ready = m.sem("xqT_ready")
        ff_ready = m.sem("ff_ready")
        ff_taken = m.sem("ff_taken")
        ff_measured = m.sem("ff_measured")
        gate_ready = m.sem("gate_ready")
        sig_ready = m.sem("sig_ready")
        sig_used = m.sem("sig_used")
        hidden_ready = m.sem("hidden_ready")
        down_ready = m.sem("down_ready")
        total_ready = m.sem("total_ready")
        res_ready = m.sem("res_ready")
        stored = [m.sem(f"stored{u}") for u in range(U)]
        dve_steps = m.sem("dve_steps")
        block = stack.enter_context(nc.Block())
        W_GATE, W_UP, W_DOWN = range(3)
        A_X, A_UP, A_GATE, A_SWISH, A_OUT = range(5)
        gate_flat = gate[:].rearrange("p n k t -> p (n k t)")
        sig_flat = sig[:].rearrange("p n t -> p (n t)")
        up_flat = up[:].rearrange("p n k t -> p (n k t)")

        @block.sync
        def _(sp):
            for n, w in ((W_GATE, "w_gate"), (W_UP, "w_up")):
                sp.dma_start(w_raw[:, n, :].rearrange("p (k i) -> p k i", i=D), p[w].rearrange("(k q) i -> q k i", q=128)).then_inc(loaded, 16)
            sp.dma_start(w_raw[:, W_DOWN, :], p["w_down"]).then_inc(loaded, 16)
            with sp.Fori(0, NG // U) as i:
                for u in range(U):
                    sp.wait_ge(res_ready, (i * U + u) * G + G)
                    sp.dma_start(out_dram[:, bass.ds((i * U + u) * G, G), :], res[:, u, :, :]).then_inc(stored[u], 16)
            for u in range(U):
                sp.wait_ge(stored[u], 16 * (NG // U))

        @block.tensor
        def _(pe):
            pe.wait_ge(w_rounded, 1)
            for n in range(3):
                for k in range(KF):
                    last = nc.tensor.transpose(ps_f[:, 0, n, k * 128:(k + 1) * 128], w_raw[:, n, k * 128:(k + 1) * 128], c.ident[:])
            last.then_inc(w_turned, 1)
            pe.wait_ge(wT_ready, 1)

            def feed_forward(n, u, first=False):
                for b in range(G):
                    pe.wait_ge(xq_ready, n * G + b + 1)
                    last = nc.tensor.transpose(ps_x[:, u, b * T:(b + 1) * T], xq[:, u, b, :], c.ident[:])
                last.then_inc(xq_turned, 1)
                pe.wait_ge(xqT_ready, n + 1)
                for w in (W_GATE, W_UP):
                    for k in range(KF):
                        if not first:
                            pe.wait_ge(ff_taken, n * 2 * KF - 2 * KF + w * KF + k + 1)
                        nc.tensor.matmul(ps_f[:, w, k, :], w_T[:, w, k * 128:(k + 1) * 128], xqT[:, u, :], start=True, stop=True).then_inc(ff_ready, 1)

            for u in range(U):
                feed_forward(u, u, first=u == 0)
            with pe.Fori(1, NG // U) as i:
                for u in range(U):
                    feed_forward(i * U + u, u)
            with pe.Fori(0, NG // U) as i:
                for u in range(U):
                    pe.wait_ge(hidden_ready, i * U + u + 1)
                    for b in range(G):
                        for k in range(KF):
                            last = nc.tensor.matmul(ps_x[:, u, b * D:(b + 1) * D], hidden[:, u, k, b * T:(b + 1) * T], w_T[:, W_DOWN, k * 128:(k + 1) * 128],
                                                    start=(b == 0 and k == 0), stop=(b == G - 1 and k == KF - 1), skip_group_check=True)
                    last.then_inc(down_ready, 1)

        @block.scalar
        def _(act):
            act.wait_ge(w_turned, 1)
            nc.scalar.copy(w_T[:], ps_f[:, 0, :, 0:F]).then_inc(wT_ready, 1)
            with act.Fori(0, NG // U) as i:
                for u in range(U):
                    n = i * U + u
                    act.wait_ge(xq_turned, n + 1)
                    nc.scalar.copy(xqT[:, u, :], ps_x[:, u, :]).then_inc(xqT_ready, 1)
                    for w, dst in ((W_GATE, gate), (W_UP, up)):
                        for k in range(KF):
                            act.wait_ge(ff_ready, n * 2 * KF + w * KF + k + 1)
                            nc.scalar.copy(dst[:, bass.ds(n, 1), k, :], ps_f[:, w, k, :].unsqueeze(1)).then_inc(ff_taken, 1)
            for n in range(NB):
                act.wait_ge(gate_ready, n + 1)
                if n >= 2:
                    act.wait_ge(sig_used, n - 1)
                nc.scalar.activation(sig[:, n % 2, :], gate_flat[:, n * PIECE:(n + 1) * PIECE], ACT.Sigmoid).then_inc(sig_ready, 1)

        @block.gpsimd
        def _(pool):
            for n, columns in enumerate((slice(A_X, A_X + 1), slice(A_UP, A_GATE + 1), slice(A_SWISH, A_SWISH + 1), slice(A_OUT, A_OUT + 1))):
                pool.wait_ge(part_ready, n + 1)
                nc.gpsimd.partition_all_reduce(amax[:, columns], amax_part[:, columns], 128, bass.bass_isa.ReduceOp.max).then_inc(amax_ready, 1)
            with pool.Fori(0, NG // U) as i:
                for u in range(U):
                    after[u].root(nc, pool, c, i)

        @block.vector
        def _(dve):
            steps = Steps(dve, dve_steps)

            def share(out, largest, q):
                steps.then(nc.vector.tensor_scalar(out, largest, 1.0 / q, None, ALU.mult))
                steps.settle()
                left = amax_left[:, 0:out.shape[-1]]
                steps.then(nc.vector.scalar_tensor_tensor(out=left, in0=out, scalar=-(q + 1.0), in1=largest, op0=ALU.mult, op1=ALU.add))
                steps.settle()
                steps.then(nc.vector.tensor_tensor(left, left, out, ALU.add))
                steps.settle()
                steps.then(nc.vector.scalar_tensor_tensor(out=out, in0=left, scalar=1.0 / q, in1=out, op0=ALU.mult, op1=ALU.add))
                steps.settle()
                steps.then(nc.vector.tensor_scalar(out, out, 1e-12, None, ALU.max))
                steps.settle()

            def scales(n, columns):
                dve.wait_ge(amax_ready, n)
                share(scale[:, columns], amax[:, columns], 2.0 ** 15 - 1.0)
                steps.then(nc.vector.reciprocal(inv[:, columns], scale[:, columns]))
                steps.settle()

            def quantize(steps, out, src, a, tmp=None):
                tmp = out if tmp is None else tmp
                steps.then(nc.vector.tensor_scalar(tmp, src, inv[:, a:a + 1], MAGIC, ALU.mult, ALU.add))
                steps.settle()
                return nc.vector.tensor_scalar(out, tmp, MAGIC, scale[:, a:a + 1], ALU.subtract, ALU.mult)

            nc.vector.tensor_reduce(amax_part[:, A_X:A_X + 1], x_all[:].rearrange("p b d -> p (b d)"), AX_X, ALU.max, apply_absolute_value=True)\
                .then_inc(part_ready, 1)
            dve.wait_ge(loaded, 48)
            blocks = w_raw[:].rearrange("p n (m j) -> p n m j", j=BLOCK)
            steps.then(nc.vector.tensor_reduce(w_amax[:], blocks, AX_X, ALU.max, apply_absolute_value=True))
            steps.settle()
            flat = lambda t: t[:].rearrange("p n m -> p (n m)")
            share(flat(w_scale), flat(w_amax), 7.0)
            steps.then(nc.vector.reciprocal(w_inv[:], w_scale[:]))
            steps.then(nc.vector.tensor_scalar(w_head[:], w_scale[:], 2.0 ** 12 + 1.0, None, ALU.mult))
            steps.settle()
            steps.then(nc.vector.tensor_tensor(w_tail[:], w_head[:], w_scale[:], ALU.subtract))
            steps.settle()
            steps.then(nc.vector.tensor_tensor(w_head[:], w_head[:], w_tail[:], ALU.subtract))
            steps.settle()
            steps.then(nc.vector.tensor_tensor(w_tail[:], w_scale[:], w_head[:], ALU.subtract))
            s_all, inv_all, head_all, tail_all = [spread(flat(t), BLOCK) for t in (w_scale, w_inv, w_head, w_tail)]
            w_all = w_raw[:].rearrange("p n (m j) -> p (n m) j", j=BLOCK)
            W = 3 * F
            quot, q_head, product, rest = [sig_flat[:, n * W:(n + 1) * W].rearrange("p (m j) -> p m j", j=BLOCK) for n in range(4)]
            steps.then(nc.vector.tensor_tensor(quot, w_all, inv_all, ALU.mult))
            steps.settle()
            steps.then(nc.vector.tensor_scalar(q_head, quot, MAGIC / 256.0, MAGIC / 256.0, ALU.add, ALU.subtract))
            steps.settle()
            steps.then(nc.vector.tensor_tensor(product, q_head, head_all, ALU.mult))
            steps.settle()
            steps.then(nc.vector.tensor_tensor(rest, w_all, product, ALU.subtract))
            steps.settle()
            steps.then(nc.vector.tensor_tensor(product, q_head, tail_all, ALU.mult))
            steps.then(nc.vector.tensor_tensor(q_head, quot, q_head, ALU.subtract))
            steps.settle()
            steps.then(nc.vector.tensor_tensor(rest, rest, product, ALU.subtract))
            steps.settle()
            steps.then(nc.vector.tensor_tensor(q_head, q_head, s_all, ALU.mult))
            steps.settle()
            steps.then(nc.vector.tensor_tensor(rest, rest, q_head, ALU.subtract))
            steps.settle()
            steps.then(nc.vector.tensor_tensor(rest, rest, inv_all, ALU.mult))
            steps.settle()
            steps.then(nc.vector.tensor_tensor(w_all, quot, rest, ALU.add))
            steps.settle()
            steps.then(nc.vector.tensor_scalar(w_all, w_all, MAGIC, MAGIC, ALU.add, ALU.subtract))
            steps.settle()
            steps.then(nc.vector.tensor_scalar(w_all, w_all, 7.0, -8.0, ALU.min, ALU.max))
            steps.settle()
            nc.vector.tensor_tensor(w_all, w_all, s_all, ALU.mult).then_inc(w_rounded, 1)

            scales(1, slice(A_X, A_X + 1))
            base = steps.n

            def round_x(steps, n, u):
                x = x_all[:, bass.ds(n * G, G), :]
                steps.then(nc.vector.tensor_scalar(xq[:, u, :, :], x, inv[:, A_X:A_X + 1], MAGIC, ALU.mult, ALU.add))
                steps.settle()
                for b in range(G):
                    nc.vector.tensor_scalar(xq[:, u, b, :], xq[:, u, b, :], MAGIC, scale[:, A_X:A_X + 1], ALU.subtract, ALU.mult).then_inc(xq_ready, 1)

            with dve.Fori(0, NG // U) as i:
                loop = Steps(dve, dve_steps, i * U + base, U)
                for u in range(U):
                    round_x(loop, i * U + u, u)
                for u in range(U):
                    n = i * U + u
                    for w, src in ((W_GATE, gate), (W_UP, up)):
                        for k in range(KF):
                            dve.wait_ge(ff_taken, n * 2 * KF + w * KF + k + 1)
                            nc.vector.tensor_reduce(amax_in[:, 1 - w, bass.ds(n * KF + k, 1)], src[:, bass.ds(n, 1), k, :].rearrange("p a t -> p (a t)"),
                                                    AX_X, ALU.max, apply_absolute_value=True).then_inc(ff_measured, 1)
                loop.closed()
            steps.base = NG
            dve.wait_ge(ff_measured, NG * 2 * KF)
            nc.vector.tensor_reduce(amax_part[:, A_UP:A_GATE + 1], amax_in[:], AX_X, ALU.max).then_inc(part_ready, 1)
            scales(2, slice(A_UP, A_GATE + 1))

            pieces = [slice(n * PIECE, (n + 1) * PIECE) for n in range(NB)]
            for n, at in enumerate(pieces):
                quantize(steps, gate_flat[:, at], gate_flat[:, at], A_GATE).then_inc(gate_ready, 1)
            for n, at in enumerate(pieces):
                steps.then(quantize(steps, up_flat[:, at], up_flat[:, at], A_UP))
            for n, at in enumerate(pieces):
                s = sig[:, n % 2, :]
                dve.wait_ge(sig_ready, n + 1)
                steps.then(nc.vector.tensor_scalar(s, s, 65536.0, MAGIC, ALU.mult, ALU.add))
                steps.settle()
                steps.then(nc.vector.tensor_scalar(s, s, MAGIC, 65535.0, ALU.subtract, ALU.min))
                steps.settle()
                nc.vector.scalar_tensor_tensor(out=gate_flat[:, at], in0=s, scalar=1.0 / 65536.0, in1=gate_flat[:, at], op0=ALU.mult, op1=ALU.mult).then_inc(sig_used, 1)
                dve.wait_ge(sig_used, n + 1)
                steps.then(nc.vector.tensor_reduce(amax_piece[:, 0, n:n + 1], gate_flat[:, at], AX_X, ALU.max, apply_absolute_value=True))
            steps.settle()
            nc.vector.tensor_reduce(amax_part[:, A_SWISH:A_SWISH + 1], amax_piece[:, 0, :], AX_X, ALU.max).then_inc(part_ready, 1)
            scales(3, slice(A_SWISH, A_SWISH + 1))
            for n, at in enumerate(pieces):
                steps.then(quantize(steps, gate_flat[:, at], gate_flat[:, at], A_SWISH))
                steps.settle()
                steps.then(nc.vector.tensor_tensor(gate_flat[:, at], gate_flat[:, at], up_flat[:, at], ALU.mult))
                steps.settle()
                steps.then(nc.vector.tensor_reduce(amax_piece[:, 1, n:n + 1], gate_flat[:, at], AX_X, ALU.max, apply_absolute_value=True))
            steps.settle()
            nc.vector.tensor_reduce(amax_part[:, A_OUT:A_OUT + 1], amax_piece[:, 1, :], AX_X, ALU.max).then_inc(part_ready, 1)
            scales(4, slice(A_OUT, A_OUT + 1))
            base = steps.base + steps.n

            def put_out(loop, i, first=False):
                for u in range(U):
                    n = i * U + u
                    at = slice(n, n + 1) if first else bass.ds(n, 1)
                    src = gate[:, at, :, :].rearrange("p a k t -> p (a k t)")
                    quantize(loop, hidden[:, u, :, :].rearrange("p k t -> p (k t)"), src, A_OUT, tmp=src).then_inc(hidden_ready, 1)
                for u in range(U):
                    n = i * U + u
                    at = slice(n * G, (n + 1) * G) if first else bass.ds(n * G, G)
                    dve.wait_ge(down_ready, n + 1)
                    nc.vector.tensor_tensor(total[:, u, :, :], ps_x[:, u, :].rearrange("p (g d) -> p g d", g=G), x_all[:, at, :], ALU.add)\
                        .then_inc(total_ready, 1)
                    dve.wait_ge(total_ready, n + 1)
                    after[u].take_moments(nc, loop, total[:, u, :, :])
                for u in range(U):
                    if not first:
                        dve.wait_ge(stored[u], i * 16)
                    after[u].apply(nc, dve, total[:, u, :, :], lambda b: res[:, u, b, :], i, res_ready)
                loop.closed()

            put_out(Steps(dve, dve_steps, base, 18), 0, first=True)
            with dve.Fori(1, NG // U) as i:
                put_out(Steps(dve, dve_steps, i * 18 + base, 18), i)


class Consts:
    pass


def build(nc, a, out):
    with ExitStack() as stack:
        m = Mem(nc, stack, "all")
        c = Consts()
        c.ident = m.sb("ident", [128, 128])
        c.ident_b = m.sb("ident_b", [128, 128], BF16)
        c.causal = m.sb("causal", [T, T])
        c.causal_b = m.sb("causal_b", [T, T], BF16)
        c.minus_half = m.sb("minus_half", [T, G])
        x_all = m.sb("x_all", [T, B, D])
        y_all = m.sb("y_all", [T, B, D])
        c.x_all, c.y_all = x_all, y_all
        c.out_dram = out.rearrange("b t d -> t b d")
        landed = m.sem("landed")
        cast = m.sem("cast")
        x_dram = a["x"].rearrange("b t d -> t b d")
        out_dram = out.rearrange("b t d -> t b d")

        with nc.Block() as block:
            @block.sync
            def _(sp):
                sp.dma_start(c.ident[:], a["ident"]).then_inc(landed, 16)
                sp.dma_start(c.causal[:], a["causal"]).then_inc(landed, 16)
                for g in range(NG):
                    sp.dma_start(x_all[:, g * G:(g + 1) * G, :], x_dram[:, g * G:(g + 1) * G, :]).then_inc(landed, 16)

            @block.vector
            def _(dve):
                dve.wait_ge(landed, 16 * (NG + 2))
                nc.vector.tensor_copy(c.ident_b[:], c.ident[:]).then_inc(cast, 1)
                nc.vector.tensor_copy(c.causal_b[:], c.causal[:]).then_inc(cast, 1)
                nc.vector.memset(c.minus_half[:], -0.5).then_inc(cast, 1)
                dve.wait_ge(cast, 3)

        clear_counts(nc)
        for k in STAGES:
            k(nc, a, c)
            clear_counts(nc)

        if not STORED_BY_LAST:
            stored = m.sem("stored")
            with nc.Block() as block:
                @block.sync
                def _(sp):
                    sp.dma_start(out_dram, x_all[:]).then_inc(stored, 16)
                    sp.wait_ge(stored, 16)


def stage_attn0(nc, a, c):
    p = "L0_attn_"
    attention(nc, "at0", c.x_all, c.y_all, c, dict(
        loads=lambda w_qkv, w_o, gain: [(w_qkv[:], a[p + "Wqkv"]), (w_o[:], a[p + "Wo"]),
                                        (gain[:, 0:1], column(a[p + "ln1_g"])), (gain[:, 1:2], column(a[p + "ln1_b"]))],
        n_loads=8, b_qkv=a[p + "bqkv"], b_o=a[p + "bo"], cos=a["rope_cos"], sin=a["rope_sin"], dve_steps=33), True)


def stage_attn1(nc, a, c):
    p = "L0_ffn_"
    attention(nc, "at1", c.x_all, c.y_all, c, dict(
        loads=lambda w_qkv, w_o, gain: [(w_qkv[:, n * D:(n + 1) * D], a[p + w]) for n, w in enumerate(("wq", "wk", "wv"))]
        + [(w_o[:], a[p + "wo"]), (gain[:, 0:1], column(a[p + "norm1_w"]))],
        n_loads=5, dve_steps=33), False)


def stage_gelu(nc, a, c):
    p = "L0_attn_"
    gelu_ffn(nc, "gelu", c.x_all, c.y_all, c, dict(w1=a[p + "W1"], b1=a[p + "b1"], w2=a[p + "W2"], b2=a[p + "b2"],
                                                   g=a[p + "ln2_g"], b=a[p + "ln2_b"]))


def stage_retention(nc, a, c):
    p = "L0_xattn_"
    retention(nc, "ret", c.x_all, a["ctx_1024"].rearrange("b t d -> t b d"), c, dict(
        w_q=a[p + "W_Q"], w_k=a[p + "W_K"], w_v=a[p + "W_V"], w_g=a[p + "g_w"], w_o=a[p + "out_w"],
        b_g=a[p + "g_b"], b_o=a[p + "out_b"], cos=a["xpos_cos"], sin=a["xpos_sin"], decay=a["decay"]))


def stage_moe(nc, a, c):
    p = "L0_ffn_"
    moe(nc, "moe", c.x_all, c.y_all, c, dict(
        e_gate=a[p + "e_gate"], e_up=a[p + "e_up"], e_down=a[p + "e_down"], sh_gate=a[p + "sh_gate"], sh_up=a[p + "sh_up"],
        sh_down=a[p + "sh_down"], router=a[p + "router_w"], gain=a[p + "norm2_w"], number=a["number"], steps=(9, 60)))


def stage_cross(nc, a, c):
    p = "L1_xattn_"
    cross_attention(nc, "xat", c.x_all, a["ctx_1024"].rearrange("b t d -> t b d"), c, dict(
        w_q=a[p + "W_Q"], w_k=a[p + "W_K"], w_v=a[p + "W_V"], w_o=a[p + "W_O"]))


def stage_mamba(nc, a, c):
    mamba(nc, "mam", c.x_all, c, dict(a=a))


def stage_quant(nc, a, c):
    quant_ffn(nc, "qua", c.x_all, c.out_dram, c, {w: a["L1_ffn_" + w] for w in ("w_gate", "w_up", "w_down")})


def dbg_copy(nc, a, c):
    with nc.semaphore("dbg") as s, nc.Block() as block:
        @block.vector
        def _(dve):
            nc.vector.tensor_copy(c.x_all[:], c.y_all[:]).then_inc(s, 1)
            dve.wait_ge(s, 1)


STAGES = [stage_attn0, stage_gelu, stage_retention, stage_attn1, stage_moe, stage_mamba, stage_cross, stage_quant]
STORED_BY_LAST = True


def tables():
    f = np.float32
    t = {"ident": np.eye(128, dtype=f)}
    t["causal"] = np.where(np.arange(T)[:, None] >= np.arange(T)[None, :], f(0), f(HUGE)).astype(f)
    inv_freq = f(1.0) / f(10000.0) ** (np.arange(0, HD, 2, dtype=f) / f(HD))
    freqs = np.arange(T, dtype=f)[:, None] * inv_freq[None, :]
    sin = np.sin(freqs).astype(f)
    t["rope_cos"] = np.tile(np.concatenate([np.cos(freqs)] * 2, -1), (1, 2 * H)).astype(f)
    t["rope_sin"] = np.tile(np.concatenate([-sin, sin], -1), (1, 2 * H)).astype(f)
    base = (np.arange(0, HD, 2, dtype=f) + f(0.4 * HD)) / f(1.4 * HD)
    power = (np.arange(-(T // 2), T - T // 2, dtype=f) / f(512.0))[:, None]
    scale = (base[None, :] ** power).astype(f)
    ang = np.arange(T, dtype=f)[:, None] * (f(1.0) / f(10000.0) ** (np.arange(HD // 2, dtype=f) / f(HD // 2)))[None, :]
    both = []
    for s in (scale, f(1.0) / scale):
        cos_s, sin_s = np.repeat(np.cos(ang) * s, 2, -1), np.repeat(np.sin(ang) * s, 2, -1)
        sin_s[:, ::2] *= -1
        both.append((np.tile(cos_s, (1, H)), np.tile(sin_s, (1, H))))
    t["xpos_cos"] = np.concatenate([both[0][0], both[1][0]], -1).astype(f)
    t["xpos_sin"] = np.concatenate([both[0][1], both[1][1]], -1).astype(f)
    gammas = f(1.0) - np.exp(np.linspace(np.log(1.0 / 32.0), np.log(1.0 / 512.0), H).astype(f)).astype(f)
    dist = np.arange(T)[None, :] - np.arange(T)[:, None]
    t["number"] = np.tile(np.arange(8, dtype=f), (T, 1))
    t["decay"] = np.where(dist[:, None, :] >= 0, gammas[None, :, None] ** np.maximum(dist, 0).astype(f)[:, None, :], 0).astype(f)
    return t


def laid_out(inputs):
    a = {k: np.asarray(v) for k, v in inputs.items()}
    for w in ("W_Q", "W_K", "W_V"):
        a["L0_xattn_" + w] = a["L0_xattn_" + w].transpose(1, 0, 2).reshape(D, D)
    for w in ("L0_xattn_g_w", "L0_xattn_out_w", "L1_xattn_W_Q", "L1_xattn_W_K", "L1_xattn_W_V", "L1_xattn_W_O"):
        a[w] = a[w].T
    for s in "fb":
        for w in ("inW", "xpW", "dtW", "outW"):
            a[f"L1_attn_{w}_{s}"] = a[f"L1_attn_{w}_{s}"].T
        a[f"L1_attn_convW_{s}"] = a[f"L1_attn_convW_{s}"][:, 0, :].T
    return a


def kernel(**inputs):
    import concourse.bacc as bacc
    from concourse.bass_utils import run_bass_kernel_spmd

    nc = bacc.Bacc("TRN2", target_bir_lowering=False, num_devices=1)
    arrays, args = {}, {}
    for name, value in list(laid_out(inputs).items()) + list(tables().items()):
        value = np.ascontiguousarray(value)
        arrays[f"in_{name}"] = value
        args[name] = nc.dram_tensor(f"in_{name}", value.shape, mybir.dt.from_np(value.dtype), kind="ExternalInput").ap()
    out = nc.dram_tensor("out", (B, T, D), F32, kind="ExternalOutput").ap()
    with nc.allow_non_contiguous_dma(reason="a few small vectors lie down the partitions"):
        build(nc, args, out)
    got = run_bass_kernel_spmd(nc, [arrays], core_ids=[0])
    return got.results[0]["out"]
```

```python
from contextlib import ExitStack

import numpy as np

import concourse.bass as bass
from concourse import mybir

ALU = mybir.AluOpType
ACT = mybir.ActivationFunctionType
F32 = mybir.dt.float32
BF16 = mybir.dt.bfloat16
U32 = mybir.dt.uint32
AX_X = mybir.AxisListType.X

B, T, D = 32, 128, 128
G = 4
NG = B // G
GT = G * T
BANK = 512
H, HD = 16, D // 16
QUAD = 32
NJ = T // QUAD
NK = H // NJ
HUGE = -1.0e30
LN_EPS = 1e-5
RMS_EPS = 1e-6


COUNTED = []


def clear_counts(nc):
    nc.clear_and_free_semaphores(COUNTED)
    COUNTED.clear()
    nc.all_engine_barrier()


class Mem:

    def __init__(self, nc, stack, stage):
        self.nc, self.stack, self.stage = nc, stack, stage

    def sb(self, name, shape, dt=F32):
        return self.stack.enter_context(self.nc.sbuf_tensor(f"{self.stage}_{name}", shape, dt))

    def ps(self, name, shape, dt=F32):
        return self.stack.enter_context(self.nc.psum_tensor(f"{self.stage}_{name}", shape, dt))

    def sem(self, name):
        semaphore = self.nc.alloc_semaphore(f"{self.stage}_{name}")
        COUNTED.append(semaphore)
        return semaphore


class Steps:

    def __init__(self, engine, sem, base=0, per_loop=0):
        self.engine, self.sem, self.base, self.n, self.per_loop = engine, sem, base, 0, per_loop

    def then(self, instruction):
        instruction.then_inc(self.sem, 1)
        self.n += 1

    def settle(self):
        self.engine.wait_ge(self.sem, self.base + self.n)

    def settle_apart(self, passed):
        self.settle()
        self.engine.sem_inc(passed, 1)

    def closed(self):
        assert self.n == self.per_loop, f"the loop's body has {self.n} steps"


def row(vector):
    return vector.rearrange("(a n) -> a n", a=1)


def column(vector):
    return vector.rearrange("(n a) -> n a", a=1)


def all_rows(vector, n=128):
    return bass.AP(vector.tensor, vector.offset, [[0, n]] + list(vector.ap))


def bn(ap, *dims):
    return bass.AP(ap.tensor, ap.offset, [ap.ap[0]] + [list(d) for d in dims])


def spread(ap, n):
    return bass.AP(ap.tensor, ap.offset, list(ap.ap) + [[0, n]])


def repeat(ap, n):
    return bass.AP(ap.tensor, ap.offset, [ap.ap[0], [0, n]] + list(ap.ap[1:]))


class Norm:

    def __init__(self, m, name, rms=False):
        self.rms = rms
        self.stats = m.sb(name + "_stats", [T, G, 6])
        self.moments = m.sb(name + "_moments", [T, G, 2])
        self.square = m.sb(name + "_square", [T, G])
        self.var = m.sb(name + "_var", [T, G])
        self.rstd = m.sb(name + "_rstd", [T, G])
        self.var_ready = m.sem(name + "_var_ready")
        self.stats_passed = m.sem(name + "_stats_passed")
        self.rstd_ready = m.sem(name + "_rstd_ready")

    def take_moments(self, nc, steps, x):
        for b in range(G):
            steps.then(nc.vector.bn_stats(self.stats[:, b, :], x[:, b, :]))
        steps.settle_apart(self.stats_passed)
        for b in range(G):
            steps.then(nc.vector.bn_aggr(self.moments[:, b, :], self.stats[:, b, :]))
        steps.settle()
        mean, var = self.moments[:, :, 0], self.moments[:, :, 1]
        if self.rms:
            steps.then(nc.vector.tensor_tensor(self.square[:], mean, mean, ALU.mult))
            steps.settle()
            nc.vector.scalar_tensor_tensor(out=self.var[:], in0=var, scalar=RMS_EPS, in1=self.square[:], op0=ALU.add, op1=ALU.add)\
                .then_inc(self.var_ready, 1)
        else:
            nc.vector.tensor_scalar(self.var[:], var, LN_EPS, None, ALU.add).then_inc(self.var_ready, 1)

    def root(self, nc, pool, c, n):
        pool.wait_ge(self.var_ready, n + 1)
        nc.gpsimd.tensor_tensor(self.rstd[:], self.var[:], c.minus_half[:], ALU.pow).then_inc(self.rstd_ready, 1)

    def apply(self, nc, dve, x, out, n, done):
        dve.wait_ge(self.rstd_ready, n + 1)
        for b in range(G):
            r = self.rstd[:, b:b + 1]
            if self.rms:
                nc.vector.tensor_scalar(out(b), x[:, b, :], r, None, ALU.mult).then_inc(done, 1)
            else:
                nc.vector.tensor_scalar(out(b), x[:, b, :], self.moments[:, b, 0:1], r, ALU.subtract, ALU.mult).then_inc(done, 1)


class Parts:
    SLOTS = 8
    ROWS = 7 * HD
    STEPS = 4
    HALF = 64

    def __init__(self, m, batches=2):
        self.stack = m.sb("parts", [T, batches, 2, H, self.SLOTS * HD], BF16)
        self.passed = m.sem("parts_passed")
        self.first_ready = m.sem("parts_first_ready")
        self.rest_ready = m.sem("parts_rest_ready")
        self.second_ready = m.sem("parts_second_ready")
        self.rest = m.sb("parts_rest", [T, 2, H, HD])
        self.qT = m.sb("qT", [T, 2, H // 2, T], BF16)
        self.kT = m.sb("kT", [T, 2, H // 2, T], BF16)

    def clear(self, nc, done):
        nc.gpsimd.memset(self.stack[:], 0.0).then_inc(done, 1)

    def slots(self, slot, n, first, stride, count):
        return bn(self.stack[:, slot, n, 0, first * HD:first * HD + 1], (self.SLOTS * HD, H), (stride * HD, count), (1, HD))

    def both(self, slot, q, k):
        return bn(self.stack[:, slot, 0, 0, q * HD:q * HD + 1], (H * self.SLOTS * HD + (k - q) * HD, 2), (self.SLOTS * HD, H), (1, HD))

    def put_first(self, nc, slot, qk):
        whole = qk.rearrange("p (n h d) -> p n h d", n=2, d=HD)
        some = lambda n: bn(whole[:, n, 0, 0:1], (HD, H), (0, 3), (1, HD))
        nc.scalar.copy(self.slots(slot, 0, 0, 3, 3), some(0)).then_inc(self.first_ready, 1)
        nc.scalar.copy(self.slots(slot, 1, 0, 1, 3), some(1)).then_inc(self.first_ready, 1)

    def put_rest(self, nc, steps, slot, qk, done):
        whole = qk.rearrange("p (n h d) -> p n h d", n=2, d=HD)
        steps.then(nc.gpsimd.tensor_tensor(self.rest[:], whole, self.both(slot, 0, 0), ALU.subtract))
        steps.settle_apart(self.passed)
        steps.then(nc.gpsimd.tensor_copy(self.slots(slot, 0, 1, 3, 2), self.twice(0)))
        steps.then(nc.gpsimd.tensor_copy(self.slots(slot, 1, 3, 1, 2), self.twice(1)))
        steps.settle()
        self.put_third(nc, steps, slot, done)

    def twice(self, n):
        return bn(self.rest[:, n, 0, 0:1], (HD, H), (0, 2), (1, HD))

    def put_second(self, nc, slot):
        nc.scalar.copy(self.slots(slot, 0, 1, 3, 2), self.twice(0)).then_inc(self.second_ready, 1)
        nc.scalar.copy(self.slots(slot, 1, 3, 1, 2), self.twice(1)).then_inc(self.second_ready, 1)

    def subtract_first(self, nc, slot, qk):
        whole = qk.rearrange("p (n h d) -> p n h d", n=2, d=HD)
        nc.gpsimd.tensor_tensor(self.rest[:], whole, self.both(slot, 0, 0), ALU.subtract).then_inc(self.rest_ready, 1)

    def put_third(self, nc, steps, slot, done):
        steps.then(nc.gpsimd.tensor_tensor(self.rest[:], self.rest[:], self.both(slot, 1, 3), ALU.subtract))
        steps.settle_apart(self.passed)
        nc.gpsimd.tensor_copy(self.both(slot, 2, 6), self.rest[:]).then_inc(done, 1)

    def block(self, slot, n, pair):
        return self.stack[:, slot, n, 2 * pair:2 * pair + 2, :].rearrange("p h c -> p (h c)")


def head_at(j, k):
    return 2 * (NK * (j // 2) + k) + j % 2


def exists(i, b):
    return not (isinstance(i, int) and not 0 <= i * G + b < B)


def all_steps(engine, before, step, after=2):
    for b in range(-before, G):
        step(0, b)
    with engine.Fori(1, NG - 1) as i:
        for b in range(G):
            step(i, b)
    for b in range(G + after):
        step(NG - 1, b)


def attention(nc, stage, x_all, y_all, c, p, rope):
    with ExitStack() as stack:
        m = Mem(nc, stack, stage)
        w_qkv = m.sb("w_qkv", [D, 3 * D])
        w_o = m.sb("w_o", [D, D])
        gain = m.sb("gain", [D, 2])
        before = Norm(m, "before", rms=not rope)
        xn = m.sb("xn", [T, G, D])
        xnT = m.sb("xnT", [D, T])
        qk = m.sb("qk", [T, 2, 2 * D])
        parts = Parts(m)
        v_wide = m.sb("v_wide", [T, G, NJ, NK, 128])
        prob = m.sb("prob", [T, 2, NJ, NK, T])
        probT = m.sb("probT", [T, 2, NJ, NK, T])
        top = m.sb("top", [T, 2, NJ, NK])
        attU = m.sb("attU", [128, NK, T])
        inv = m.sb("inv", [T, 2, H])
        att = m.sb("att", [T, 2, D])
        attT = m.sb("attT", [D, T])
        if rope:
            b_qkv = m.sb("b_qkv", [T, 3 * D])
            b_o = m.sb("b_o", [T, D])
            cos = m.sb("cos", [T, 2 * D])
            sin = m.sb("sin", [T, 2 * D])
            raw = m.sb("raw", [T, 2, 2 * D])
            turned = m.sb("turned", [T, 2, 2 * D])
        ps_s = m.ps("ps_s", [T, NJ, NK, T])
        ps_t = m.ps("ps_t", [T, 2, BANK])
        ps_a = m.ps("ps_a", [T, BANK])
        ps_o = m.ps("ps_o", [T, BANK])

        loaded = m.sem("loaded")
        padded = m.sem("padded")
        xn_ready = m.sem("xn_ready")
        turned_in = m.sem("turned_in")
        turned_copied = m.sem("turned_copied")
        proj_ready = m.sem("proj_ready")
        proj_taken = m.sem("proj_taken")
        qk_ready = m.sem("qk_ready")
        whole_ready = m.sem("whole_ready") if rope else proj_taken
        turn_filled = m.sem("turn_filled")
        turn_taken = m.sem("turn_taken")
        scores_ready = m.sem("scores_ready")
        shifted = m.sem("shifted")
        exp_ready = m.sem("exp_ready")
        pv_ready = m.sem("pv_ready")
        attU_ready = m.sem("attU_ready")
        attU_turned = m.sem("attU_turned")
        zeroed = m.sem("zeroed")
        att_ready = m.sem("att_ready")
        dve_steps = m.sem("dve_steps")
        pool_steps = m.sem("pool_steps")

        block = stack.enter_context(nc.Block())


        def fills_before(i, b):
            if isinstance(i, int):
                n = i * G + b
                return 2 * max(0, min(n + 1, B)) + NJ * min(max(n - 1, 0), B)
            return i * (G * (2 + NJ)) + 2 * (b + 1) + NJ * (b - 1)

        @block.sync
        def _(sp):
            n = 0
            for dst, src in p["loads"](w_qkv, w_o, gain):
                sp.dma_start(dst, src).then_inc(loaded, 16)
                n += 1
            if rope:
                for dst, src in ((b_qkv[:], all_rows(p["b_qkv"])), (b_o[:], all_rows(p["b_o"])),
                                 (cos[:], p["cos"]), (sin[:], p["sin"])):
                    sp.dma_start(dst, src).then_inc(loaded, 16)
                    n += 1
            assert n == p["n_loads"]

        ALL_LOADED = 16 * p["n_loads"]

        @block.tensor
        def _(pe):
            pe.wait_ge(loaded, ALL_LOADED)

            def turn(n, bank, blocks):
                pe.wait_ge(turn_taken, n + 1)
                for k in range(4):
                    last = nc.tensor.matmul(ps_t[:, bank, k * T:(k + 1) * T], blocks(k), c.ident[:], is_transpose=True,
                                            start=(k == 0), stop=(k == 3), skip_group_check=True)
                last.then_inc(turn_filled, 1)

            def scores(i, b):
                pe.wait_ge(turn_taken, fills_before(i, b) + 2)
                if exists(i, b - 1):
                    pe.wait_ge(shifted, (i * G + b) * NJ)
                for two in range(NJ // 2):
                    if rope:
                        for j in (2 * two, 2 * two + 1):
                            nc.tensor.matmul(ps_s[:, j, :, :], c.ident_b[:], repeat(c.causal_b[:], NK), start=True, stop=False, skip_group_check=True)
                    for k in range(NK):
                        for j in (2 * two, 2 * two + 1):
                            r = slice(j % 2 * parts.HALF, j % 2 * parts.HALF + parts.ROWS)
                            last = nc.tensor.matmul(ps_s[:, j, k, :], parts.qT[r, b % 2, NK * two + k, :], parts.kT[r, b % 2, NK * two + k, :],
                                                    start=(not rope and k == 0), stop=(k == NK - 1), skip_group_check=True)
                            if k == NK - 1:
                                last.then_inc(scores_ready, 1)

            def turn_probabilities(i, b, n):
                for j in range(NJ):
                    pe.wait_ge(exp_ready, (i * G + b) * NJ + j + 1)
                    turn(n + j, j % 2, lambda k: prob[:, b % 2, j, k, :])

            def turn_parts(i, b, n):
                pe.wait_ge(qk_ready, i * G + b + 1)
                for at in range(2):
                    pe.wait_ge(turn_taken, n + at + 1)
                    for pair in range(H // 2):
                        last = nc.tensor.matmul(ps_t[:, at, :].bitcast(BF16)[:, pair * T:(pair + 1) * T], parts.block(b % 2, at, pair), c.ident_b[:],
                                                is_transpose=True, start=(pair == 0), stop=(pair == H // 2 - 1), skip_group_check=True)
                    last.then_inc(turn_filled, 1)

            def values(i, b, n):
                if exists(i, b - 1):
                    pe.wait_ge(att_ready, i * G + b)
                pe.wait_ge(turn_taken, n + NJ + 2)
                for k in range(NK):
                    for j in range(NJ):
                        last = nc.tensor.matmul(ps_o[:, k * T:(k + 1) * T], v_wide[:, b % G, j, k, :], probT[:, b % 2, j, k, :],
                                                start=(j == 0 and k == 0), stop=(j == NJ - 1 and k == NK - 1), skip_group_check=True)
                last.then_inc(pv_ready, 1)

            def turn_back(i, b):
                pe.wait_ge(attU_ready, i * G + b + 1)
                for k in range(NK):
                    last = nc.tensor.matmul(ps_o[:, k * T:(k + 1) * T], attU[:, k, :], c.ident[:], is_transpose=True,
                                            start=(k == 0), stop=(k == NK - 1), skip_group_check=True)
                last.then_inc(attU_turned, 1)

            def step(i, b):
                if exists(i, b):
                    scores(i, b)
                if b > -3:
                    pe.wait_ge(turned_copied, i * G + b + 3)
                    if exists(i, b - 3):
                        last = nc.tensor.matmul(ps_a[:, 0:D], attT[:], w_o[:], start=True, stop=True, skip_group_check=True)
                    if exists(i, b + 2):
                        last = nc.tensor.matmul(ps_a[:, D:4 * D], xnT[:], w_qkv[:], start=not exists(i, b - 3), stop=True, skip_group_check=True)
                    last.then_inc(proj_ready, 1)
                if exists(i, b - 2):
                    turn_back(i, b - 2)
                n = fills_before(i, b)
                if exists(i, b - 1):
                    turn_probabilities(i, b - 1, n)
                if exists(i, b + 1):
                    turn_parts(i, b + 1, n + NJ if exists(i, b - 1) else n)
                if exists(i, b - 1):
                    values(i, b - 1, n)
                if b > -3:
                    pe.wait_ge(proj_taken, i * G + b + 3)
                if exists(i, b - 2):
                    pe.wait_ge(att_ready, i * G + b - 1)
                    last = nc.tensor.transpose(ps_a[:, 0:T], att[:, b % 2, :], c.ident[:])
                if exists(i, b + 3):
                    pe.wait_ge(xn_ready, i * G + b + 4)
                    last = nc.tensor.transpose(ps_a[:, T:2 * T], xn[:, (b + 3) % G, :], c.ident[:])
                if exists(i, b - 2) or exists(i, b + 3):
                    last.then_inc(turned_in, 1)

            all_steps(pe, 3, step, 3)

        @block.scalar
        def _(act):
            act.wait_ge(loaded, ALL_LOADED)
            act.sem_inc(turn_taken, 2)

            def copy_turn(n, bank, dst):
                act.wait_ge(turn_filled, n + 1)
                nc.scalar.copy(dst, ps_t[:, bank, :]).then_inc(turn_taken, 1)

            def step(i, b):
                n = fills_before(i, b)
                if exists(i, b - 2):
                    act.wait_ge(pv_ready, i * G + b - 1)
                    nc.scalar.copy(attU[:], ps_o[:].rearrange("p (k t) -> p k t", k=NK)).then_inc(attU_ready, 1)
                for j in range(NJ):
                    if exists(i, b - 1):
                        copy_turn(n + j, j % 2, probT[:, (b - 1) % 2, j, :, :])
                    if j == NJ - 1 and exists(i, b + 1):
                        m = n + NJ if exists(i, b - 1) else n
                        for at, dst in enumerate((parts.qT, parts.kT)):
                            act.wait_ge(turn_filled, m + at + 1)
                            nc.scalar.copy(dst[:, (b + 1) % 2, :, :], ps_t[:, at, :].bitcast(BF16)).then_inc(turn_taken, 1)
                    if exists(i, b) and j > 0:
                        for k in ((j - 1, j) if j == NJ - 1 else (j - 1,)):
                            act.wait_ge(shifted, (i * G + b) * NJ + k + 1)
                            nc.scalar.activation(prob[:, b % 2, k, :, :], prob[:, b % 2, k, :, :], ACT.Exp, scale=HD ** -0.5).then_inc(exp_ready, 1)
                if exists(i, b + 2):
                    act.wait_ge(whole_ready, i * G + b + 3)
                    parts.put_first(nc, b % 2, qk[:, b % 2, :])
                if exists(i, b - 2) or exists(i, b + 3):
                    act.wait_ge(turned_in, i * G + b + 4)
                if exists(i, b - 2):
                    last = nc.scalar.copy(attT[:], ps_a[:, 0:T])
                if exists(i, b + 3):
                    if rope:
                        last = nc.scalar.activation(xnT[:], ps_a[:, T:2 * T], ACT.Identity, bias=gain[:, 1:2], scale=gain[:, 0:1])
                    else:
                        last = nc.scalar.activation(xnT[:], ps_a[:, T:2 * T], ACT.Copy, scale=gain[:, 0:1])
                if exists(i, b - 2) or exists(i, b + 3):
                    last.then_inc(turned_copied, 1)

            all_steps(act, 3, step, 3)

        @block.gpsimd
        def _(pool):
            parts.clear(nc, padded)
            pool.memset(v_wide[:], 0.0).then_inc(zeroed, 1)
            pool.wait_ge(zeroed, 1)
            for j in range(NJ):
                last = pool.memset(v_wide[:, :, j, :, j * QUAD + HD], 1.0)
            last.then_inc(padded, 1)
            pool.wait_ge(loaded, ALL_LOADED)
            before.root(nc, pool, c, 0)

            def step(i, b):
                if exists(i, b + 2):
                    slot = b % 2
                    STEPS = Parts.STEPS + (3 if rope else 0)
                    steps = Steps(pool, pool_steps, (i * G + b + 2) * STEPS)
                if rope and exists(i, b + 2):
                    pool.wait_ge(proj_taken, i * G + b + 3)
                    halves = raw[:, slot, :].rearrange("p (h s d) -> p h s d", s=2, d=HD // 2)
                    t = turned[:, slot, :].rearrange("p (h s d) -> p h s d", s=2, d=HD // 2)
                    s = sin[:].rearrange("p (h s d) -> p h s d", s=2, d=HD // 2)
                    out = qk[:, slot, :]
                    steps.then(nc.gpsimd.tensor_tensor(t[:, :, 0, :], halves[:, :, 1, :], s[:, :, 0, :], ALU.mult))
                    steps.then(nc.gpsimd.tensor_tensor(t[:, :, 1, :], halves[:, :, 0, :], s[:, :, 1, :], ALU.mult))
                    steps.then(nc.gpsimd.tensor_tensor(out, raw[:, slot, :], cos[:], ALU.mult))
                    steps.settle()
                    nc.gpsimd.tensor_tensor(out, out, turned[:, slot, :], ALU.add).then_inc(whole_ready, 1)
                if exists(i, b + 2):
                    pool.wait_ge(parts.first_ready, (i * G + b + 2) * 2 + 2)
                    parts.put_rest(nc, steps, slot, qk[:, slot, :], qk_ready)
                if b == 0 and exists(i, G):
                    before.root(nc, pool, c, i + 1)

            all_steps(pool, 2, step, 0)

        @block.vector
        def _(dve):
            dve.wait_ge(loaded, ALL_LOADED)
            dve.wait_ge(padded, 2)
            heads = lambda t: t.rearrange("p (h d) -> p h d", d=HD)

            def shift(steps, i, b, banks):
                for j in banks:
                    dve.wait_ge(scores_ready, (i * G + b) * NJ + j + 1)
                    src = ps_s[:, j, :, :]
                    steps.then(nc.vector.tensor_reduce(top[:, b % 2, j, :], src, AX_X, ALU.max))
                    steps.settle()
                    nc.vector.tensor_tensor(prob[:, b % 2, j, :, :], src, spread(top[:, b % 2, j, :], T), ALU.subtract)\
                        .then_inc(shifted, 1)

            def divide(steps, i, b):
                dve.wait_ge(attU_turned, i * G + b + 1)
                o = ps_o[:].rearrange("p (h d) -> p h d", d=QUAD)
                steps.then(nc.vector.reciprocal(inv[:, b % 2, :], o[:, :, HD]))
                steps.settle()
                nc.vector.tensor_tensor(heads(att[:, b % 2, :]), o[:, :, 0:HD], spread(inv[:, b % 2, :], HD), ALU.mult).then_inc(att_ready, 1)

            def take_projected(steps, i, b):
                dve.wait_ge(proj_ready, i * G + b + 3)
                come, go = exists(i, b + 2), exists(i, b - 3)
                wide = lambda two: bn(v_wide[:, (b + 2) % G, 2 * two, 0, 2 * two * QUAD:2 * two * QUAD + 1], (NK * 128 + QUAD, 2), (128, NK), (1, HD))
                flat = lambda t, two: bn(t[:, two * D // 2:two * D // 2 + 1], (HD, 2), (2 * HD, NK), (1, HD))
                if come:
                    for two in range(NJ // 2):
                        if rope:
                            steps.then(nc.vector.tensor_tensor(wide(two), flat(ps_a[:, 3 * D:4 * D], two), flat(b_qkv[:, 2 * D:3 * D], two), ALU.add))
                        else:
                            steps.then(nc.vector.tensor_copy(wide(two), flat(ps_a[:, 3 * D:4 * D], two)))
                if go:
                    at = bass.ds(i * G + b - 3, 1)
                    y = y_all[:, at, :]
                    steps.then(nc.vector.tensor_tensor(y, ps_a[:, 0:D].unsqueeze(1), x_all[:, at, :], ALU.add))
                    steps.settle()
                    if rope:
                        steps.then(nc.vector.tensor_tensor(y, y, b_o[:].unsqueeze(1), ALU.add))
                steps.settle()
                if come and rope:
                    nc.vector.tensor_tensor(raw[:, b % 2, :], ps_a[:, D:3 * D], b_qkv[:, 0:2 * D], ALU.add).then_inc(proj_taken, 1)
                elif come:
                    nc.vector.tensor_copy(qk[:, b % 2, :], ps_a[:, D:3 * D]).then_inc(proj_taken, 1)
                else:
                    dve.sem_inc(proj_taken, 1)

            def norm(steps, i, b):
                x = x_all[:, bass.ds(i * G + G, G), :]
                if b == 0:
                    before.take_moments(nc, steps, x)
                elif b == 1:
                    before.apply(nc, dve, x, lambda n: xn[:, n, :], i + 1, xn_ready)

            def step(steps, i, b):
                if exists(i, b):
                    shift(steps, i, b, (0, 1))
                take_projected(steps, i, b)
                if exists(i, b - 2):
                    divide(steps, i, b - 2)
                if exists(i, b):
                    shift(steps, i, b, (2, 3))
                if exists(i, G):
                    norm(steps, i, b)

            steps = Steps(dve, dve_steps)
            norm(steps, -1, 0)
            norm(steps, -1, 1)
            for b in range(-2, G):
                step(steps, 0, b)
            peeled, per_loop = steps.n, p["dve_steps"]
            with dve.Fori(1, NG - 1) as i:
                steps = Steps(dve, dve_steps, i * per_loop + peeled - per_loop, per_loop)
                for b in range(G):
                    step(steps, i, b)
                steps.closed()
            steps = Steps(dve, dve_steps, (NG - 2) * per_loop + peeled)
            for b in range(G + 3):
                step(steps, NG - 1, b)


U = 2


def gelu_ffn(nc, stage, x_all, y_all, c, p):
    F = 4 * D
    KF = F // 128
    with ExitStack() as stack:
        m = Mem(nc, stack, stage)
        w1 = m.sb("w1", [D, F])
        w2 = m.sb("w2", [128, KF, D])
        b1 = m.sb("b1", [128, KF])
        b2 = m.sb("b2", [T, D])
        gain = m.sb("gain", [D, 2])
        before = [Norm(m, f"before{u}") for u in range(U)]
        after = [Norm(m, f"after{u}") for u in range(U)]
        yn = m.sb("yn", [T, U, G, D])
        ynT = m.sb("ynT", [D, U, GT])
        hidden = m.sb("hidden", [128, U, KF, GT])
        skip = m.sb("skip", [T, U, G, D])
        total = m.sb("total", [T, U, G, D])
        ps_a = m.ps("ps_a", [D, U, GT])
        ps_h = m.ps("ps_h", [128, 4, GT])
        ps_y = m.ps("ps_y", [T, U, G, D])

        loaded = m.sem("loaded")
        yn_ready = m.sem("yn_ready")
        yn_turned = m.sem("yn_turned")
        ynT_ready = m.sem("ynT_ready")
        h_ready = m.sem("h_ready")
        gelu_ready = m.sem("gelu_ready")
        out_ready = m.sem("out_ready")
        skip_ready = m.sem("skip_ready")
        total_ready = m.sem("total_ready")
        x_ready = m.sem("x_ready")
        dve_steps = m.sem("dve_steps")
        pool_steps = m.sem("pool_steps")
        block = stack.enter_context(nc.Block())
        ALL_LOADED = 16 * 6

        @block.sync
        def _(sp):
            for dst, src in ((w1[:], p["w1"]), (w2[:], p["w2"].rearrange("(k p) n -> p k n", p=128)),
                             (b1[:], p["b1"].rearrange("(k p) -> p k", p=128)), (b2[:], all_rows(p["b2"])),
                             (gain[:, 0:1], column(p["g"])), (gain[:, 1:2], column(p["b"]))):
                sp.dma_start(dst, src).then_inc(loaded, 16)

        LOOPS = NG // U

        def looped(engine, step):
            with engine.Fori(0, LOOPS - 1) as i:
                step(i, True)
            step(LOOPS - 1, False)

        @block.tensor
        def _(pe):
            pe.wait_ge(loaded, ALL_LOADED)

            def turn(i):
                for u in range(U):
                    for b in range(G):
                        pe.wait_ge(yn_ready, (i * U + u) * G + b + 1)
                        last = nc.tensor.transpose(ps_a[:, u, b * T:(b + 1) * T], yn[:, u, b, :], c.ident[:])
                    last.then_inc(yn_turned, 1)

            def step(i, more):
                for u in range(U):
                    pe.wait_ge(ynT_ready, i * U + u + 1)
                    for k in range(KF):
                        if u > 0:
                            pe.wait_ge(gelu_ready, i * U * KF + (u - 1) * KF + k + 1)
                        nc.tensor.matmul(ps_h[:, k, :], w1[:, k * 128:(k + 1) * 128], ynT[:, u, :], start=True, stop=True).then_inc(h_ready, 1)
                if more:
                    turn(i + 1)
                for u in range(U):
                    for k in range(KF):
                        pe.wait_ge(gelu_ready, (i * U + u) * KF + k + 1)
                        for b in range(G):
                            last = nc.tensor.matmul(ps_y[:, u, b, :], hidden[:, u, k, b * T:(b + 1) * T], w2[:, k, :],
                                                    start=(k == 0 and b == 0), stop=(k == KF - 1 and b == G - 1), skip_group_check=True)
                    last.then_inc(out_ready, 1)
                if more:
                    pe.wait_ge(total_ready, i * U + U)

            turn(0)
            looped(pe, step)

        @block.scalar
        def _(act):
            act.wait_ge(loaded, ALL_LOADED)

            def copy_turned(i):
                for u in range(U):
                    act.wait_ge(yn_turned, i * U + u + 1)
                    nc.scalar.activation(ynT[:, u, :], ps_a[:, u, :], ACT.Identity, bias=gain[:, 1:2], scale=gain[:, 0:1]).then_inc(ynT_ready, 1)

            def step(i, more):
                for u in range(U):
                    for k in range(KF):
                        act.wait_ge(h_ready, (i * U + u) * KF + k + 1)
                        nc.scalar.activation(hidden[:, u, k, :], ps_h[:, k, :], ACT.Gelu, bias=b1[:, k:k + 1]).then_inc(gelu_ready, 1)
                if more:
                    copy_turned(i + 1)

            copy_turned(0)
            looped(act, step)

        @block.gpsimd
        def _(pool):
            pool.wait_ge(loaded, ALL_LOADED)
            for u in range(U):
                before[u].root(nc, pool, c, 0)

            def step(i, more):
                steps = Steps(pool, pool_steps, i * U, U)
                for u in range(U):
                    at = bass.ds((i * U + u) * G, G)
                    steps.then(nc.gpsimd.tensor_tensor(skip[:, u, :, :], x_all[:, at, :], y_all[:, at, :], ALU.add))
                    steps.settle()
                    nc.gpsimd.tensor_tensor(skip[:, u, :, :], skip[:, u, :, :], repeat(b2[:], G), ALU.add).then_inc(skip_ready, 1)
                if more:
                    for u in range(U):
                        before[u].root(nc, pool, c, i + 1)
                for u in range(U):
                    after[u].root(nc, pool, c, i)
                steps.closed()

            looped(pool, step)

        @block.vector
        def _(dve):
            dve.wait_ge(loaded, ALL_LOADED)

            def normed(steps, i, first=False):
                y = [y_all[:, bass.ds((i * U + u) * G, G), :] for u in range(U)]
                for u in range(U):
                    before[u].take_moments(nc, steps, y[u])
                if not first:
                    dve.wait_ge(yn_turned, i * U)
                for u in range(U):
                    before[u].apply(nc, dve, y[u], lambda b: yn[:, u, b, :], i, yn_ready)

            def step(steps, i, more):
                if more:
                    normed(steps, i + 1)
                for u in range(U):
                    dve.wait_ge(out_ready, i * U + u + 1)
                    dve.wait_ge(skip_ready, i * U + u + 1)
                    nc.vector.tensor_tensor(total[:, u, :, :], ps_y[:, u, :, :], skip[:, u, :, :], ALU.add).then_inc(total_ready, 1)
                    dve.wait_ge(total_ready, i * U + u + 1)
                    after[u].take_moments(nc, steps, total[:, u, :, :])
                for u in range(U):
                    after[u].apply(nc, dve, total[:, u, :, :], lambda b: x_all[:, bass.ds((i * U + u) * G + b, 1), :], i, x_ready)
                dve.wait_ge(x_ready, i * U * G + U * G)

            HALF = 2 * U * G
            normed(Steps(dve, dve_steps), 0, first=True)
            with dve.Fori(0, LOOPS - 1) as i:
                steps = Steps(dve, dve_steps, i * (2 * HALF) + HALF, 2 * HALF)
                step(steps, i, True)
                steps.closed()
            step(Steps(dve, dve_steps, (LOOPS - 1) * (2 * HALF) + HALF), LOOPS - 1, False)


def retention(nc, stage, x_all, ctx_dram, c, p):
    with ExitStack() as stack:
        m = Mem(nc, stack, stage)
        w_qg = m.sb("w_qg", [D, 2 * D])
        w_kv = m.sb("w_kv", [D, 2 * D])
        w_o = m.sb("w_o", [D, D])
        b_g = m.sb("b_g", [T, D])
        b_o = m.sb("b_o", [T, D])
        cos = m.sb("cos", [T, 2 * D])
        sin = m.sb("sin", [T, 2 * D])
        decay = m.sb("decay", [T, NJ, NK, T])
        xg = m.sb("xg", [T, G, D])
        ctx = m.sb("ctx", [T, G, D])
        inT = m.sb("inT", [D, 3, T])
        turned = m.sb("turned", [T, 2, 2 * D])
        qk = m.sb("qk", [T, 2, 2 * D])
        parts = Parts(m)
        v_wide = m.sb("v_wide", [T, G, H, D])
        retT = m.sb("retT", [D, T])
        gate_in = m.sb("gate_in", [T, 2, D])
        gate = m.sb("gate", [T, G, D])
        sim = m.sb("sim", [T, 2, NJ, NK, T])
        head_sum = m.sb("head_sum", [T, 2, H])
        head_var = m.sb("head_var", [T, 2, H])
        head_rstd = m.sb("head_rstd", [T, 2, H])
        minus_half = m.sb("minus_half", [T, H])
        centred = m.sb("centred", [T, 2, H, HD])
        square = m.sb("square", [T, 2, H, HD])
        gated = m.sb("gated", [T, 2, D])
        after = Norm(m, "after")
        ps_s = m.ps("ps_s", [T, NJ, NK, T])
        ps_t = m.ps("ps_t", [T, 2, BANK])
        ps_a = m.ps("ps_a", [T, BANK])
        ps_o = m.ps("ps_o", [T, 3, D])

        loaded = m.sem("loaded")
        arrived = [m.sem(f"arrived{b}") for b in range(G)]
        padded = m.sem("padded")
        turned_in = m.sem("turned_in")
        turned_copied = m.sem("turned_copied")
        proj_ready = m.sem("proj_ready")
        proj_taken = m.sem("proj_taken")
        gate_ready = m.sem("gate_ready")
        qk_ready = m.sem("qk_ready")
        whole_ready = m.sem("whole_ready")
        turn_filled = m.sem("turn_filled")
        turn_taken = m.sem("turn_taken")
        scores_ready = m.sem("scores_ready")
        sim_ready = m.sem("sim_ready")
        pv_ready = m.sem("pv_ready")
        retT_ready = m.sem("retT_ready")
        ret_ready = m.sem("ret_ready")
        ret_taken = m.sem("ret_taken")
        centred_ready = m.sem("centred_ready")
        square_ready = m.sem("square_ready")
        head_var_ready = m.sem("head_var_ready")
        head_rstd_ready = m.sem("head_rstd_ready")
        gated_ready = m.sem("gated_ready")
        x_ready = m.sem("x_ready")
        dve_steps = m.sem("dve_steps")
        pool_steps = m.sem("pool_steps")
        block = stack.enter_context(nc.Block())
        LOADS = ((w_qg[:, 0:D], p["w_q"]), (w_qg[:, D:2 * D], p["w_g"]), (w_kv[:, 0:D], p["w_k"]), (w_kv[:, D:2 * D], p["w_v"]),
                 (w_o[:], p["w_o"]), (b_g[:], all_rows(p["b_g"])), (b_o[:], all_rows(p["b_o"])),
                 (cos[:], p["cos"]), (sin[:], p["sin"]), (decay[:], p["decay"]))
        ALL_LOADED = 16 * len(LOADS)


        @block.sync
        def _(sp):
            for dst, src in LOADS[:4]:
                sp.dma_start(dst, src).then_inc(loaded, 16)

            def bring(i, b):
                for dst, src in ((xg, x_all), (ctx, ctx_dram)):
                    sp.dma_start(dst[:, b:b + 1, :], src[:, bass.ds(i * G + b, 1), :]).then_inc(arrived[b], 16)

            for b in range(G):
                bring(0, b)
            for dst, src in LOADS[4:]:
                sp.dma_start(dst, src).then_inc(loaded, 16)

            def bring_next(i, b):
                sp.wait_ge(turned_in, i * G + b - G + 1)
                bring(i, b)

            for b in range(G):
                bring_next(1, b)
            with sp.Fori(2, NG) as i:
                for b in range(G):
                    bring_next(i, b)

        @block.tensor
        def _(pe):
            pe.wait_ge(loaded, ALL_LOADED)

            def scores(i, b):
                pe.wait_ge(turn_taken, (i * G + b) * 2 + 2)
                if exists(i, b - 1):
                    pe.wait_ge(sim_ready, (i * G + b) * NJ)
                for two in range(NJ // 2):
                    for k in range(NK):
                        for j in (2 * two, 2 * two + 1):
                            r = slice(j % 2 * parts.HALF, j % 2 * parts.HALF + parts.ROWS)
                            last = nc.tensor.matmul(ps_s[:, j, k, :], parts.kT[r, b % 2, NK * two + k, :], parts.qT[r, b % 2, NK * two + k, :],
                                                    start=(k == 0), stop=(k == NK - 1), skip_group_check=True)
                            if k == NK - 1:
                                last.then_inc(scores_ready, 1)

            def turn_parts(i, b):
                pe.wait_ge(qk_ready, i * G + b + 1)
                for at in range(2):
                    if exists(i, b - 1):
                        pe.wait_ge(turn_taken, (i * G + b) * 2 + at - 1)
                    for pair in range(H // 2):
                        last = nc.tensor.matmul(ps_t[:, at, :].bitcast(BF16)[:, pair * T:(pair + 1) * T], parts.block(b % 2, at, pair), c.ident_b[:],
                                                is_transpose=True, start=(pair == 0), stop=(pair == H // 2 - 1), skip_group_check=True)
                    last.then_inc(turn_filled, 1)

            def values(i, b):
                for j in range(NJ):
                    pe.wait_ge(sim_ready, (i * G + b) * NJ + j + 1)
                    for k in range(NK):
                        h = head_at(j, k)
                        last = nc.tensor.matmul(ps_o[:, 0, :], v_wide[:, b % G, h, :], sim[:, b % 2, j, k, :],
                                                start=(j == 0 and k == 0), stop=(j == NJ - 1 and k == NK - 1), skip_group_check=True)
                last.then_inc(pv_ready, 1)

            def step(i, b):
                if exists(i, b):
                    scores(i, b)
                if exists(i, b + 2) or exists(i, b - 3):
                    if b > -3:
                        pe.wait_ge(turned_copied, i * G + b + 3)
                if b > -3 and exists(i, b + 2):
                    nc.tensor.matmul(ps_a[:, 0:2 * D], inT[:, 0, :], w_qg[:], start=True, stop=True, skip_group_check=True)
                    nc.tensor.matmul(ps_a[:, 2 * D:4 * D], inT[:, 1, :], w_kv[:], start=False, stop=True, skip_group_check=True).then_inc(proj_ready, 1)
                if exists(i, b + 1):
                    turn_parts(i, b + 1)
                if exists(i, b - 2) or exists(i, b - 3):
                    pe.wait_ge(ret_taken, i * G + b - 1)
                if exists(i, b - 3):
                    last = nc.tensor.matmul(ps_o[:, 1, :], inT[:, 2, :], w_o[:], start=True, stop=True, skip_group_check=True)
                if exists(i, b - 1):
                    values(i, b - 1)
                elif exists(i, b - 3):
                    last.then_inc(ret_ready, 1)
                if b > -3 and exists(i, b + 2):
                    pe.wait_ge(proj_taken, i * G + b + 3)
                if exists(i, b + 3):
                    pe.wait_ge(arrived[(b + 3) % G], (i + (b + 3) // G) * 32 + 32)
                    nc.tensor.transpose(ps_a[:, 0:T], xg[:, (b + 3) % G, :], c.ident[:])
                    last = nc.tensor.transpose(ps_a[:, T:2 * T], ctx[:, (b + 3) % G, :], c.ident[:])
                if exists(i, b - 2):
                    pe.wait_ge(gated_ready, i * G + b - 1)
                    last = nc.tensor.transpose(ps_a[:, 2 * T:3 * T], gated[:, b % 2, :], c.ident[:])
                if exists(i, b - 2) or exists(i, b + 3):
                    last.then_inc(turned_in, 1)
                if exists(i, b - 1):
                    pe.wait_ge(retT_ready, i * G + b)
                    nc.tensor.matmul(ps_o[:, 2, :], retT[:], c.ident[:], is_transpose=True, start=True, stop=True, skip_group_check=True)\
                        .then_inc(ret_ready, 1)

            all_steps(pe, 3, step, 3)

        @block.scalar
        def _(act):
            def step(i, b):
                if exists(i, b + 1):
                    for at, dst in enumerate((parts.qT, parts.kT)):
                        act.wait_ge(turn_filled, (i * G + b + 1) * 2 + at + 1)
                        nc.scalar.copy(dst[:, (b + 1) % 2, :, :], ps_t[:, at, :].bitcast(BF16)).then_inc(turn_taken, 1)
                    act.wait_ge(proj_taken, i * G + b + 2)
                    nc.scalar.activation(gate[:, (b + 1) % G, :], gate_in[:, (b + 1) % 2, :], ACT.Silu).then_inc(gate_ready, 1)
                if exists(i, b + 2):
                    act.wait_ge(whole_ready, i * G + b + 3)
                    parts.put_first(nc, b % 2, qk[:, b % 2, :])
                    act.wait_ge(parts.rest_ready, i * G + b + 3)
                    parts.put_second(nc, b % 2)
                if exists(i, b - 1):
                    act.wait_ge(pv_ready, i * G + b)
                    nc.scalar.copy(retT[:], ps_o[:, 0, :]).then_inc(retT_ready, 1)
                if exists(i, b - 2) or exists(i, b + 3):
                    act.wait_ge(turned_in, i * G + b + 4)
                    a0 = 0 if exists(i, b + 3) else 2
                    a1 = 3 if exists(i, b - 2) else 2
                    nc.scalar.copy(inT[:, a0:a1, :], ps_a[:, a0 * T:a1 * T]).then_inc(turned_copied, 1)
                if exists(i, b - 1):
                    act.wait_ge(centred_ready, i * G + b)
                    slot = (b - 1) % 2
                    nc.scalar.activation(square[:, slot, :, :], centred[:, slot, :, :], ACT.Square).then_inc(square_ready, 1)

            all_steps(act, 3, step, 2)

        @block.gpsimd
        def _(pool):
            parts.clear(nc, padded)
            pool.memset(minus_half[:], -0.5).then_inc(padded, 1)
            pool.memset(v_wide[:], 0.0).then_inc(padded, 1)
            pool.wait_ge(loaded, ALL_LOADED)
            pool.wait_ge(padded, 3)

            def step(i, b):
                if b == 3 and exists(i, -1):
                    after.root(nc, pool, c, i - 1)
                if exists(i, b - 2):
                    pool.wait_ge(head_var_ready, i * G + b - 1)
                    nc.gpsimd.tensor_tensor(head_rstd[:, b % 2, :], head_var[:, b % 2, :], minus_half[:], ALU.pow).then_inc(head_rstd_ready, 1)
                if exists(i, b + 2):
                    slot = b % 2
                    STEPS = 1
                    steps = Steps(pool, pool_steps, (i * G + b + 2) * STEPS)
                    pool.wait_ge(parts.first_ready, (i * G + b + 2) * 2 + 2)
                    parts.subtract_first(nc, slot, qk[:, slot, :])
                    pool.wait_ge(parts.second_ready, (i * G + b + 2) * 2 + 2)
                    parts.put_third(nc, steps, slot, qk_ready)

            all_steps(pool, 2, step, 2)
            after.root(nc, pool, c, NG - 1)

        @block.vector
        def _(dve):
            dve.wait_ge(loaded, ALL_LOADED)
            dve.wait_ge(padded, 3)
            heads = lambda t: t.rearrange("p (h d) -> p h d", d=HD)

            def damp(i, b, banks):
                for j in banks:
                    dve.wait_ge(scores_ready, (i * G + b) * NJ + j + 1)
                    nc.vector.tensor_tensor(sim[:, b % 2, j, :, :], ps_s[:, j, :, :], decay[:, j, :, :], ALU.mult).then_inc(sim_ready, 1)

            def head_moments(steps, i, b):
                dve.wait_ge(square_ready, i * G + b + 1)
                steps.then(nc.vector.tensor_reduce(head_var[:, b % 2, :], square[:, b % 2, :, :], AX_X, ALU.add))
                steps.settle()
                nc.vector.tensor_scalar(head_var[:, b % 2, :], head_var[:, b % 2, :], 1.0 / HD, LN_EPS, ALU.mult, ALU.add).then_inc(head_var_ready, 1)

            def take_projected(steps, i, b):
                dve.wait_ge(proj_ready, i * G + b + 1)
                steps.then(nc.vector.tensor_tensor(gate_in[:, b % 2, :], ps_a[:, D:2 * D], b_g[:], ALU.add))
                steps.then(nc.vector.tensor_copy(bn(v_wide[:, b % G, 0, 0:1], (D + HD, H), (1, HD)), heads(ps_a[:, 3 * D:4 * D])))
                slot = b % 2
                out = qk[:, slot, :].rearrange("p (n d) -> p n d", n=2)
                for s in range(2):
                    one = lambda t: bn(t[:, slot, s:s + 1], (D, 2), (2, D // 2))
                    steps.then(nc.vector.tensor_tensor(one(turned), bn(ps_a[:, 1 - s:2 - s], (2 * D, 2), (2, D // 2)), bn(sin[:, s:s + 1], (D, 2), (2, D // 2)), ALU.mult))
                steps.settle()
                nc.vector.tensor_tensor(out, bn(ps_a[:, 0:1], (2 * D, 2), (1, D)), cos[:].rearrange("p (n d) -> p n d", n=2), ALU.mult).then_inc(proj_taken, 1)
                dve.wait_ge(proj_taken, i * G + b + 1)
                nc.vector.tensor_tensor(qk[:, slot, :], qk[:, slot, :], turned[:, slot, :], ALU.add).then_inc(whole_ready, 1)

            def gate_heads(steps, i, b):
                slot = b % 2
                dve.wait_ge(gate_ready, i * G + b + 1)
                steps.then(nc.vector.tensor_tensor(centred[:, slot, :, :], centred[:, slot, :, :], heads(gate[:, b % G, :]), ALU.mult))
                steps.settle()
                dve.wait_ge(head_rstd_ready, i * G + b + 1)
                nc.vector.tensor_tensor(heads(gated[:, slot, :]), centred[:, slot, :, :], spread(head_rstd[:, slot, :], HD), ALU.mult).then_inc(gated_ready, 1)

            def take_values(steps, i, b):
                dve.wait_ge(ret_ready, i * G + b)
                come, go = exists(i, b - 1), exists(i, b - 3)
                slot = (b - 1) % 2
                if come:
                    steps.then(nc.vector.tensor_reduce(head_sum[:, slot, :], heads(ps_o[:, 2, :]), AX_X, ALU.add))
                    steps.settle()
                    nc.vector.scalar_tensor_tensor(out=centred[:, slot, :, :], in0=spread(head_sum[:, slot, :], HD), scalar=-1.0 / HD,
                                                   in1=heads(ps_o[:, 2, :]), op0=ALU.mult, op1=ALU.add).then_inc(centred_ready, 1)
                    dve.wait_ge(centred_ready, i * G + b)
                if go:
                    x = x_all[:, bass.ds(i * G + b - 3, 1), :]
                    nc.vector.tensor_tensor(x, ps_o[:, 1:2, :], x, ALU.add).then_inc(ret_taken, 1)
                    dve.wait_ge(ret_taken, i * G + b)
                    steps.then(nc.vector.tensor_tensor(x, x, b_o[:].unsqueeze(1), ALU.add))
                else:
                    dve.sem_inc(ret_taken, 1)

            def norm(steps, g, first):
                x = x_all[:, bass.ds(g * G, G), :]
                if first:
                    steps.settle()
                    after.take_moments(nc, steps, x)
                else:
                    after.apply(nc, dve, x, lambda n: x_all[:, bass.ds(g * G + n, 1), :], g, x_ready)

            def step(steps, i, b):
                if exists(i, b - 2):
                    head_moments(steps, i, b - 2)
                if exists(i, b):
                    damp(i, b, (0, 1))
                if exists(i, b + 2):
                    take_projected(steps, i, b + 2)
                if exists(i, b):
                    damp(i, b, (2, 3))
                if exists(i, b - 2):
                    gate_heads(steps, i, b - 2)
                if exists(i, b - 1) or exists(i, b - 3):
                    take_values(steps, i, b)
                if b == 2 and exists(i, -1):
                    norm(steps, i - 1, True)
                if b == 3 and exists(i, -1):
                    norm(steps, i - 1, False)

            steps = Steps(dve, dve_steps)
            for b in range(-2, G):
                step(steps, 0, b)
            peeled, per_loop = steps.n, p["dve_steps"]
            with dve.Fori(1, NG - 1) as i:
                steps = Steps(dve, dve_steps, i * per_loop + peeled - per_loop, per_loop)
                for b in range(G):
                    step(steps, i, b)
                steps.closed()
            steps = Steps(dve, dve_steps, (NG - 2) * per_loop + peeled)
            for b in range(G + 3):
                step(steps, NG - 1, b)
            norm(steps, NG - 1, True)
            norm(steps, NG - 1, False)
            dve.wait_ge(x_ready, B)


def moe(nc, stage, x_all, y_all, c, p):
    E, F = 8, 256
    KF = F // 128
    ORDER = [E] + list(range(E))
    with ExitStack() as stack:
        m = Mem(nc, stack, stage)
        w_gate = m.sb("w_gate", [D, E + 1, F])
        w_up = m.sb("w_up", [D, E + 1, F])
        w_down = m.sb("w_down", [128, E + 1, KF, D])
        w_router = m.sb("w_router", [D, E])
        gain = m.sb("gain", [D, 1])
        number = m.sb("number", [T, E])
        before = Norm(m, "before", rms=True)
        after = Norm(m, "after")
        yn = m.sb("yn", [T, G, D])
        ynT = m.sb("ynT", [D, GT])
        silu = m.sb("silu", [128, KF, GT])
        hidden = m.sb("hidden", [128, 2, KF, GT])
        acc = m.sb("acc", [T, G, D])
        skip = m.sb("skip", [T, G, D])
        logit_top = m.sb("logit_top", [T, G])
        shifted = m.sb("shifted", [T, G, E])
        prob = m.sb("prob", [T, G, E])
        prob_sum = m.sb("prob_sum", [T, G])
        prob_inv = m.sb("prob_inv", [T, G])
        best = m.sb("best", [T, G, 8])
        best_at = m.sb("best_at", [T, G, 8], U32)
        at = m.sb("at", [T, G, 2])
        gap = m.sb("gap", [T, G])
        weight = m.sb("weight", [T, G, 2])
        weight_sum = m.sb("weight_sum", [T, G])
        chosen = m.sb("chosen", [T, G, 2, E])
        combine = m.sb("combine", [T, G, E])
        ps_g = m.ps("ps_g", [128, KF, GT])
        ps_u = m.ps("ps_u", [128, KF, GT])
        ps_d = m.ps("ps_d", [T, 2, G, D])
        ps_a = m.ps("ps_a", [D, GT])
        ps_r = m.ps("ps_r", [T, BANK])

        loaded = m.sem("loaded")
        yn_ready = m.sem("yn_ready")
        yn_turned = m.sem("yn_turned")
        ynT_ready = m.sem("ynT_ready")
        gate_ready = m.sem("gate_ready")
        up_ready = m.sem("up_ready")
        silu_ready = m.sem("silu_ready")
        hidden_ready = m.sem("hidden_ready")
        down_ready = m.sem("down_ready")
        down_taken = m.sem("down_taken")
        logits_ready = m.sem("logits_ready")
        shifted_ready = m.sem("shifted_ready")
        exp_ready = m.sem("exp_ready")
        gap_ready = m.sem("gap_ready")
        weight_ready = m.sem("weight_ready")
        skip_ready = m.sem("skip_ready")
        x_ready = m.sem("x_ready")
        dve_steps = m.sem("dve_steps")
        passed = m.sem("passed")
        block = stack.enter_context(nc.Block())
        LOADS = ((w_gate[:, 0:E, :], p["e_gate"].rearrange("e d f -> d e f")), (w_gate[:, E, :], p["sh_gate"]),
                 (w_up[:, 0:E, :], p["e_up"].rearrange("e d f -> d e f")), (w_up[:, E, :], p["sh_up"]),
                 (w_down[:, 0:E, :, :], p["e_down"].rearrange("e (k q) d -> q e k d", q=128)),
                 (w_down[:, E, :, :], p["sh_down"].rearrange("(k q) d -> q k d", q=128)),
                 (w_router[:], p["router"]), (gain[:], column(p["gain"])), (number[:], p["number"]))
        ALL_LOADED = 16 * len(LOADS)
        NE = len(ORDER)

        @block.sync
        def _(sp):
            for dst, src in LOADS:
                sp.dma_start(dst, src).then_inc(loaded, 16)

        @block.tensor
        def _(pe):
            pe.wait_ge(loaded, ALL_LOADED)

            def turn(n):
                for b in range(G):
                    pe.wait_ge(yn_ready, n * G + b + 1)
                    last = nc.tensor.transpose(ps_a[:, b * T:(b + 1) * T], yn[:, b, :], c.ident[:])
                last.then_inc(yn_turned, 1)

            def group(i, more, first=False):
                def up(o):
                    e = ORDER[o]
                    for k in range(KF):
                        if not (first and o == 0):
                            pe.wait_ge(silu_ready, (i * NE + o - 1) * KF + k + 1)
                        nc.tensor.matmul(ps_g[:, k, :], w_gate[:, e, k * 128:(k + 1) * 128], ynT[:], start=True, stop=True).then_inc(gate_ready, 1)
                        if not (first and o == 0):
                            pe.wait_ge(hidden_ready, (i * NE + o - 1) * KF + k + 1)
                        last = nc.tensor.matmul(ps_u[:, k, :], w_up[:, e, k * 128:(k + 1) * 128], ynT[:], start=True, stop=True)
                        last.then_inc(up_ready, 1)

                def down(o):
                    e = ORDER[o]
                    if not (first and o < 2):
                        pe.wait_ge(down_taken, i * NE + max(o - 1, 0))
                    for k in range(KF):
                        pe.wait_ge(hidden_ready, (i * NE + o) * KF + k + 1)
                        for b in range(G):
                            last = nc.tensor.matmul(ps_d[:, o % 2, b, :], hidden[:, o % 2, k, b * T:(b + 1) * T], w_down[:, e, k, :],
                                                    start=(k == 0 and b == 0), stop=(k == KF - 1 and b == G - 1), skip_group_check=True)
                    last.then_inc(down_ready, 1)

                pe.wait_ge(ynT_ready, i + 1)
                for o in range(NE):
                    up(o)
                    if o == 0:
                        for b in range(G):
                            last = nc.tensor.matmul(ps_r[:, b * E:(b + 1) * E], ynT[:, b * T:(b + 1) * T], w_router[:],
                                                    start=(b == 0), stop=(b == G - 1), skip_group_check=True)
                        last.then_inc(logits_ready, 1)
                    if o > 0:
                        down(o - 1)
                    if o == 5 and more:
                        turn(i + 1)
                down(NE - 1)

            turn(0)
            group(0, True, first=True)
            with pe.Fori(1, NG - 1) as i:
                group(i, True)
            group(NG - 1, False)

        @block.scalar
        def _(act):
            act.wait_ge(loaded, ALL_LOADED)

            def copy_turned(n, after_group):
                act.wait_ge(yn_turned, n + 1)
                if after_group is not None:
                    act.wait_ge(up_ready, (after_group + 1) * (NE * KF))
                nc.scalar.activation(ynT[:], ps_a[:], ACT.Copy, scale=gain[:, 0:1]).then_inc(ynT_ready, 1)

            def group(i, more, first=False):
                for o in range(NE):
                    for k in range(KF):
                        act.wait_ge(gate_ready, (i * NE + o) * KF + k + 1)
                        if not (first and o == 0):
                            act.wait_ge(hidden_ready, (i * NE + o - 1) * KF + k + 1)
                        nc.scalar.activation(silu[:, k, :], ps_g[:, k, :], ACT.Silu).then_inc(silu_ready, 1)
                    if o == 1:
                        act.wait_ge(shifted_ready, i + 1)
                        nc.scalar.activation(prob[:], shifted[:], ACT.Exp).then_inc(exp_ready, 1)
                        act.wait_ge(gap_ready, i + 1)
                        nc.scalar.activation(weight[:, :, 1], gap[:], ACT.Exp).then_inc(weight_ready, 1)
                if more:
                    copy_turned(i + 1, i)

            copy_turned(0, None)
            group(0, True, first=True)
            with act.Fori(1, NG - 1) as i:
                group(i, True)
            group(NG - 1, False)

        @block.gpsimd
        def _(pool):
            pool.wait_ge(loaded, ALL_LOADED)

            def group(i, more):
                at_i = bass.ds(i * G, G)
                nc.gpsimd.tensor_tensor(skip[:], x_all[:, at_i, :], y_all[:, at_i, :], ALU.add).then_inc(skip_ready, 1)
                if more:
                    before.root(nc, pool, c, i + 1)
                after.root(nc, pool, c, i)

            before.root(nc, pool, c, 0)
            with pool.Fori(0, NG - 1) as i:
                group(i, True)
            group(NG - 1, False)

        @block.vector
        def _(dve):
            dve.wait_ge(loaded, ALL_LOADED)

            def normed(steps, n):
                y = y_all[:, bass.ds(n * G, G), :]
                before.take_moments(nc, steps, y)
                before.apply(nc, dve, y, lambda b: yn[:, b, :], n, yn_ready)

            def route(steps, i):
                dve.wait_ge(logits_ready, i + 1)
                logits = ps_r[:, 0:G * E].rearrange("p (g e) -> p g e", e=E)
                steps.then(nc.vector.tensor_reduce(logit_top[:], logits, AX_X, ALU.max))
                steps.settle()
                nc.vector.tensor_tensor(shifted[:], logits, spread(logit_top[:], E), ALU.subtract).then_inc(shifted_ready, 1)
                dve.wait_ge(exp_ready, i + 1)
                steps.then(nc.vector.tensor_reduce(prob_sum[:], prob[:], AX_X, ALU.add))
                steps.settle()
                steps.then(nc.vector.reciprocal(prob_inv[:], prob_sum[:]))
                steps.settle()
                steps.then(nc.vector.tensor_tensor(prob[:], prob[:], spread(prob_inv[:], E), ALU.mult))
                steps.settle_apart(passed)
                for b in range(G):
                    steps.then(nc.vector.max(best[:, b, :], prob[:, b, :]))
                steps.settle_apart(passed)
                for b in range(G):
                    steps.then(nc.vector.max_index(best_at[:, b, :], best[:, b, :], prob[:, b, :]))
                nc.vector.tensor_tensor(gap[:], best[:, :, 1], best[:, :, 0], ALU.subtract).then_inc(gap_ready, 1)
                steps.settle()
                steps.then(nc.vector.tensor_copy(at[:], best_at[:, :, 0:2]))
                dve.wait_ge(weight_ready, i + 1)
                steps.then(nc.vector.tensor_scalar(weight_sum[:], weight[:, :, 1], 1.0, None, ALU.add))
                steps.settle()
                steps.then(nc.vector.reciprocal(weight[:, :, 0], weight_sum[:]))
                number_all = bn(number[:, 0:1], (0, G * 2), (1, E))
                steps.then(nc.vector.tensor_tensor(chosen[:].rearrange("p g n e -> p (g n) e"), number_all,
                                                   spread(at[:].rearrange("p g n -> p (g n)"), E), ALU.is_equal))
                steps.settle()
                steps.then(nc.vector.tensor_tensor(weight[:, :, 1], weight[:, :, 1], weight[:, :, 0], ALU.mult))
                steps.settle()
                steps.then(nc.vector.tensor_tensor(chosen[:].rearrange("p g n e -> p (g n) e"), chosen[:].rearrange("p g n e -> p (g n) e"),
                                                   spread(weight[:].rearrange("p g n -> p (g n)"), E), ALU.mult))
                steps.settle()
                steps.then(nc.vector.tensor_tensor(combine[:], chosen[:, :, 0, :], chosen[:, :, 1, :], ALU.add))
                steps.settle()

            def group(i, more, steps, first=False):
                def multiply(o):
                    for k in range(KF):
                        dve.wait_ge(silu_ready, (i * NE + o) * KF + k + 1)
                        dve.wait_ge(up_ready, (i * NE + o) * KF + k + 1)
                        nc.vector.tensor_tensor(hidden[:, o % 2, k, :], silu[:, k, :], ps_u[:, k, :], ALU.mult).then_inc(hidden_ready, 1)

                def add(o):
                    dve.wait_ge(down_ready, i * NE + o + 1)
                    if o == 0:
                        dve.wait_ge(skip_ready, i + 1)
                        nc.vector.tensor_tensor(acc[:], ps_d[:, o % 2, :, :], skip[:], ALU.add).then_inc(down_taken, 1)
                        return
                    dve.wait_ge(down_taken, i * NE + o)
                    for b in range(G):
                        e = ORDER[o]
                        ins = nc.vector.scalar_tensor_tensor(out=acc[:, b, :], in0=ps_d[:, o % 2, b, :], scalar=combine[:, b, e:e + 1],
                                                             in1=acc[:, b, :], op0=ALU.mult, op1=ALU.add)
                        if b < G - 1:
                            steps.then(ins)
                    ins.then_inc(down_taken, 1)
                    steps.settle()

                for o in range(NE):
                    multiply(o)
                    if o == 0:
                        route(steps, i)
                    if o > 0:
                        add(o - 1)
                    if o == 3 and more:
                        normed(steps, i + 1)
                add(NE - 1)
                dve.wait_ge(down_taken, (i + 1) * NE)
                after.take_moments(nc, steps, acc[:])
                after.apply(nc, dve, acc[:], lambda b: x_all[:, bass.ds(i * G + b, 1), :], i, x_ready)
                dve.wait_ge(x_ready, i * G + G)

            HEAD, per_loop = p["steps"]
            steps = Steps(dve, dve_steps)
            normed(steps, 0)
            assert steps.n == HEAD, steps.n
            group(0, True, Steps(dve, dve_steps, HEAD, per_loop), first=True)
            with dve.Fori(1, NG - 1) as i:
                steps = Steps(dve, dve_steps, i * per_loop + HEAD, per_loop)
                group(i, True, steps)
                steps.closed()
            group(NG - 1, False, Steps(dve, dve_steps, (NG - 1) * per_loop + HEAD, per_loop))


LOG1P = (0.9999999698793575, -0.4999949313792134, 0.333190967542795, -0.2484298178988968, 0.19106005102618012,
         -0.13663242268700254, 0.07822591031320165, -0.029505213253769987, 0.005232687895002128)


class Fills:

    def __init__(self, base):
        self.base, self.n = base, 0

    def next(self):
        self.n += 1
        return self.base + self.n - 1, (self.n - 1) % 2


def mamba(nc, stage, x_all, c, p):
    DT, N, R, W = 2, 16, D // 16, 4
    PAD = W - 1
    TP = T + PAD
    C2 = 2
    CH = N // C2
    S = CH * DT
    SLOTS = 4
    AHEAD = 2
    ROWS = 3 * 2 * N
    with ExitStack() as stack:
        m = Mem(nc, stack, stage)
        w_in = m.sb("w_in", [D, 2, 2 * DT * 128])
        w_tap = m.sb("w_tap", [D, 2, W, DT * 128])
        b_conv = m.sb("b_conv", [128, 2, DT])
        w_bc = m.sb("w_bc", [128, 2, DT, ROWS + R])
        w_dt = m.sb("w_dt", [128, 2, DT * 128])
        b_dt = m.sb("b_dt", [128, 2, DT])
        a_log = m.sb("a_log", [128, 2, DT, N])
        a_neg = m.sb("a_neg", [128, 2, DT, N])
        d_skip = m.sb("d_skip", [128, 2, DT])
        w_out = m.sb("w_out", [128, 2, DT, D])
        pick = m.sb("pick", [ROWS, 2 * N, 128], BF16)
        xg = m.sb("xg", [T, G, D])
        xT = m.sb("xT", [D, 2, G, TP])
        uz = m.sb("uz", [128, 2, 2 * DT, GT])
        u, sz = uz[:, :, 0:DT, :], uz[:, :, DT:2 * DT, :]
        xz = m.sb("xz", [128, 2 * DT, GT])
        bc = m.sb("bc", [128, 2, GT])
        rest = m.sb("rest", [ROWS, GT])
        mid = m.sb("mid", [ROWS, GT], BF16)
        parts = m.sb("parts", [ROWS, 2, GT], BF16)
        pre = m.sb("pre", [128, DT, GT])
        soft = m.sb("soft", [128, DT, GT])
        poly = m.sb("poly", [128, DT, GT])
        delta = m.sb("delta", [128, 2, DT, GT])
        du = m.sb("du", [128, 2, DT, GT])
        decay = m.sb("decay", [128, SLOTS, C2, G, T])
        h = m.sb("h", [128, SLOTS, C2, GT])
        c_all = m.sb("c_all", [128, SLOTS, C2, GT])
        y = m.sb("y", [128, DT, GT])
        g = m.sb("g", [128, 2, DT, G, T])
        half = m.sb("half", [T, G, D])
        total = m.sb("total", [T, G, D])
        after = Norm(m, "after")
        ps_b = m.ps("ps_b", [128, 2, C2, GT])
        ps_y = m.ps("ps_y", [128, DT, GT])
        ps_t = m.ps("ps_t", [128, 2, BANK])

        loaded = m.sem("loaded")
        prepared = m.sem("prepared")
        a_ready = m.sem("a_ready")
        group_in = m.sem("group_in")
        filled = m.sem("filled")
        taken = m.sem("taken")
        parts_ready = m.sem("parts_ready")
        pre_exp = m.sem("pre_exp")
        act_steps = m.sem("act_steps")
        soft_ready = m.sem("soft_ready")
        silu_ready = m.sem("silu_ready")
        delta_ready = m.sem("delta_ready")
        du_ready = m.sem("du_ready")
        b_ready = m.sem("b_ready")
        decay_ready = m.sem("decay_ready")
        h_ready = m.sem("h_ready")
        hc_ready = m.sem("hc_ready")
        y_done = m.sem("y_done")
        y_read = m.sem("y_read")
        g_ready = m.sem("g_ready")
        total_ready = m.sem("total_ready")
        x_ready = m.sem("x_ready")
        dve_steps = m.sem("dve_steps")
        block = stack.enter_context(nc.Block())
        LOADS = []
        for d, s in enumerate(("f", "b")):
            q = lambda name: p["a"][f"L1_attn_{name}_{s}"]
            LOADS += [(w_in[:, d, :], q("inW")), (b_conv[:, d, :], q("convB").rearrange("(t q) -> q t", q=128)),
                      (w_dt[ROWS:ROWS + R, d, :], q("dtW")), (b_dt[:, d, :], q("dtB").rearrange("(t q) -> q t", q=128)),
                      (a_log[:, d, :, :], q("Alog").rearrange("(t q) n -> q t n", q=128)),
                      (d_skip[:, d, :], q("Dp").rearrange("(t q) -> q t", q=128)),
                      (w_out[:, d, :, :], q("outW").rearrange("(t q) n -> q t n", q=128)),
                      (w_bc[:, d, :, ROWS:ROWS + R], q("xpW").rearrange("(t q) n -> q t n", q=128)[:, :, 0:R])]
            LOADS.append((w_tap[:, d, :, :], all_rows(q("convW"))))
            LOADS += [(w_bc[:, d, :, k * 2 * N:(k + 1) * 2 * N], q("xpW").rearrange("(t q) n -> q t n", q=128)[:, :, R:R + 2 * N]) for k in range(3)]
        ALL_LOADED = 16 * len(LOADS)
        PRO = 12 + C2
        PER = 2 * (7 + N) + 2
        ALL_TAKEN = 2

        AT_X, AT_SILU, AT_BC, AT_DELTA, AT_LOG, AT_SPLIT, AT_CONV, AT_Z = 1, 3, 5, (6, 7), (9, 10, 11), 12, (9, 10), (11, 12)
        AT_GATE, AT_OUT, AT_TOTAL, AT_ROOT, AT_FINISH = 1, 3, 6, 7, 8
        LAG = 2

        def fillings(d, s, more):
            head = d == 0 or more
            n = C2 * (s % DT == 0 and (s + DT < S or head)) + (s == AT_OUT and d == 0)
            return n + head * ((s == AT_BC) + (s in AT_DELTA)) + more * ((s == AT_X and d == 0) + (s in AT_CONV) + (s in AT_Z))

        def fillings_before(d, s, more=True):
            return sum(fillings(0, r, more) for r in range(S if d else s)) + sum(fillings(1, r, more) for r in range(s if d else 0))

        def taken_by(i, n):
            return i * PER + (PRO + ALL_TAKEN + n)

        assert PER == fillings_before(1, S)
        TURNED = PRO + fillings_before(0, AT_X + 1)

        @block.sync
        def _(sp):
            for dst, src in LOADS:
                sp.dma_start(dst, src).then_inc(loaded, 16)
            sp.dma_start(xg[:], x_all[:, 0:G, :]).then_inc(group_in, 16)
            sp.wait_ge(filled, 1)
            sp.dma_start(xg[:], x_all[:, G:2 * G, :]).then_inc(group_in, 16)
            with sp.Fori(2, NG) as i:
                sp.wait_ge(filled, i * PER + TURNED - 2 * PER)
                sp.dma_start(xg[:], x_all[:, bass.ds(i * G, G), :]).then_inc(group_in, 16)

        @block.tensor
        def _(pe):
            pe.wait_ge(loaded, ALL_LOADED)
            pe.wait_ge(prepared, 4 + ROWS // (2 * N))

            def fill(f, emit):
                seq, bank = f.next()
                pe.wait_ge(taken, seq + 1)
                emit(ps_t[:, bank, :]).then_inc(filled, 1)
                return seq

            def turn_x(f, n):
                pe.wait_ge(group_in, n * 16 + 16)

                def emit(dst):
                    for b in range(G):
                        last = nc.tensor.transpose(dst[:, b * T:(b + 1) * T], xg[:, b, :], c.ident[:])
                    return last
                fill(f, emit)

            def conv(f, d, t):
                pe.wait_ge(taken, f.base + f.n + 1)

                def emit(dst):
                    for k in range(W):
                        last = nc.tensor.matmul(dst, w_tap[:, d, k, t * 128:(t + 1) * 128], xT[:, d, :, k:k + T], start=(k == 0), stop=(k == W - 1))
                    return last
                fill(f, emit)

            def gate(f, d, t):
                at = (DT + t) * 128
                fill(f, lambda dst: nc.tensor.matmul(dst, w_in[:, d, at:at + 128], xT[:, d, :, PAD:TP], start=True, stop=True))

            def bc_dt(f, d):
                def emit(dst):
                    for t in range(DT):
                        last = nc.tensor.matmul(dst[0:ROWS + R, :], w_bc[:, d, t, :], u[:, d, t, :], start=(t == 0), stop=(t == DT - 1))
                    return last
                fill(f, emit)

            def delta_in(f, d, t):
                fill(f, lambda dst: nc.tensor.matmul(dst, w_dt[ROWS:ROWS + R, d, t * 128:(t + 1) * 128], bc[ROWS:ROWS + R, d, :], start=True, stop=True))

            def c_rows(f, d, chunk):
                for n in range(C2):
                    fill(f, lambda dst: nc.tensor.matmul(dst, pick[:, N + chunk * C2 + n, :], parts[:, d, :], start=True, stop=True))

            def b_rows(q, d, s, slot, spare=False):
                if not spare:
                    pe.wait_ge(h_ready, q - 1)
                for n in range(C2):
                    last = nc.tensor.matmul(ps_b[:, slot, n, :], pick[:, (s // DT) * C2 + n, :], parts[:, d, :], start=True, stop=True)
                last.then_inc(b_ready, 1)

            def sum_states(q, d, s):
                pe.wait_ge(hc_ready, q + 1)
                for n in range(C2):
                    last = nc.tensor.matmul(ps_y[:, s % DT, :], c.ident[:], h[:, s % SLOTS, n, :], start=(s < DT and n == 0),
                                            stop=(s >= S - DT and n == C2 - 1))
                last.then_inc(y_done, 1)

            def output(f, n):
                pe.wait_ge(g_ready, n * 2 * DT + 2 * DT)

                def emit(dst):
                    for b in range(G):
                        for o in range(2 * DT):
                            d, t = o // DT, o % DT
                            last = nc.tensor.matmul(dst[:, b * D:(b + 1) * D], g[:, d, t, b, :], w_out[:, d, t, :],
                                                    start=(b == 0 and o == 0), stop=(b == G - 1 and o == 2 * DT - 1), skip_group_check=True)
                    return last
                fill(f, emit)

            def copied(f):
                pe.wait_ge(taken, f.base + f.n + ALL_TAKEN)

            def group(i, more, first=False):
                f = Fills(i * PER + PRO)
                for d in range(2):
                    head = d == 0 or more
                    nd = 1 - d
                    for s in range(S):
                        q = i * (2 * S) + d * S + s
                        if s + 1 < S or head:
                            if s + 1 == S:
                                pe.wait_ge(parts_ready, i * 2 + d + 2)
                            b_rows(q + 1, d if s + 1 < S else nd, (s + 1) % S, (s + 1) % 2, spare=first and d == 0 and s == 0)
                        if s % DT == 0 and (s + DT < S or head):
                            if s + DT == S:
                                pe.wait_ge(parts_ready, i * 2 + d + 2)
                            c_rows(f, d if s + DT < S else nd, (s // DT + 1) % CH)
                        if s == AT_X and d == 0 and more:
                            turn_x(f, i + 1)
                        if head:
                            if s == AT_BC:
                                pe.wait_ge(silu_ready, i * 2 + d + 2)
                                bc_dt(f, nd)
                            for t in range(DT):
                                if s == AT_DELTA[t]:
                                    if t == 0:
                                        copied(f)
                                    delta_in(f, nd, t)
                        if more:
                            for t in range(DT):
                                if s == AT_CONV[t]:
                                    if t == 0 and d == 0:
                                        pe.wait_ge(taken, taken_by(i, fillings_before(0, AT_X + 1)))
                                    conv(f, d, t)
                                if s == AT_Z[t]:
                                    gate(f, d, t)
                        if s == AT_OUT and d == 0:
                            if first:
                                fill(f, lambda dst: nc.tensor.matmul(dst, c.ident[:], repeat(c.ident[:], G), start=True, stop=True))
                            else:
                                output(f, i - 1)
                        if not (first and d == 0 and s < LAG):
                            if s == LAG:
                                if not (first and d == 0):
                                    pe.wait_ge(y_read, (i * 2 + d) * DT)
                            sum_states(q - LAG, d, (s - LAG) % S)
                    if not head:
                        for s in range(S - LAG, S):
                            sum_states(i * (2 * S) + d * S + s, d, s)
                return f

            f = Fills(0)
            turn_x(f, 0)
            copied(f)
            for t in range(DT):
                conv(f, 0, t)
            for t in range(DT):
                gate(f, 0, t)
            pe.wait_ge(silu_ready, 1)
            bc_dt(f, 0)
            copied(f)
            for t in range(DT):
                delta_in(f, 0, t)
            for t in range(DT):
                conv(f, 1, t)
            for t in range(DT):
                gate(f, 1, t)
            pe.wait_ge(parts_ready, 1)
            c_rows(f, 0, 0)
            b_rows(0, 0, 0, 0, spare=True)
            assert f.n == PRO
            group(0, True, first=True)
            with pe.Fori(1, NG - 1) as i:
                assert group(i, True).n == PER
            f = group(NG - 1, False)
            output(f, NG - 1)

        @block.scalar
        def _(act):
            for at in range(0, ROWS, 2 * N):
                nc.scalar.copy(pick[at:at + 2 * N, :, :], spread(c.ident[at:at + 2 * N, at:at + 2 * N], 128)).then_inc(prepared, 1)
            act.wait_ge(loaded, ALL_LOADED)
            act.sem_inc(taken, ALL_TAKEN)
            nc.scalar.activation(a_neg[:], a_log[:], ACT.Exp).then_inc(pre_exp, 1)
            act.wait_ge(a_ready, 1)
            act.wait_ge(prepared, 4 + ROWS // (2 * N))

            def take(f, emit):
                seq, bank = f.next()
                act.wait_ge(filled, seq + 1)
                emit(ps_t[:, bank, :]).then_inc(taken, 1)

            def halve(f):
                take(f, lambda src: nc.scalar.activation(half[:], src.rearrange("p (g d) -> p g d", g=G), ACT.Copy, scale=0.5))

            def copy_x(f):
                def emit(src):
                    src = src.rearrange("p (g t) -> p g t", g=G)
                    nc.scalar.copy(xT[:, 0, :, PAD:TP], src)
                    back = bn(src[:, 0, T - 1:T], (T, G), (-1, T))
                    return nc.scalar.copy(xT[:, 1, :, PAD:TP], back)
                take(f, emit)

            def copy_u(f, d, t):
                take(f, lambda src: nc.scalar.activation(xz[:, t, :], src, ACT.Identity, bias=b_conv[:, d, t:t + 1]))

            def copy_z(f, d, t):
                take(f, lambda src: nc.scalar.copy(xz[:, DT + t, :], src))

            def silu(f, d):
                act.wait_ge(taken, f.base + f.n + ALL_TAKEN)
                nc.scalar.activation(uz[:, d, :, :], xz[:], ACT.Silu).then_inc(silu_ready, 1)

            def copy_bc(f, d):
                take(f, lambda src: nc.scalar.copy(bc[0:ROWS + R, d, :], src[0:ROWS + R, :]))

            def softplus(f, steps, d, t, n):
                if n is not None and t == 0:
                    act.wait_ge(delta_ready, n)
                take(f, lambda src: nc.scalar.activation(pre[:, t, :], src, ACT.Identity, bias=b_dt[:, d, t:t + 1]))
                if t == DT - 1:
                    act.wait_ge(taken, f.base + f.n + ALL_TAKEN)
                    steps.then(nc.scalar.activation(soft[:], pre[:], ACT.Abs))
                    steps.settle()
                    nc.scalar.activation(soft[:], soft[:], ACT.Exp, scale=-1.0).then_inc(soft_ready, 1)

            def copy_c(f, q, slot, spare=False):
                if not spare:
                    act.wait_ge(hc_ready, q - (SLOTS - 1) * DT)
                for n in range(C2):
                    take(f, lambda src: nc.scalar.copy(c_all[:, slot, n, :], src))

            def exps(q, d, s, spare=False):
                if not spare:
                    act.wait_ge(h_ready, q - SLOTS + 1)
                src = delta[:, d, s % DT, :].rearrange("p (g t) -> p g t", g=G)[:, :, 1:T]
                for n in range(C2):
                    st = (s // DT) * C2 + n
                    last = nc.scalar.activation(decay[:, s % SLOTS, n, :, 1:T], src, ACT.Exp, scale=a_neg[:, d, s % DT, st:st + 1])
                last.then_inc(decay_ready, 1)

            def group(i, more, first=False):
                f = Fills(i * PER + PRO)
                steps = Steps(act, act_steps, i * 2 + 1, 2)
                for d in range(2):
                    head = d == 0 or more
                    nd = 1 - d
                    for s in range(S):
                        q = i * (2 * S) + d * S + s
                        r = s + AHEAD
                        if r < S or head:
                            if r == S:
                                act.wait_ge(delta_ready, i * 2 + d + 2)
                            exps(q + AHEAD, d if r < S else nd, r % S, spare=first and d == 0 and r < SLOTS)
                        if s % DT == 0 and (s + DT < S or head):
                            copy_c(f, q + DT, (s // DT + 1) % SLOTS, spare=first and d == 0 and s // DT + 1 < SLOTS)
                        if s == AT_X and d == 0 and more:
                            copy_x(f)
                        if head:
                            if s == AT_SILU:
                                if not (first and d == 0):
                                    act.wait_ge(g_ready, (i * 2 + d) * DT)
                                silu(f, nd)
                            if s == AT_BC:
                                copy_bc(f, nd)
                            for t in range(DT):
                                if s == AT_DELTA[t]:
                                    softplus(f, steps, nd, t, i * 2 + d + 1)
                        if more:
                            for t in range(DT):
                                if s == AT_CONV[t]:
                                    copy_u(f, d, t)
                                if s == AT_Z[t]:
                                    copy_z(f, d, t)
                        if s == AT_OUT and d == 0:
                            halve(f)
                return f

            f = Fills(0)
            copy_x(f)
            for t in range(DT):
                copy_u(f, 0, t)
            for t in range(DT):
                copy_z(f, 0, t)
            silu(f, 0)
            copy_bc(f, 0)
            steps = Steps(act, act_steps)
            for t in range(DT):
                softplus(f, steps, 0, t, None)
            for t in range(DT):
                copy_u(f, 1, t)
            for t in range(DT):
                copy_z(f, 1, t)
            copy_c(f, 0, 0, spare=True)
            act.wait_ge(delta_ready, 1)
            for q in range(AHEAD):
                exps(q, 0, q, spare=True)
            group(0, True, first=True)
            with act.Fori(1, NG - 1) as i:
                group(i, True)
            f = group(NG - 1, False)
            halve(f)

        @block.gpsimd
        def _(pool):
            pool.memset(xT[:, :, :, 0:PAD], 0.0).then_inc(prepared, 1)
            for slot in range(SLOTS):
                last = pool.memset(decay[:, slot, :, :, 0], 0.0)
            last.then_inc(prepared, 1)

            def times_u(d, n):
                pool.wait_ge(delta_ready, n + 1)
                nc.gpsimd.tensor_tensor(du[:, d, :, :], delta[:, d, :, :], u[:, d, :, :], ALU.mult).then_inc(du_ready, 1)

            def gating(d, n):
                for t in range(DT):
                    pool.wait_ge(y_read, n * DT + t + 1)
                    dst = g[:, d, t, :, :] if d == 0 else bn(g[:, d, t, 0, T - 1:T], (T, G), (-1, T))
                    nc.gpsimd.tensor_tensor(dst, y[:, t, :].rearrange("p (g t) -> p g t", g=G), sz[:, d, t, :].rearrange("p (g t) -> p g t", g=G), ALU.mult)\
                        .then_inc(g_ready, 1)

            def group(i, more, first=False):
                for d in range(2):
                    head = d == 0 or more
                    for s in range(S):
                        q = i * (2 * S) + d * S + s
                        if s == AT_GATE + 1 and not (first and d == 0):
                            gating(1 - d, i * 2 + d - 1)
                        if s == AT_LOG[-1] + 1 and head:
                            times_u(1 - d, i * 2 + d + 1)
                        if s % DT == 0:
                            if s > 0:
                                pool.wait_ge(taken, taken_by(i, fillings_before(d, s - DT, more) + C2))
                            else:
                                pool.wait_ge(taken, taken_by(i, d and fillings_before(0, S - DT, more) + C2))
                        pool.wait_ge(h_ready, q + 1)
                        slot, chunk = s % SLOTS, (s // DT) % SLOTS
                        nc.gpsimd.tensor_tensor(h[:, slot, :, :], h[:, slot, :, :], c_all[:, chunk, :, :], ALU.mult).then_inc(hc_ready, 1)
                        if s == AT_ROOT and d == 0 and not first:
                            after.root(nc, pool, c, i - 1)

            times_u(0, 0)
            group(0, True, first=True)
            with pool.Fori(1, NG - 1) as i:
                group(i, True)
            group(NG - 1, False)
            gating(1, NG * 2 - 1)
            after.root(nc, pool, c, NG - 1)

        @block.vector
        def _(dve):
            dve.wait_ge(loaded, ALL_LOADED)
            for d in range(2):
                nc.vector.tensor_tensor(w_tap[:, d, :, :], w_tap[:, d, :, :], repeat(w_in[:, d, 0:DT * 128], W), ALU.mult).then_inc(prepared, 1)
            dve.wait_ge(pre_exp, 1)
            nc.vector.tensor_scalar(a_neg[:], a_neg[:], -1.0, None, ALU.mult).then_inc(a_ready, 1)

            def split(steps, d, copied):
                dve.wait_ge(taken, copied)
                whole = bc[0:ROWS, d, :]
                steps.then(nc.vector.tensor_copy(parts[:, d, :], whole))
                steps.settle()
                steps.then(nc.vector.tensor_tensor(rest[:], whole, parts[:, d, :], ALU.subtract))
                steps.settle()
                steps.then(nc.vector.tensor_copy(mid[:], rest[:]))
                steps.then(nc.vector.tensor_copy(parts[32:64, d, :], rest[32:64, :]))
                steps.settle()
                nc.vector.tensor_tensor(parts[64:ROWS, d, :], rest[64:ROWS, :], mid[64:ROWS, :], ALU.subtract).then_inc(parts_ready, 1)

            def log1p(steps, part):
                if part == 0:
                    steps.then(nc.vector.tensor_scalar(poly[:], soft[:], LOG1P[8], LOG1P[7], ALU.mult, ALU.add))
                    steps.settle()
                    steps.then(nc.vector.tensor_tensor(poly[:], poly[:], soft[:], ALU.mult))
                    steps.settle()
                for k in {0: (6, 5), 1: (4, 3, 2), 2: (1, 0)}[part]:
                    steps.then(nc.vector.scalar_tensor_tensor(out=poly[:], in0=poly[:], scalar=LOG1P[k], in1=soft[:], op0=ALU.add, op1=ALU.mult))
                    steps.settle()

            def deltas(d):
                nc.vector.scalar_tensor_tensor(out=delta[:, d, :, :], in0=pre[:], scalar=0.0, in1=poly[:], op0=ALU.max, op1=ALU.add)\
                    .then_inc(delta_ready, 1)

            def skipped(d, n):
                dve.wait_ge(y_done, (n + 1) * S)
                for t in range(DT):
                    nc.vector.scalar_tensor_tensor(out=y[:, t, :], in0=u[:, d, t, :], scalar=d_skip[:, d, t:t + 1], in1=ps_y[:, t, :],
                                                   op0=ALU.mult, op1=ALU.add).then_inc(y_read, 1)

            def total_of(steps, n, copied):
                dve.wait_ge(taken, copied)
                nc.vector.tensor_tensor(total[:], half[:], x_all[:, bass.ds(n * G, G), :], ALU.add).then_inc(total_ready, 1)
                dve.wait_ge(total_ready, n + 1)
                after.take_moments(nc, steps, total[:])

            def finish(n):
                after.apply(nc, dve, total[:], lambda b: x_all[:, bass.ds(n * G + b, 1), :], n, x_ready)
                dve.wait_ge(x_ready, n * G + G)

            def group(i, more, steps, first=False):
                for d in range(2):
                    head = d == 0 or more
                    nd = 1 - d
                    for s in range(S):
                        q = i * (2 * S) + d * S + s
                        if s == 0:
                            dve.wait_ge(du_ready, i * 2 + d + 1)
                        dve.wait_ge(b_ready, q + 1)
                        b = ps_b[:, s % 2, :, :]
                        steps.then(nc.vector.tensor_tensor(b, b, repeat(du[:, d, s % DT, :], C2), ALU.mult))
                        steps.settle()
                        dve.wait_ge(decay_ready, q + 1)
                        if not (first and d == 0 and s < SLOTS):
                            dve.wait_ge(y_done, q - SLOTS + 1)
                        nc.vector.tensor_tensor_scan(h[:, s % SLOTS, :, :].rearrange("p n t -> p (n t)"),
                                                     decay[:, s % SLOTS, :, :, :].rearrange("p n g t -> p (n g t)"),
                                                     b.rearrange("p n t -> p (n t)"), 0.0, ALU.mult, ALU.add).then_inc(h_ready, 1)
                        if s == AT_GATE and not (first and d == 0):
                            skipped(nd, i * 2 + d - 1)
                        if head:
                            if s == AT_SPLIT:
                                split(steps, nd, taken_by(i, fillings_before(d, AT_BC + 1, more)))
                            if s in AT_LOG:
                                if s == AT_LOG[0]:
                                    dve.wait_ge(soft_ready, i * 2 + d + 2)
                                log1p(steps, s - AT_LOG[0])
                            if s == AT_LOG[-1]:
                                deltas(nd)
                        if d == 0 and not first:
                            if s == AT_TOTAL:
                                total_of(steps, i - 1, taken_by(i, fillings_before(0, AT_OUT + 1, more)))
                            if s == AT_FINISH:
                                finish(i - 1)

            HEAD = 4 + 9
            FIRST, per_loop = 2 * S + 2 * HEAD, 2 * S + 2 * HEAD + 2 * G
            steps = Steps(dve, dve_steps)
            split(steps, 0, 1 + 2 * DT + 1 + ALL_TAKEN)
            dve.wait_ge(soft_ready, 1)
            for part in range(3):
                log1p(steps, part)
            deltas(0)
            assert steps.n == HEAD
            steps = Steps(dve, dve_steps, HEAD)
            group(0, True, steps, first=True)
            assert steps.n == FIRST
            with dve.Fori(1, NG - 1) as i:
                steps = Steps(dve, dve_steps, i * per_loop + HEAD + FIRST - per_loop, per_loop)
                group(i, True, steps)
                steps.closed()
            steps = Steps(dve, dve_steps, (NG - 1) * per_loop + HEAD + FIRST - per_loop)
            group(NG - 1, False, steps)
            skipped(1, NG * 2 - 1)
            total_of(steps, NG - 1, taken_by(NG - 1, fillings_before(1, S, False) + 1))
            finish(NG - 1)


def cross_attention(nc, stage, x_all, ctx_dram, c, p):
    XH, XD = 8, D // 8
    XK = XH // NJ
    PAIRS = G // 2
    N2 = 2 * T
    with ExitStack() as stack:
        m = Mem(nc, stack, stage)
        PADDED = D + QUAD - XD
        w_q = m.sb("w_q", [D, PADDED])
        w_k = m.sb("w_k", [D, PADDED])
        w_v = m.sb("w_v", [D, D])
        w_o = m.sb("w_o", [D, D])
        xg = m.sb("xg", [T, G, D])
        ctx = m.sb("ctx", [T, G, D])
        xT = m.sb("xT", [D, GT])
        ctxT = m.sb("ctxT", [D, GT])
        qT = m.sb("qT", [T, XK, GT])
        kT = m.sb("kT", [T, XK, GT])
        v_wide = m.sb("v_wide", [T, G, XH, D])
        e = m.sb("e", [T, PAIRS, XH, N2])
        top = m.sb("top", [T, PAIRS, N2])
        total_e = m.sb("total_e", [T, PAIRS, N2])
        inv = m.sb("inv", [T, PAIRS, N2])
        attT = m.sb("attT", [D, GT])
        total = m.sb("total", [T, G, D])
        after = Norm(m, "after")
        ps_s = m.ps("ps_s", [T, NJ, XK, N2])
        ps_t = m.ps("ps_t", [T, 2, BANK])
        ps_o = m.ps("ps_o", [T, BANK])
        ps_y = m.ps("ps_y", [T, BANK])

        loaded = m.sem("loaded")
        group_in = m.sem("group_in")
        padded = m.sem("padded")
        filled = m.sem("filled")
        taken = m.sem("taken")
        scores_ready = m.sem("scores_ready")
        shifted = m.sem("shifted")
        exp_ready = m.sem("exp_ready")
        inv_ready = m.sem("inv_ready")
        att_w_ready = m.sem("att_w_ready")
        v_filled = m.sem("v_filled")
        v_taken = m.sem("v_taken")
        values_ready = m.sem("values_ready")
        att_ready = m.sem("att_ready")
        out_ready = m.sem("out_ready")
        total_ready = m.sem("total_ready")
        x_ready = m.sem("x_ready")
        dve_steps = m.sem("dve_steps")
        block = stack.enter_context(nc.Block())
        LOADS = ((w_q[:, 0:D], p["w_q"]), (w_k[:, 0:D], p["w_k"]), (w_v[:], p["w_v"]), (w_o[:], p["w_o"]))
        ALL_LOADED = 16 * len(LOADS)
        PER = 6
        ALL_TAKEN = 2

        @block.sync
        def _(sp):
            for dst, src in LOADS:
                sp.dma_start(dst, src).then_inc(loaded, 16)
            for dst, src in ((xg, x_all), (ctx, ctx_dram)):
                sp.dma_start(dst[:], src[:, 0:G, :]).then_inc(group_in, 16)

            def next_group(i):
                for dst, src in ((xg, x_all), (ctx, ctx_dram)):
                    sp.dma_start(dst[:], src[:, bass.ds(i * G, G), :]).then_inc(group_in, 16)

            sp.wait_ge(filled, 2)
            next_group(1)
            with sp.Fori(2, NG) as i:
                sp.wait_ge(filled, i * PER - PER + 2)
                next_group(i)

        @block.tensor
        def _(pe):
            pe.wait_ge(loaded, ALL_LOADED)
            pe.wait_ge(padded, 3)

            def fill(seq, bank, emit):
                pe.wait_ge(taken, seq + 1)
                emit(ps_t[:, bank, :]).then_inc(filled, 1)

            def turn(src):
                def emit(dst):
                    for b in range(G):
                        last = nc.tensor.transpose(dst[:, b * T:(b + 1) * T], src[:, b, :], c.ident[:])
                    return last
                return emit

            def turn_in(n, seq, bank):
                pe.wait_ge(group_in, n * 32 + 32)
                fill(seq, bank, turn(xg))
                fill(seq + 1, 1 - bank, turn(ctx))

            def project(seq, bank):
                pe.wait_ge(taken, seq + 2 + ALL_TAKEN)
                for o, (w, src) in enumerate(((w_q, xT), (w_q, xT), (w_k, ctxT), (w_k, ctxT))):
                    k = o % 2
                    fill(seq + 2 + o, (bank + o) % 2, lambda dst: nc.tensor.matmul(dst, w[:, k * XD:k * XD + T], src[:], start=True, stop=True))

            def values_in():
                for b in range(G):
                    last = nc.tensor.matmul(ps_y[:, b * D:(b + 1) * D], ctxT[:, b * T:(b + 1) * T], w_v[:],
                                            start=(b == 0), stop=(b == G - 1), skip_group_check=True)
                last.then_inc(v_filled, 1)

            def scores(i, pair, first=False):
                if not (first and pair == 0):
                    pe.wait_ge(shifted, i * PAIRS + pair)
                for n in range(2):
                    t = slice((pair * 2 + n) * T, (pair * 2 + n + 1) * T)
                    for k in range(XK):
                        for j in range(NJ):
                            r = slice(j * QUAD, j * QUAD + XD)
                            last = nc.tensor.matmul(ps_s[:, j, k, n * T:(n + 1) * T], kT[r, k, t], qT[r, k, t],
                                                    start=(n == 0 and k == 0), stop=(n == 1 and k == XK - 1), skip_group_check=True)
                last.then_inc(scores_ready, 1)

            def values(i, pair):
                pe.wait_ge(att_w_ready, i * PAIRS + pair + 1)
                for n in range(2):
                    b = pair * 2 + n
                    for h in range(XH):
                        last = nc.tensor.matmul(ps_o[:, b * T:(b + 1) * T], v_wide[:, b, h, :], e[:, pair, h, n * T:(n + 1) * T],
                                                start=(b == 0 and h == 0), stop=(b == G - 1 and h == XH - 1), skip_group_check=True)
                if pair == PAIRS - 1:
                    last.then_inc(values_ready, 1)

            def output(i):
                pe.wait_ge(att_ready, i + 1)
                for b in range(G):
                    last = nc.tensor.matmul(ps_y[:, b * D:(b + 1) * D], attT[:, b * T:(b + 1) * T], w_o[:],
                                            start=(b == 0), stop=(b == G - 1), skip_group_check=True)
                last.then_inc(out_ready, 1)

            def group(i, more, second=False):
                first = isinstance(i, int) and i == 0
                seq = i * PER + PER
                pe.wait_ge(taken, seq + ALL_TAKEN)
                scores(i, 0, first)
                if not first:
                    values(i - 1, 1)
                if not first and not second:
                    pe.wait_ge(total_ready, i - 1)
                values_in()
                if more:
                    turn_in(i + 1, seq, 0)
                pe.wait_ge(v_taken, i + 1)
                if not first:
                    output(i - 1)
                scores(i, 1)
                values(i, 0)
                if more:
                    project(seq, 0)

            turn_in(0, 0, 0)
            project(0, 0)
            group(0, True)
            group(1, True, second=True)
            with pe.Fori(2, NG - 1) as i:
                group(i, True)
            group(NG - 1, False)
            values(NG - 1, 1)
            pe.wait_ge(total_ready, NG - 1)
            output(NG - 1)

        @block.scalar
        def _(act):
            act.sem_inc(taken, ALL_TAKEN)

            def copy_out(seq, bank, dst):
                act.wait_ge(filled, seq + 1)
                nc.scalar.copy(dst, ps_t[:, bank, :]).then_inc(taken, 1)

            def copy_turned(seq, bank):
                copy_out(seq, bank, xT[:])
                copy_out(seq + 1, 1 - bank, ctxT[:])

            def copy_projected(seq, bank):
                for o, dst in enumerate((qT[:, 0, :], qT[:, 1, :], kT[:, 0, :], kT[:, 1, :])):
                    copy_out(seq + 2 + o, (bank + o) % 2, dst)

            def exp(i, pair):
                act.wait_ge(shifted, i * PAIRS + pair + 1)
                nc.scalar.activation(e[:, pair, :, :], e[:, pair, :, :], ACT.Exp, scale=XD ** -0.5).then_inc(exp_ready, 1)

            def copy_attention(i):
                act.wait_ge(values_ready, i + 1)
                nc.scalar.copy(attT[:], ps_o[:]).then_inc(att_ready, 1)

            def group(i, more, first=False):
                seq = i * PER + PER
                exp(i, 0)
                if not first:
                    copy_attention(i - 1)
                act.wait_ge(v_filled, i + 1)
                nc.scalar.copy(bn(v_wide[:, 0, 0, 0:1], (XH * D, G), (D + XD, XH), (1, XD)), ps_y[:].rearrange("p (g h d) -> p g h d", g=G, h=XH))\
                    .then_inc(v_taken, 1)
                if more:
                    copy_turned(seq, 0)
                exp(i, 1)
                if more:
                    copy_projected(seq, 0)

            act.wait_ge(padded, 3)
            copy_turned(0, 0)
            copy_projected(0, 0)
            group(0, True, first=True)
            with act.Fori(1, NG - 1) as i:
                group(i, True)
            group(NG - 1, False)
            copy_attention(NG - 1)

        @block.gpsimd
        def _(pool):
            pool.memset(w_q[:, D:PADDED], 0.0).then_inc(padded, 1)
            pool.memset(w_k[:, D:PADDED], 0.0).then_inc(padded, 1)
            pool.memset(v_wide[:], 0.0).then_inc(padded, 1)

            def group(i, first=False):
                for pair in range(PAIRS):
                    pool.wait_ge(inv_ready, i * PAIRS + pair + 1)
                    nc.gpsimd.tensor_tensor(e[:, pair, :, :], e[:, pair, :, :], repeat(inv[:, pair, :], XH), ALU.mult).then_inc(att_w_ready, 1)
                if not first:
                    after.root(nc, pool, c, i - 1)

            group(0, first=True)
            with pool.Fori(1, NG) as i:
                group(i)
            after.root(nc, pool, c, NG - 1)

        @block.vector
        def _(dve):

            def pairs(steps, i):
                for pair in range(PAIRS):
                    dve.wait_ge(scores_ready, i * PAIRS + pair + 1)
                    s = ps_s[:].rearrange("p j k n -> p (j k) n")
                    steps.then(nc.vector.tensor_reduce(top[:, pair, :], s.rearrange("p h n -> p n h"), AX_X, ALU.max))
                    steps.settle()
                    nc.vector.tensor_tensor(e[:, pair, :, :], s, repeat(top[:, pair, :], XH), ALU.subtract).then_inc(shifted, 1)
                    dve.wait_ge(exp_ready, i * PAIRS + pair + 1)
                    steps.then(nc.vector.tensor_reduce(total_e[:, pair, :], e[:, pair, :, :].rearrange("p h n -> p n h"), AX_X, ALU.add))
                    steps.settle()
                    nc.vector.reciprocal(inv[:, pair, :], total_e[:, pair, :]).then_inc(inv_ready, 1)

            def finish(steps, i):
                dve.wait_ge(out_ready, i + 1)
                nc.vector.tensor_tensor(total[:], ps_y[:].rearrange("p (g d) -> p g d", g=G), x_all[:, bass.ds(i * G, G), :], ALU.add)\
                    .then_inc(total_ready, 1)
                dve.wait_ge(total_ready, i + 1)
                after.take_moments(nc, steps, total[:])
                after.apply(nc, dve, total[:], lambda b: x_all[:, bass.ds(i * G + b, 1), :], i, x_ready)
                dve.wait_ge(x_ready, i * G + G)

            PAIR_STEPS, per_loop = 2 * PAIRS, 2 * PAIRS + 2 * G
            pairs(Steps(dve, dve_steps), 0)
            with dve.Fori(1, NG) as i:
                steps = Steps(dve, dve_steps, i * per_loop + PAIR_STEPS - per_loop, per_loop)
                pairs(steps, i)
                finish(steps, i - 1)
                steps.closed()
            finish(Steps(dve, dve_steps, (NG - 1) * per_loop + PAIR_STEPS), NG - 1)


MAGIC = 1.5 * 2.0 ** 23


def quant_ffn(nc, stage, x_all, out_dram, c, p):
    F = 3 * 128
    KF = F // 128
    BLOCK = 32
    NB = 4
    PIECE = KF * B * T // NB
    with ExitStack() as stack:
        m = Mem(nc, stack, stage)
        w_raw = m.sb("w_raw", [128, 3, F])
        w_amax = m.sb("w_amax", [128, 3, F // BLOCK])
        w_scale = m.sb("w_scale", [128, 3, F // BLOCK])
        w_T = m.sb("w_T", [128, 3, F])
        w_inv = m.sb("w_inv", [128, 3, F // BLOCK])
        w_head = m.sb("w_head", [128, 3, F // BLOCK])
        w_tail = m.sb("w_tail", [128, 3, F // BLOCK])
        magic = m.sb("magic", [128, 2])
        amax_part = m.sb("amax_part", [128, 5])
        amax = m.sb("amax", [128, 5])
        scale = m.sb("scale", [128, 5])
        inv = m.sb("inv", [128, 5])
        amax_in = m.sb("amax_in", [128, 2, NG * KF])
        amax_left = m.sb("amax_left", [128, 3 * F // BLOCK])
        amax_piece = m.sb("amax_piece", [128, 2, NB])
        xq = m.sb("xq", [T, U, G, D])
        xqT = m.sb("xqT", [D, U, GT])
        gate = m.sb("gate", [128, NG, KF, GT])
        up = m.sb("up", [128, NG, KF, GT])
        sig = m.sb("sig", [128, 2, PIECE])
        hidden = m.sb("hidden", [128, U, KF, GT])
        total = m.sb("total", [T, U, G, D])
        res = m.sb("res", [T, U, G, D])
        after = [Norm(m, f"after{u}") for u in range(U)]
        ps_x = m.ps("ps_x", [128, U, BANK])
        ps_f = m.ps("ps_f", [128, 2, KF, GT])

        loaded = m.sem("loaded")
        w_rounded = m.sem("w_rounded")
        w_turned = m.sem("w_turned")
        wT_ready = m.sem("wT_ready")
        part_ready = m.sem("part_ready")
        amax_ready = m.sem("amax_ready")
        xq_ready = m.sem("xq_ready")
        xq_turned = m.sem("xq_turned")
        xqT_ready = m.sem("xqT_ready")
        ff_ready = m.sem("ff_ready")
        ff_taken = m.sem("ff_taken")
        ff_measured = m.sem("ff_measured")
        gate_ready = m.sem("gate_ready")
        magic_ready = m.sem("magic_ready")
        scale_ready = m.sem("scale_ready")
        up_shifted = m.sem("up_shifted")
        up_ready = m.sem("up_ready")
        sig_steps = m.sem("sig_steps")
        sig_ready = m.sem("sig_ready")
        sig_used = m.sem("sig_used")
        hidden_ready = m.sem("hidden_ready")
        down_ready = m.sem("down_ready")
        total_ready = m.sem("total_ready")
        res_ready = m.sem("res_ready")
        stored = [m.sem(f"stored{u}") for u in range(U)]
        dve_steps = m.sem("dve_steps")
        block = stack.enter_context(nc.Block())
        W_GATE, W_UP, W_DOWN = range(3)
        A_X, A_UP, A_GATE, A_SWISH, A_OUT = range(5)
        gate_flat = gate[:].rearrange("p n k t -> p (n k t)")
        sig_flat = sig[:].rearrange("p n t -> p (n t)")
        up_flat = up[:].rearrange("p n k t -> p (n k t)")

        @block.sync
        def _(sp):
            for n, w in ((W_GATE, "w_gate"), (W_UP, "w_up")):
                sp.dma_start(w_raw[:, n, :].rearrange("p (k i) -> p k i", i=D), p[w].rearrange("(k q) i -> q k i", q=128)).then_inc(loaded, 16)
            sp.dma_start(w_raw[:, W_DOWN, :], p["w_down"]).then_inc(loaded, 16)
            with sp.Fori(0, NG // U) as i:
                for u in range(U):
                    sp.wait_ge(res_ready, (i * U + u) * G + G)
                    sp.dma_start(out_dram[:, bass.ds((i * U + u) * G, G), :], res[:, u, :, :]).then_inc(stored[u], 16)
            for u in range(U):
                sp.wait_ge(stored[u], 16 * (NG // U))

        @block.tensor
        def _(pe):
            pe.wait_ge(w_rounded, 1)
            for n in range(3):
                for k in range(KF):
                    last = nc.tensor.transpose(ps_f[:, 0, n, k * 128:(k + 1) * 128], w_raw[:, n, k * 128:(k + 1) * 128], c.ident[:])
            last.then_inc(w_turned, 1)
            pe.wait_ge(wT_ready, 1)

            def feed_forward(n, u, first=False):
                for b in range(G):
                    pe.wait_ge(xq_ready, n * G + b + 1)
                    last = nc.tensor.transpose(ps_x[:, u, b * T:(b + 1) * T], xq[:, u, b, :], c.ident[:])
                last.then_inc(xq_turned, 1)
                pe.wait_ge(xqT_ready, n + 1)
                for w in (W_GATE, W_UP):
                    for k in range(KF):
                        if not first:
                            pe.wait_ge(ff_taken, n * 2 * KF - 2 * KF + w * KF + k + 1)
                        nc.tensor.matmul(ps_f[:, w, k, :], w_T[:, w, k * 128:(k + 1) * 128], xqT[:, u, :], start=True, stop=True).then_inc(ff_ready, 1)

            for u in range(U):
                feed_forward(u, u, first=u == 0)
            with pe.Fori(1, NG // U) as i:
                for u in range(U):
                    feed_forward(i * U + u, u)
            with pe.Fori(0, NG // U) as i:
                for u in range(U):
                    pe.wait_ge(hidden_ready, i * U + u + 1)
                    for b in range(G):
                        for k in range(KF):
                            last = nc.tensor.matmul(ps_x[:, u, b * D:(b + 1) * D], hidden[:, u, k, b * T:(b + 1) * T], w_T[:, W_DOWN, k * 128:(k + 1) * 128],
                                                    start=(b == 0 and k == 0), stop=(b == G - 1 and k == KF - 1), skip_group_check=True)
                    last.then_inc(down_ready, 1)

        @block.scalar
        def _(act):
            act.wait_ge(w_turned, 1)
            nc.scalar.copy(w_T[:], ps_f[:, 0, :, 0:F]).then_inc(wT_ready, 1)
            with act.Fori(0, NG // U) as i:
                for u in range(U):
                    n = i * U + u
                    act.wait_ge(xq_turned, n + 1)
                    nc.scalar.copy(xqT[:, u, :], ps_x[:, u, :]).then_inc(xqT_ready, 1)
                    for w, dst in ((W_GATE, gate), (W_UP, up)):
                        for k in range(KF):
                            act.wait_ge(ff_ready, n * 2 * KF + w * KF + k + 1)
                            nc.scalar.copy(dst[:, bass.ds(n, 1), k, :], ps_f[:, w, k, :].unsqueeze(1)).then_inc(ff_taken, 1)
            act.wait_ge(magic_ready, 2)
            for n in range(NB):
                at = slice(n * PIECE, (n + 1) * PIECE)
                act.wait_ge(gate_ready, n + 1)
                if n >= 2:
                    act.wait_ge(sig_used, n - 1)
                nc.scalar.activation(sig[:, n % 2, :], gate_flat[:, at], ACT.Sigmoid).then_inc(sig_steps, 1)
                act.wait_ge(sig_steps, n + 1)
                nc.scalar.activation(sig[:, n % 2, :], sig[:, n % 2, :], ACT.Identity, bias=magic[:, 0:1], scale=65536.0).then_inc(sig_ready, 1)
                act.wait_ge(scale_ready, 1)
                nc.scalar.activation(up_flat[:, at], up_flat[:, at], ACT.Identity, bias=magic[:, 0:1], scale=inv[:, A_UP:A_UP + 1]).then_inc(up_shifted, 1)
                act.wait_ge(up_shifted, n + 1)
                nc.scalar.activation(up_flat[:, at], up_flat[:, at], ACT.Identity, bias=magic[:, 1:2]).then_inc(up_ready, 1)

        @block.gpsimd
        def _(pool):
            for n, columns in enumerate((slice(A_X, A_X + 1), slice(A_UP, A_GATE + 1), slice(A_SWISH, A_SWISH + 1), slice(A_OUT, A_OUT + 1))):
                pool.wait_ge(part_ready, n + 1)
                nc.gpsimd.partition_all_reduce(amax[:, columns], amax_part[:, columns], 128, bass.bass_isa.ReduceOp.max).then_inc(amax_ready, 1)
            with pool.Fori(0, NG // U) as i:
                for u in range(U):
                    after[u].root(nc, pool, c, i)

        @block.vector
        def _(dve):
            steps = Steps(dve, dve_steps)

            def share(out, largest, q):
                steps.then(nc.vector.tensor_scalar(out, largest, 1.0 / q, None, ALU.mult))
                steps.settle()
                left = amax_left[:, 0:out.shape[-1]]
                steps.then(nc.vector.scalar_tensor_tensor(out=left, in0=out, scalar=-(q + 1.0), in1=largest, op0=ALU.mult, op1=ALU.add))
                steps.settle()
                steps.then(nc.vector.tensor_tensor(left, left, out, ALU.add))
                steps.settle()
                steps.then(nc.vector.scalar_tensor_tensor(out=out, in0=left, scalar=1.0 / q, in1=out, op0=ALU.mult, op1=ALU.add))
                steps.settle()
                steps.then(nc.vector.tensor_scalar(out, out, 1e-12, None, ALU.max))
                steps.settle()

            def scales(n, columns):
                dve.wait_ge(amax_ready, n)
                share(scale[:, columns], amax[:, columns], 2.0 ** 15 - 1.0)
                steps.then(nc.vector.reciprocal(inv[:, columns], scale[:, columns]))
                steps.settle()

            def quantize(steps, out, src, a, tmp=None):
                tmp = out if tmp is None else tmp
                steps.then(nc.vector.tensor_scalar(tmp, src, inv[:, a:a + 1], MAGIC, ALU.mult, ALU.add))
                steps.settle()
                return nc.vector.tensor_scalar(out, tmp, MAGIC, scale[:, a:a + 1], ALU.subtract, ALU.mult)

            nc.vector.memset(magic[:, 0:1], MAGIC).then_inc(magic_ready, 1)
            nc.vector.memset(magic[:, 1:2], -MAGIC).then_inc(magic_ready, 1)
            nc.vector.tensor_reduce(amax_part[:, A_X:A_X + 1], x_all[:].rearrange("p b d -> p (b d)"), AX_X, ALU.max, apply_absolute_value=True)\
                .then_inc(part_ready, 1)
            dve.wait_ge(loaded, 48)
            blocks = w_raw[:].rearrange("p n (m j) -> p n m j", j=BLOCK)
            steps.then(nc.vector.tensor_reduce(w_amax[:], blocks, AX_X, ALU.max, apply_absolute_value=True))
            steps.settle()
            flat = lambda t: t[:].rearrange("p n m -> p (n m)")
            share(flat(w_scale), flat(w_amax), 7.0)
            steps.then(nc.vector.reciprocal(w_inv[:], w_scale[:]))
            steps.then(nc.vector.tensor_scalar(w_head[:], w_scale[:], 2.0 ** 12 + 1.0, None, ALU.mult))
            steps.settle()
            steps.then(nc.vector.tensor_tensor(w_tail[:], w_head[:], w_scale[:], ALU.subtract))
            steps.settle()
            steps.then(nc.vector.tensor_tensor(w_head[:], w_head[:], w_tail[:], ALU.subtract))
            steps.settle()
            steps.then(nc.vector.tensor_tensor(w_tail[:], w_scale[:], w_head[:], ALU.subtract))
            s_all, inv_all, head_all, tail_all = [spread(flat(t), BLOCK) for t in (w_scale, w_inv, w_head, w_tail)]
            w_all = w_raw[:].rearrange("p n (m j) -> p (n m) j", j=BLOCK)
            W = 3 * F
            quot, q_head, product, rest = [sig_flat[:, n * W:(n + 1) * W].rearrange("p (m j) -> p m j", j=BLOCK) for n in range(4)]
            steps.then(nc.vector.tensor_tensor(quot, w_all, inv_all, ALU.mult))
            steps.settle()
            steps.then(nc.vector.tensor_scalar(q_head, quot, MAGIC / 256.0, MAGIC / 256.0, ALU.add, ALU.subtract))
            steps.settle()
            steps.then(nc.vector.tensor_tensor(product, q_head, head_all, ALU.mult))
            steps.settle()
            steps.then(nc.vector.tensor_tensor(rest, w_all, product, ALU.subtract))
            steps.settle()
            steps.then(nc.vector.tensor_tensor(product, q_head, tail_all, ALU.mult))
            steps.then(nc.vector.tensor_tensor(q_head, quot, q_head, ALU.subtract))
            steps.settle()
            steps.then(nc.vector.tensor_tensor(rest, rest, product, ALU.subtract))
            steps.settle()
            steps.then(nc.vector.tensor_tensor(q_head, q_head, s_all, ALU.mult))
            steps.settle()
            steps.then(nc.vector.tensor_tensor(rest, rest, q_head, ALU.subtract))
            steps.settle()
            steps.then(nc.vector.tensor_tensor(rest, rest, inv_all, ALU.mult))
            steps.settle()
            steps.then(nc.vector.tensor_tensor(w_all, quot, rest, ALU.add))
            steps.settle()
            steps.then(nc.vector.tensor_scalar(w_all, w_all, MAGIC, MAGIC, ALU.add, ALU.subtract))
            steps.settle()
            steps.then(nc.vector.tensor_scalar(w_all, w_all, 7.0, -8.0, ALU.min, ALU.max))
            steps.settle()
            nc.vector.tensor_tensor(w_all, w_all, s_all, ALU.mult).then_inc(w_rounded, 1)

            scales(1, slice(A_X, A_X + 1))
            base = steps.n

            def round_x(steps, n, u):
                x = x_all[:, bass.ds(n * G, G), :]
                steps.then(nc.vector.tensor_scalar(xq[:, u, :, :], x, inv[:, A_X:A_X + 1], MAGIC, ALU.mult, ALU.add))
                steps.settle()
                for b in range(G):
                    nc.vector.tensor_scalar(xq[:, u, b, :], xq[:, u, b, :], MAGIC, scale[:, A_X:A_X + 1], ALU.subtract, ALU.mult).then_inc(xq_ready, 1)

            with dve.Fori(0, NG // U) as i:
                loop = Steps(dve, dve_steps, i * U + base, U)
                for u in range(U):
                    round_x(loop, i * U + u, u)
                for u in range(U):
                    n = i * U + u
                    for w, src in ((W_GATE, gate), (W_UP, up)):
                        for k in range(KF):
                            dve.wait_ge(ff_taken, n * 2 * KF + w * KF + k + 1)
                            nc.vector.tensor_reduce(amax_in[:, 1 - w, bass.ds(n * KF + k, 1)], src[:, bass.ds(n, 1), k, :].rearrange("p a t -> p (a t)"),
                                                    AX_X, ALU.max, apply_absolute_value=True).then_inc(ff_measured, 1)
                loop.closed()
            steps.base = NG
            dve.wait_ge(ff_measured, NG * 2 * KF)
            nc.vector.tensor_reduce(amax_part[:, A_UP:A_GATE + 1], amax_in[:], AX_X, ALU.max).then_inc(part_ready, 1)
            scales(2, slice(A_UP, A_GATE + 1))
            dve.sem_inc(scale_ready, 1)

            pieces = [slice(n * PIECE, (n + 1) * PIECE) for n in range(NB)]
            for n, at in enumerate(pieces):
                quantize(steps, gate_flat[:, at], gate_flat[:, at], A_GATE).then_inc(gate_ready, 1)
            for n, at in enumerate(pieces):
                s = sig[:, n % 2, :]
                dve.wait_ge(sig_ready, n + 1)
                steps.then(nc.vector.tensor_scalar(s, s, MAGIC, 65535.0, ALU.subtract, ALU.min))
                steps.settle()
                nc.vector.scalar_tensor_tensor(out=gate_flat[:, at], in0=s, scalar=1.0 / 65536.0, in1=gate_flat[:, at], op0=ALU.mult, op1=ALU.mult).then_inc(sig_used, 1)
                dve.wait_ge(sig_used, n + 1)
                steps.then(nc.vector.tensor_reduce(amax_piece[:, 0, n:n + 1], gate_flat[:, at], AX_X, ALU.max, apply_absolute_value=True))
            steps.settle()
            nc.vector.tensor_reduce(amax_part[:, A_SWISH:A_SWISH + 1], amax_piece[:, 0, :], AX_X, ALU.max).then_inc(part_ready, 1)
            scales(3, slice(A_SWISH, A_SWISH + 1))
            for n, at in enumerate(pieces):
                steps.then(quantize(steps, gate_flat[:, at], gate_flat[:, at], A_SWISH))
                steps.settle()
                dve.wait_ge(up_ready, n + 1)
                steps.then(nc.vector.scalar_tensor_tensor(out=gate_flat[:, at], in0=up_flat[:, at], scalar=scale[:, A_UP:A_UP + 1], in1=gate_flat[:, at],
                                                          op0=ALU.mult, op1=ALU.mult))
                steps.settle()
                steps.then(nc.vector.tensor_reduce(amax_piece[:, 1, n:n + 1], gate_flat[:, at], AX_X, ALU.max, apply_absolute_value=True))
            steps.settle()
            nc.vector.tensor_reduce(amax_part[:, A_OUT:A_OUT + 1], amax_piece[:, 1, :], AX_X, ALU.max).then_inc(part_ready, 1)
            scales(4, slice(A_OUT, A_OUT + 1))
            base = steps.base + steps.n

            def last_round(loop, i):
                for u in range(U):
                    src = gate[:, bass.ds(i * U + u, 1), :, :].rearrange("p a k t -> p (a k t)")
                    quantize(loop, hidden[:, u, :, :].rearrange("p k t -> p (k t)"), src, A_OUT, tmp=src).then_inc(hidden_ready, 1)

            def put_out(loop, i, more, first=False):
                if not first:
                    dve.wait_ge(res_ready, i * (U * G))
                for u in range(U):
                    n = i * U + u
                    dve.wait_ge(down_ready, n + 1)
                    nc.vector.tensor_tensor(total[:, u, :, :], ps_x[:, u, :].rearrange("p (g d) -> p g d", g=G), x_all[:, bass.ds(n * G, G), :], ALU.add)\
                        .then_inc(total_ready, 1)
                dve.wait_ge(total_ready, i * U + U)
                if more:
                    last_round(loop, i + 1)
                for u in range(U):
                    after[u].take_moments(nc, loop, total[:, u, :, :])
                for u in range(U):
                    if not first:
                        dve.wait_ge(stored[u], i * 16)
                    after[u].apply(nc, dve, total[:, u, :, :], lambda b: res[:, u, b, :], i, res_ready)

            last_round(Steps(dve, dve_steps, base), 0)
            put_out(Steps(dve, dve_steps, base + U, 18), 0, True, first=True)
            with dve.Fori(1, NG // U - 1) as i:
                loop = Steps(dve, dve_steps, i * 18 + base + U, 18)
                put_out(loop, i, True)
                loop.closed()
            last = NG // U - 1
            put_out(Steps(dve, dve_steps, last * 18 + base + U), last, False)


class Consts:
    pass


def build(nc, a, out):
    with ExitStack() as stack:
        m = Mem(nc, stack, "all")
        c = Consts()
        c.ident = m.sb("ident", [128, 128])
        c.ident_b = m.sb("ident_b", [128, 128], BF16)
        c.causal = m.sb("causal", [T, T])
        c.causal_b = m.sb("causal_b", [T, T], BF16)
        c.minus_half = m.sb("minus_half", [T, G])
        x_all = m.sb("x_all", [T, B, D])
        y_all = m.sb("y_all", [T, B, D])
        c.x_all, c.y_all = x_all, y_all
        c.out_dram = out.rearrange("b t d -> t b d")
        landed = m.sem("landed")
        cast = m.sem("cast")
        x_dram = a["x"].rearrange("b t d -> t b d")

        with nc.Block() as block:
            @block.sync
            def _(sp):
                sp.dma_start(c.ident[:], a["ident"]).then_inc(landed, 16)
                sp.dma_start(c.causal[:], a["causal"]).then_inc(landed, 16)
                for g in range(NG):
                    sp.dma_start(x_all[:, g * G:(g + 1) * G, :], x_dram[:, g * G:(g + 1) * G, :]).then_inc(landed, 16)

            @block.vector
            def _(dve):
                dve.wait_ge(landed, 16 * (NG + 2))
                nc.vector.tensor_copy(c.ident_b[:], c.ident[:]).then_inc(cast, 1)
                nc.vector.tensor_copy(c.causal_b[:], c.causal[:]).then_inc(cast, 1)
                nc.vector.memset(c.minus_half[:], -0.5).then_inc(cast, 1)
                dve.wait_ge(cast, 3)

        clear_counts(nc)
        for k in STAGES:
            k(nc, a, c)
            clear_counts(nc)


def stage_attn0(nc, a, c):
    p = "L0_attn_"
    attention(nc, "at0", c.x_all, c.y_all, c, dict(
        loads=lambda w_qkv, w_o, gain: [(w_qkv[:], a[p + "Wqkv"]), (w_o[:], a[p + "Wo"]),
                                        (gain[:, 0:1], column(a[p + "ln1_g"])), (gain[:, 1:2], column(a[p + "ln1_b"]))],
        n_loads=8, b_qkv=a[p + "bqkv"], b_o=a[p + "bo"], cos=a["rope_cos"], sin=a["rope_sin"], dve_steps=44), True)


def stage_attn1(nc, a, c):
    p = "L0_ffn_"
    attention(nc, "at1", c.x_all, c.y_all, c, dict(
        loads=lambda w_qkv, w_o, gain: [(w_qkv[:, n * D:(n + 1) * D], a[p + w]) for n, w in enumerate(("wq", "wk", "wv"))]
        + [(w_o[:], a[p + "wo"]), (gain[:, 0:1], column(a[p + "norm1_w"]))],
        n_loads=5, dve_steps=41), False)


def stage_gelu(nc, a, c):
    p = "L0_attn_"
    gelu_ffn(nc, "gelu", c.x_all, c.y_all, c, dict(w1=a[p + "W1"], b1=a[p + "b1"], w2=a[p + "W2"], b2=a[p + "b2"],
                                                   g=a[p + "ln2_g"], b=a[p + "ln2_b"]))


def stage_retention(nc, a, c):
    p = "L0_xattn_"
    retention(nc, "ret", c.x_all, a["ctx_1024"].rearrange("b t d -> t b d"), c, dict(
        w_q=a[p + "W_Q"], w_k=a[p + "W_K"], w_v=a[p + "W_V"], w_g=a[p + "g_w"], w_o=a[p + "out_w"],
        b_g=a[p + "g_b"], b_o=a[p + "out_b"], cos=a["xpos_cos"], sin=a["xpos_sin"], decay=a["decay"], dve_steps=40))


def stage_moe(nc, a, c):
    p = "L0_ffn_"
    moe(nc, "moe", c.x_all, c.y_all, c, dict(
        e_gate=a[p + "e_gate"], e_up=a[p + "e_up"], e_down=a[p + "e_down"], sh_gate=a[p + "sh_gate"], sh_up=a[p + "sh_up"],
        sh_down=a[p + "sh_down"], router=a[p + "router_w"], gain=a[p + "norm2_w"], number=a["number"], steps=(9, 60)))


def stage_cross(nc, a, c):
    p = "L1_xattn_"
    cross_attention(nc, "xat", c.x_all, a["ctx_1024"].rearrange("b t d -> t b d"), c, dict(
        w_q=a[p + "W_Q"], w_k=a[p + "W_K"], w_v=a[p + "W_V"], w_o=a[p + "W_O"]))


def stage_mamba(nc, a, c):
    mamba(nc, "mam", c.x_all, c, dict(a=a))


def stage_quant(nc, a, c):
    quant_ffn(nc, "qua", c.x_all, c.out_dram, c, {w: a["L1_ffn_" + w] for w in ("w_gate", "w_up", "w_down")})


STAGES = [stage_attn0, stage_gelu, stage_retention, stage_attn1, stage_moe, stage_mamba, stage_cross, stage_quant]


def tables():
    f = np.float32
    t = {"ident": np.eye(128, dtype=f)}
    t["causal"] = np.where(np.arange(T)[:, None] >= np.arange(T)[None, :], f(0), f(HUGE)).astype(f)
    inv_freq = f(1.0) / f(10000.0) ** (np.arange(0, HD, 2, dtype=f) / f(HD))
    freqs = np.arange(T, dtype=f)[:, None] * inv_freq[None, :]
    sin = np.sin(freqs).astype(f)
    t["rope_cos"] = np.tile(np.concatenate([np.cos(freqs)] * 2, -1), (1, 2 * H)).astype(f)
    t["rope_sin"] = np.tile(np.concatenate([-sin, sin], -1), (1, 2 * H)).astype(f)
    base = (np.arange(0, HD, 2, dtype=f) + f(0.4 * HD)) / f(1.4 * HD)
    power = (np.arange(-(T // 2), T - T // 2, dtype=f) / f(512.0))[:, None]
    scale = (base[None, :] ** power).astype(f)
    ang = np.arange(T, dtype=f)[:, None] * (f(1.0) / f(10000.0) ** (np.arange(HD // 2, dtype=f) / f(HD // 2)))[None, :]
    both = []
    for s in (scale, f(1.0) / scale):
        cos_s, sin_s = np.repeat(np.cos(ang) * s, 2, -1), np.repeat(np.sin(ang) * s, 2, -1)
        sin_s[:, ::2] *= -1
        both.append((np.tile(cos_s, (1, H)), np.tile(sin_s, (1, H))))
    t["xpos_cos"] = np.concatenate([both[0][0], both[1][0]], -1).astype(f)
    t["xpos_sin"] = np.concatenate([both[0][1], both[1][1]], -1).astype(f)
    gammas = f(1.0) - np.exp(np.linspace(np.log(1.0 / 32.0), np.log(1.0 / 512.0), H).astype(f)).astype(f)
    dist = np.arange(T)[None, :] - np.arange(T)[:, None]
    t["number"] = np.tile(np.arange(8, dtype=f), (T, 1))
    decay = np.where(dist[:, None, :] >= 0, gammas[None, :, None] ** np.maximum(dist, 0).astype(f)[:, None, :], 0).astype(f)
    t["decay"] = decay[:, [head_at(j, k) for j in range(NJ) for k in range(NK)], :].reshape(T, NJ, NK, T)
    return t


def laid_out(inputs):
    a = {k: np.asarray(v) for k, v in inputs.items()}
    for w in ("W_Q", "W_K", "W_V"):
        a["L0_xattn_" + w] = a["L0_xattn_" + w].transpose(1, 0, 2).reshape(D, D)
    for w in ("L0_xattn_g_w", "L0_xattn_out_w", "L1_xattn_W_Q", "L1_xattn_W_K", "L1_xattn_W_V", "L1_xattn_W_O"):
        a[w] = a[w].T
    for w in ("L0_attn_Wo", "L0_ffn_wo"):
        a[w] = a[w].reshape(2, NK, NJ // 2, HD, D).transpose(1, 0, 2, 3, 4).reshape(D, D)
    for s in "fb":
        for w in ("inW", "xpW", "dtW", "outW"):
            a[f"L1_attn_{w}_{s}"] = a[f"L1_attn_{w}_{s}"].T
        a[f"L1_attn_convW_{s}"] = a[f"L1_attn_convW_{s}"][:, 0, :].T
    return a


def kernel(**inputs):
    import concourse.bacc as bacc
    from concourse.bass_utils import run_bass_kernel_spmd

    nc = bacc.Bacc("TRN2", target_bir_lowering=False, num_devices=1)
    arrays, args = {}, {}
    for name, value in list(laid_out(inputs).items()) + list(tables().items()):
        value = np.ascontiguousarray(value)
        arrays[f"in_{name}"] = value
        args[name] = nc.dram_tensor(f"in_{name}", value.shape, mybir.dt.from_np(value.dtype), kind="ExternalInput").ap()
    out = nc.dram_tensor("out", (B, T, D), F32, kind="ExternalOutput").ap()
    with nc.allow_non_contiguous_dma(reason="a few small vectors lie down the partitions"):
        build(nc, args, out)
    got = run_bass_kernel_spmd(nc, [arrays], core_ids=[0])
    return got.results[0]["out"]
```
